# Optimizing a Trainium2 kernel written in Bass

```python
import numpy as np
import jax
import jax.numpy as jnp

def _softmax(x, axis=-1):
    return jax.nn.softmax(x, axis=axis)

def _gelu(x):
    return jax.nn.gelu(x, approximate=True)

def _silu(x):
    return jax.nn.silu(x)

def _sigmoid(x):
    return jax.nn.sigmoid(x)

def _layernorm(x, axis=-1, eps=1e-05):
    m = jnp.mean(x, axis=axis, keepdims=True)
    v = jnp.var(x, axis=axis, keepdims=True)
    return (x - m) / jnp.sqrt(v + eps)

def _scatter_add(tgt, idx, src, axis=0):
    return tgt.at[idx].add(src)

def _segment_sum(src, seg, n):
    return jax.ops.segment_sum(src, seg, n)
kernel_name = 'mk_flamingo_gated_d2_seqx_r8_46c3a9'

def setup_inputs(seed: int=0):
    np.random.seed(seed)
    _w = jnp.asarray

    def _rec_inputs():
        import jax
        import jax.numpy as jnp
        _rk = jax.random.key(seed)
        x = -0.0002928 + 1 * jax.random.normal(jax.random.fold_in(_rk, 1), (16, 128, 256), jnp.float32)
        _lenS = 128 - jax.random.randint(jax.random.fold_in(_rk, 7), (16,), 0, max(1, 128 // 4) + 1, jnp.int32)
        _lenS2 = 128 - jax.random.randint(jax.random.fold_in(_rk, 8), (16,), 0, max(1, 128 // 4) + 1, jnp.int32)
        _ctx_2048P = jax.random.normal(jax.random.fold_in(_rk, 11), (16, 16, 256), jnp.float32)
        _ctx_2048c = jax.random.dirichlet(jax.random.fold_in(_rk, 511), 0.3 * jnp.ones((16,), jnp.float32), (16, 128))
        _ctx_2048t = jnp.einsum('bsk,bkd->bsd', _ctx_2048c, _ctx_2048P)
        _ctx_2048t = _ctx_2048t * jax.lax.rsqrt(jnp.mean(jnp.square(_ctx_2048t)) + 1e-12) * 0.953939
        ctx_2048 = -1.39393e-06 + 0.999914 * (_ctx_2048t + 0.3 * jax.random.normal(jax.random.fold_in(_rk, 611), (16, 128, 256), jnp.float32))
        _validS = jnp.arange(128)[None, :] < _lenS[:, None]
        _validS2 = jnp.arange(128)[None, :] < _lenS2[:, None]
        _causal = jnp.tril(jnp.ones((128, 128), dtype=bool))
        mask_Bx1x2048_fk1 = jnp.where(jnp.ones((16, 1, 256), dtype=bool), 1.0, 0.0).astype(jnp.float32)
        _g = jax.random.normal(jax.random.fold_in(_rk, 9001), (2, 2), jnp.float32)
        _g = jnp.sign(_g) * jnp.maximum(jnp.abs(_g), 1.0) + (_g == 0) * 1.0
        g_xattn = _g[0]
        g_ffn = _g[1]
        return (x, ctx_2048, mask_Bx1x2048_fk1, g_xattn, g_ffn)
    x, ctx_2048, mask_Bx1x2048_fk1, g_xattn, g_ffn = _rec_inputs()

    def _L0_xattn_setup():
        import math
        import jax, jax.numpy as jnp
        import numpy as np
        SIZE = 128
        HEADS = 16
        HEAD_DIM = SIZE // HEADS
        B, T, S = (2, 256, 256)
        NEG = 1000000.0
        key = jax.random.key(seed)
        ks = jax.random.split(key, 10)
        target = jax.random.normal(ks[0], (B, SIZE, T), dtype=jnp.float32)
        source = jax.random.normal(ks[1], (B, SIZE, S), dtype=jnp.float32)
        target_mask = (jax.random.uniform(ks[2], (B, 1, T)) > 0.1).astype(jnp.float32)
        source_mask = (jax.random.uniform(ks[3], (B, 1, S)) > 0.1).astype(jnp.float32)
        scale = 1.0 / math.sqrt(SIZE)
        Wq = jax.random.normal(ks[4], (SIZE, SIZE), dtype=jnp.float32) * scale
        Wk = jax.random.normal(ks[5], (SIZE, SIZE), dtype=jnp.float32) * scale
        Wv = jax.random.normal(ks[6], (SIZE, SIZE), dtype=jnp.float32) * scale
        bq = jax.random.normal(ks[7], (SIZE,), dtype=jnp.float32) * 0.01
        bk = jax.random.normal(ks[8], (SIZE,), dtype=jnp.float32) * 0.01
        bv = jax.random.normal(ks[9], (SIZE,), dtype=jnp.float32) * 0.01
        return {'target': target, 'source': source, 'target_mask': target_mask, 'source_mask': source_mask, 'Wq': Wq, 'bq': bq, 'Wk': Wk, 'bk': bk, 'Wv': Wv, 'bv': bv}
    _L0_xattn_all = _L0_xattn_setup()
    _L0_xattn_in = {k: v for k, v in _L0_xattn_all.items() if k in ('Wq', 'bq', 'Wk', 'bk', 'Wv', 'bv')}
    del _L0_xattn_all

    def _L0_ffn_setup():
        import jax, jax.numpy as jnp
        import numpy as np
        D_MODEL = 256
        HIDDEN = 4 * D_MODEL
        B, S = (2, 512)

        def bit_linear(x, w, b):
            gamma_x = jnp.clip(jnp.max(jnp.abs(x), axis=-1, keepdims=True), 1e-05, None)
            scale_x = 127.0 / gamma_x
            x_dq = jnp.clip(jnp.round(x * scale_x), -128.0, 127.0) / scale_x
            x_ste = x + jax.lax.stop_gradient(x_dq - x)
            gamma_w = jnp.clip(jnp.mean(jnp.abs(w)), 1e-05, None)
            w_dq = jnp.clip(jnp.round(w / gamma_w), -1.0, 1.0) * gamma_w
            w_ste = w + jax.lax.stop_gradient(w_dq - w)
            return jnp.einsum('bsd,hd->bsh', x_ste, w_ste) + b
        key = jax.random.key(seed)
        ks = jax.random.split(key, 7)
        std = 0.02
        return {'x': jax.random.normal(ks[0], (B, S, D_MODEL), dtype=jnp.float32), 'gate_w': jax.random.normal(ks[1], (HIDDEN, D_MODEL), dtype=jnp.float32) * std, 'gate_b': jnp.zeros((HIDDEN,), dtype=jnp.float32), 'val_w': jax.random.normal(ks[2], (HIDDEN, D_MODEL), dtype=jnp.float32) * std, 'val_b': jnp.zeros((HIDDEN,), dtype=jnp.float32), 'out_w': jax.random.normal(ks[3], (D_MODEL, HIDDEN), dtype=jnp.float32) * std, 'out_b': jnp.zeros((D_MODEL,), dtype=jnp.float32)}
    _L0_ffn_all = _L0_ffn_setup()
    _L0_ffn_in = {k: v for k, v in _L0_ffn_all.items() if k in ('gate_w', 'gate_b', 'val_w', 'val_b', 'out_w', 'out_b')}
    del _L0_ffn_all

    def _L1_xattn_setup():
        import jax, jax.numpy as jnp
        import numpy as np
        DIM = 256
        H = 16
        D = 128
        INNER = H * D
        N_IMG = 257
        EPS = 1e-06

        def rms_norm(x, scale, eps=EPS):
            ms = jnp.mean(jnp.square(x), axis=-1, keepdims=True)
            return x * jax.lax.rsqrt(ms + eps) * scale

        def sdpa(q, k, v):
            scale = 1.0 / jnp.sqrt(jnp.asarray(D, q.dtype))
            scores = jnp.einsum('bshd,blhd->bhsl', q, k) * scale
            attn = jax.nn.softmax(scores, axis=-1)
            return jnp.einsum('bhsl,blhd->bshd', attn, v)
        key = jax.random.key(seed)
        ks = jax.random.split(key, 16)
        std = 1.0 / np.sqrt(DIM)
        inp = {'x': jax.random.normal(ks[0], (2, 512, DIM), jnp.float32), 'context': jax.random.normal(ks[1], (2, 769, DIM), jnp.float32), 'q_w': jax.random.normal(ks[2], (DIM, INNER), jnp.float32) * std, 'q_b': jnp.zeros((INNER,), jnp.float32), 'k_w': jax.random.normal(ks[3], (DIM, INNER), jnp.float32) * std, 'k_b': jnp.zeros((INNER,), jnp.float32), 'v_w': jax.random.normal(ks[4], (DIM, INNER), jnp.float32) * std, 'v_b': jnp.zeros((INNER,), jnp.float32), 'ki_w': jax.random.normal(ks[5], (DIM, INNER), jnp.float32) * std, 'ki_b': jnp.zeros((INNER,), jnp.float32), 'vi_w': jax.random.normal(ks[6], (DIM, INNER), jnp.float32) * std, 'vi_b': jnp.zeros((INNER,), jnp.float32), 'o_w': jax.random.normal(ks[7], (INNER, DIM), jnp.float32) * std, 'o_b': jnp.zeros((DIM,), jnp.float32), 'nq_s': jnp.ones((INNER,), jnp.float32), 'nkt_s': jnp.ones((INNER,), jnp.float32), 'nki_s': jnp.ones((INNER,), jnp.float32)}
        return inp
    _L1_xattn_all = _L1_xattn_setup()
    _L1_xattn_in = {k: v for k, v in _L1_xattn_all.items() if k in ('q_w', 'q_b', 'k_w', 'k_b', 'v_w', 'v_b', 'ki_w', 'ki_b', 'vi_w', 'vi_b', 'o_w', 'o_b', 'nq_s', 'nkt_s', 'nki_s')}
    del _L1_xattn_all

    def _L1_ffn_setup():
        import jax, jax.numpy as jnp
        import numpy as np
        H = 256
        NH = 16
        NOPE = 128
        ROPE = 64
        VD = 128
        QHD = NOPE + ROPE
        E = 16
        I = 176
        TOPK = 4
        NSH = 2
        SHI = I * NSH
        EPS = 1e-06
        B, S = (2, 128)

        def rmsnorm(x, w):
            return x * jax.lax.rsqrt(jnp.mean(x * x, axis=-1, keepdims=True) + EPS) * w
        key = jax.random.key(seed)
        ks = jax.random.split(key, 12)
        sd = lambda fan_in: 1.0 / np.sqrt(fan_in)
        return {'hidden_states': jax.random.normal(ks[0], (B, S, H), jnp.float32), 'positions': jnp.broadcast_to(jnp.arange(S, dtype=jnp.int32), (B, S)), 'ln1_w': jnp.ones((H,), jnp.float32), 'ln2_w': jnp.ones((H,), jnp.float32), 'q_w': jax.random.normal(ks[1], (NH * QHD, H), jnp.float32) * sd(H), 'kv_w': jax.random.normal(ks[2], (NH * (NOPE + VD) + ROPE, H), jnp.float32) * sd(H), 'o_w': jax.random.normal(ks[3], (H, NH * VD), jnp.float32) * sd(NH * VD), 'gate_w': jax.random.normal(ks[4], (E, H), jnp.float32) * sd(H), 'w1': jax.random.normal(ks[5], (E, 2 * I, H), jnp.float32) * sd(H), 'w2': jax.random.normal(ks[6], (E, H, I), jnp.float32) * sd(I), 'sh_gu_w': jax.random.normal(ks[7], (2 * SHI, H), jnp.float32) * sd(H), 'sh_down_w': jax.random.normal(ks[8], (H, SHI), jnp.float32) * sd(SHI)}
    _L1_ffn_all = _L1_ffn_setup()
    _L1_ffn_in = {k: v for k, v in _L1_ffn_all.items() if k in ('positions', 'ln1_w', 'ln2_w', 'q_w', 'kv_w', 'o_w', 'gate_w', 'w1', 'w2', 'sh_gu_w', 'sh_down_w')}
    del _L1_ffn_all
    return {'x': x, 'ctx_2048': ctx_2048, 'mask_Bx1x2048_fk1': mask_Bx1x2048_fk1, 'g_xattn': g_xattn, 'g_ffn': g_ffn, 'L0_xattn_Wq': _L0_xattn_in['Wq'], 'L0_xattn_bq': _L0_xattn_in['bq'], 'L0_xattn_Wk': _L0_xattn_in['Wk'], 'L0_xattn_bk': _L0_xattn_in['bk'], 'L0_xattn_Wv': _L0_xattn_in['Wv'], 'L0_xattn_bv': _L0_xattn_in['bv'], 'L0_ffn_gate_w': _L0_ffn_in['gate_w'], 'L0_ffn_gate_b': _L0_ffn_in['gate_b'], 'L0_ffn_val_w': _L0_ffn_in['val_w'], 'L0_ffn_val_b': _L0_ffn_in['val_b'], 'L0_ffn_out_w': _L0_ffn_in['out_w'], 'L0_ffn_out_b': _L0_ffn_in['out_b'], 'L1_xattn_q_w': _L1_xattn_in['q_w'], 'L1_xattn_q_b': _L1_xattn_in['q_b'], 'L1_xattn_k_w': _L1_xattn_in['k_w'], 'L1_xattn_k_b': _L1_xattn_in['k_b'], 'L1_xattn_v_w': _L1_xattn_in['v_w'], 'L1_xattn_v_b': _L1_xattn_in['v_b'], 'L1_xattn_ki_w': _L1_xattn_in['ki_w'], 'L1_xattn_ki_b': _L1_xattn_in['ki_b'], 'L1_xattn_vi_w': _L1_xattn_in['vi_w'], 'L1_xattn_vi_b': _L1_xattn_in['vi_b'], 'L1_xattn_o_w': _L1_xattn_in['o_w'], 'L1_xattn_o_b': _L1_xattn_in['o_b'], 'L1_xattn_nq_s': _L1_xattn_in['nq_s'], 'L1_xattn_nkt_s': _L1_xattn_in['nkt_s'], 'L1_xattn_nki_s': _L1_xattn_in['nki_s'], 'L1_ffn_positions': _L1_ffn_in['positions'], 'L1_ffn_ln1_w': _L1_ffn_in['ln1_w'], 'L1_ffn_ln2_w': _L1_ffn_in['ln2_w'], 'L1_ffn_q_w': _L1_ffn_in['q_w'], 'L1_ffn_kv_w': _L1_ffn_in['kv_w'], 'L1_ffn_o_w': _L1_ffn_in['o_w'], 'L1_ffn_gate_w': _L1_ffn_in['gate_w'], 'L1_ffn_w1': _L1_ffn_in['w1'], 'L1_ffn_w2': _L1_ffn_in['w2'], 'L1_ffn_sh_gu_w': _L1_ffn_in['sh_gu_w'], 'L1_ffn_sh_down_w': _L1_ffn_in['sh_down_w']}

def reference(x, ctx_2048, mask_Bx1x2048_fk1, g_xattn, g_ffn, L0_xattn_Wq, L0_xattn_bq, L0_xattn_Wk, L0_xattn_bk, L0_xattn_Wv, L0_xattn_bv, L0_ffn_gate_w, L0_ffn_gate_b, L0_ffn_val_w, L0_ffn_val_b, L0_ffn_out_w, L0_ffn_out_b, L1_xattn_q_w, L1_xattn_q_b, L1_xattn_k_w, L1_xattn_k_b, L1_xattn_v_w, L1_xattn_v_b, L1_xattn_ki_w, L1_xattn_ki_b, L1_xattn_vi_w, L1_xattn_vi_b, L1_xattn_o_w, L1_xattn_o_b, L1_xattn_nq_s, L1_xattn_nkt_s, L1_xattn_nki_s, L1_ffn_positions, L1_ffn_ln1_w, L1_ffn_ln2_w, L1_ffn_q_w, L1_ffn_kv_w, L1_ffn_o_w, L1_ffn_gate_w, L1_ffn_w1, L1_ffn_w2, L1_ffn_sh_gu_w, L1_ffn_sh_down_w):
    import jax
    import jax.numpy as jnp

    def _L0_xattn_ref(target, source, target_mask, source_mask, Wq, bq, Wk, bk, Wv, bv):
        import math
        import jax, jax.numpy as jnp
        import numpy as np
        SIZE = 128
        HEADS = 16
        HEAD_DIM = SIZE // HEADS
        B, T, S = (2, 256, 256)
        NEG = 1000000.0
        b, _, t = target.shape
        s = source.shape[-1]
        q = jnp.einsum('oc,bct->bot', Wq, target) + bq[None, :, None]
        k = jnp.einsum('oc,bcs->bos', Wk, source) + bk[None, :, None]
        v = jnp.einsum('oc,bcs->bos', Wv, source) + bv[None, :, None]
        q = q.reshape(b, HEADS, HEAD_DIM, t)
        k = k.reshape(b, HEADS, HEAD_DIM, s)
        v = v.reshape(b, HEADS, HEAD_DIM, s)
        dot = jnp.einsum('bhdt,bhds->bhts', q, k) / math.sqrt(HEAD_DIM)
        mask = target_mask[:, :, :, None] * source_mask[:, :, None, :]
        dot = mask * dot - (1.0 - mask) * NEG
        amap = jax.nn.softmax(dot, axis=-1) * mask
        out = jnp.einsum('bhts,bhds->bhdt', amap, v)
        return out.reshape(b, HEADS * HEAD_DIM, t)

    def _L0_ffn_ref(x, gate_w, gate_b, val_w, val_b, out_w, out_b):
        import jax, jax.numpy as jnp
        import numpy as np
        D_MODEL = 256
        HIDDEN = 4 * D_MODEL
        B, S = (2, 512)

        def bit_linear(x, w, b):
            gamma_x = jnp.clip(jnp.max(jnp.abs(x), axis=-1, keepdims=True), 1e-05, None)
            scale_x = 127.0 / gamma_x
            x_dq = jnp.clip(jnp.round(x * scale_x), -128.0, 127.0) / scale_x
            x_ste = x + jax.lax.stop_gradient(x_dq - x)
            gamma_w = jnp.clip(jnp.mean(jnp.abs(w)), 1e-05, None)
            w_dq = jnp.clip(jnp.round(w / gamma_w), -1.0, 1.0) * gamma_w
            w_ste = w + jax.lax.stop_gradient(w_dq - w)
            return jnp.einsum('bsd,hd->bsh', x_ste, w_ste) + b
        gate = jax.nn.silu(bit_linear(x, gate_w, gate_b))
        val = bit_linear(x, val_w, val_b)
        return bit_linear(gate * val, out_w, out_b)

    def _L1_xattn_ref(x, context, q_w, q_b, k_w, k_b, v_w, v_b, ki_w, ki_b, vi_w, vi_b, o_w, o_b, nq_s, nkt_s, nki_s):
        import jax, jax.numpy as jnp
        import numpy as np
        DIM = 256
        H = 16
        D = 128
        INNER = H * D
        N_IMG = 257
        EPS = 1e-06

        def rms_norm(x, scale, eps=EPS):
            ms = jnp.mean(jnp.square(x), axis=-1, keepdims=True)
            return x * jax.lax.rsqrt(ms + eps) * scale

        def sdpa(q, k, v):
            scale = 1.0 / jnp.sqrt(jnp.asarray(D, q.dtype))
            scores = jnp.einsum('bshd,blhd->bhsl', q, k) * scale
            attn = jax.nn.softmax(scores, axis=-1)
            return jnp.einsum('bhsl,blhd->bshd', attn, v)
        B, S, _ = x.shape
        img_ctx = context[:, :N_IMG]
        txt_ctx = context[:, N_IMG:]
        q = rms_norm(x @ q_w + q_b, nq_s).reshape(B, S, H, D)
        k_txt = rms_norm(txt_ctx @ k_w + k_b, nkt_s).reshape(B, -1, H, D)
        v_txt = (txt_ctx @ v_w + v_b).reshape(B, -1, H, D)
        out_txt = sdpa(q, k_txt, v_txt)
        k_img = rms_norm(img_ctx @ ki_w + ki_b, nki_s).reshape(B, -1, H, D)
        v_img = (img_ctx @ vi_w + vi_b).reshape(B, -1, H, D)
        out_img = sdpa(q, k_img, v_img)
        out = (out_txt + out_img).reshape(B, S, INNER)
        return out @ o_w + o_b

    def _L1_ffn_ref(hidden_states, positions, ln1_w, ln2_w, q_w, kv_w, o_w, gate_w, w1, w2, sh_gu_w, sh_down_w):
        import jax, jax.numpy as jnp
        import numpy as np
        H = 256
        NH = 16
        NOPE = 128
        ROPE = 64
        VD = 128
        QHD = NOPE + ROPE
        E = 16
        I = 176
        TOPK = 4
        NSH = 2
        SHI = I * NSH
        EPS = 1e-06
        B, S = (2, 128)

        def rmsnorm(x, w):
            return x * jax.lax.rsqrt(jnp.mean(x * x, axis=-1, keepdims=True) + EPS) * w
        b, s, h = hidden_states.shape
        x = rmsnorm(hidden_states, ln1_w)
        q = jnp.einsum('bsh,dh->bsd', x, q_w).reshape(b, s, NH, QHD)[..., :NOPE]
        kv = jnp.einsum('bsh,dh->bsd', x, kv_w)
        k = kv[..., :NH * NOPE].reshape(b, s, NH, NOPE)
        v = kv[..., NH * NOPE:NH * (NOPE + VD)].reshape(b, s, NH, VD)
        scale = QHD ** (-0.5)
        scores = jnp.einsum('bqnd,bknd->bnqk', q, k) * scale
        causal = jnp.tril(jnp.ones((s, s), bool))
        scores = jnp.where(causal, scores, -1000000000.0)
        p = jax.nn.softmax(scores, axis=-1)
        attn = jnp.einsum('bnqk,bknd->bqnd', p, v).reshape(b, s, NH * VD)
        attn_out = jnp.einsum('bsd,hd->bsh', attn, o_w)
        hid = hidden_states + attn_out
        x2 = rmsnorm(hid, ln2_w).reshape(-1, h)
        logits = x2 @ gate_w.T
        probs = jax.nn.softmax(logits, axis=-1)
        top_w, top_i = jax.lax.top_k(probs, TOPK)
        top_w = top_w / jnp.sum(top_w, axis=-1, keepdims=True)
        wfull = jnp.sum(jax.nn.one_hot(top_i, E, dtype=x2.dtype) * top_w[..., None], axis=1)
        gu = jnp.einsum('th,eih->tei', x2, w1)
        g, u = (gu[..., :I], gu[..., I:])
        act = jax.nn.silu(g) * u
        down = jnp.einsum('tei,ehi->teh', act, w2)
        routed = jnp.einsum('te,teh->th', wfull, down)
        sgu = x2 @ sh_gu_w.T
        sg, su = (sgu[..., :SHI], sgu[..., SHI:])
        shared = jax.nn.silu(sg) * su @ sh_down_w.T
        return hid + (routed + shared).reshape(b, s, h)
    x = x + jnp.tanh(g_xattn[0]) * _L0_xattn_ref(_layernorm(x, axis=-1), ctx_2048, mask_Bx1x2048_fk1, mask_Bx1x2048_fk1, L0_xattn_Wq, L0_xattn_bq, L0_xattn_Wk, L0_xattn_bk, L0_xattn_Wv, L0_xattn_bv)
    x = x + jnp.tanh(g_ffn[0]) * _L0_ffn_ref(_layernorm(x, axis=-1), L0_ffn_gate_w, L0_ffn_gate_b, L0_ffn_val_w, L0_ffn_val_b, L0_ffn_out_w, L0_ffn_out_b)
    x = x + jnp.tanh(g_xattn[1]) * _L1_xattn_ref(_layernorm(x, axis=-1), ctx_2048, L1_xattn_q_w, L1_xattn_q_b, L1_xattn_k_w, L1_xattn_k_b, L1_xattn_v_w, L1_xattn_v_b, L1_xattn_ki_w, L1_xattn_ki_b, L1_xattn_vi_w, L1_xattn_vi_b, L1_xattn_o_w, L1_xattn_o_b, L1_xattn_nq_s, L1_xattn_nkt_s, L1_xattn_nki_s)
    x = x + jnp.tanh(g_ffn[1]) * _L1_ffn_ref(_layernorm(x, axis=-1), L1_ffn_positions, L1_ffn_ln1_w, L1_ffn_ln2_w, L1_ffn_q_w, L1_ffn_kv_w, L1_ffn_o_w, L1_ffn_gate_w, L1_ffn_w1, L1_ffn_w2, L1_ffn_sh_gu_w, L1_ffn_sh_down_w)
    return x

_drawn_inputs = setup_inputs


def setup_inputs(seed=0):
    import zlib

    import numpy as np

    out = dict(_drawn_inputs(seed))
    spreads = {'g_ffn': (-1.0, 0.6),
     'L0_ffn_gate_b': (0.0, 0.8),
     'L0_ffn_val_b': (0.0, 0.8),
     'L0_ffn_out_b': (0.0, 0.704),
     'L1_xattn_q_b': (0.0, 0.8),
     'L1_xattn_k_b': (0.0, 0.1),
     'L1_xattn_v_b': (0.0, 0.1),
     'L1_xattn_ki_b': (0.0, 2.0),
     'L1_xattn_vi_b': (0.0, 0.1),
     'L1_xattn_o_b': (0.0, 0.554),
     'L1_xattn_nq_s': (1.0, 0.6),
     'L1_xattn_nkt_s': (1.0, 0.2),
     'L1_xattn_nki_s': (1.0, 0.6),
     'L1_ffn_ln1_w': (1.0, 0.6),
     'L1_ffn_ln2_w': (1.0, 0.2)}
    factors = {'L0_xattn_bv': 6.597, 'L0_ffn_gate_w': 8.0, 'L0_ffn_val_w': 8.0, 'L0_ffn_out_w': 8.0}
    for name, (base, spread) in spreads.items():
        noise = np.random.default_rng([zlib.crc32(name.encode()), seed]).standard_normal(out[name].shape)
        drawn = base * np.exp(spread * noise) if base else spread * noise
        out[name] = jnp.asarray(drawn.astype(out[name].dtype))
    for name, factor in factors.items():
        out[name] = (out[name] * factor).astype(out[name].dtype)
    return out
```

```python
import numpy as np
from contextlib import ExitStack

import concourse.bass as bass
from concourse import mybir
from concourse.bass import ds

F32 = mybir.dt.float32
F32R = mybir.dt.float32r
BF16 = mybir.dt.bfloat16
ALU = mybir.AluOpType
ACT = mybir.ActivationFunctionType
AX = mybir.AxisListType

P = 128
BATCHES, TOKENS, DIM = 16, 128, 256
KT = DIM // P
NEG = 1.0e6

A_HEADS, A_HD = 16, 8
A_SLOTS = 4
A_TILES = A_HEADS // A_SLOTS
A_ROWS = P // A_SLOTS
A_ROOT = float(A_HD) ** 0.5

ROUND = 12582912.0


class Scope:

    def __init__(self, nc, stack, tag):
        self.nc, self.stack, self.tag, self.sems = nc, stack, tag, []
        stack.callback(self.release)

    def release(self):
        if self.sems:
            self.nc.clear_and_free_semaphores(self.sems)
            self.nc.all_engine_barrier()

    def sb(self, name, shape, dt=F32):
        return self.stack.enter_context(self.nc.sbuf_tensor(f"{self.tag}_{name}", shape, dt))

    def ps(self, name, shape, dt=F32):
        return self.stack.enter_context(self.nc.psum_tensor(f"{self.tag}_{name}", shape, dt))

    def sem(self, name):
        self.sems.append(self.nc.alloc_semaphore(f"{self.tag}_{name}"))
        return self.sems[-1]


def after(eng, sem, value):
    if not (isinstance(value, int) and value <= 0):
        eng.wait_ge(sem, value)


def settled(eng, sem, value, met):
    eng.wait_ge(*met)
    after(eng, sem, value)


def pairs(eng, count, body):
    for p in range(2):
        body(0, p)
    with eng.Fori(1, count // 2 - 1) as i:
        for p in range(2):
            body(i, p)
    for p in range(2):
        body(count // 2 - 1, p)



def make_resident(nc, stack, io):
    x = stack.enter_context(nc.sbuf_tensor("x_sb", [P, BATCHES, DIM], F32))
    ident = stack.enter_context(nc.sbuf_tensor("ident", [P, P], F32))
    blank = nc.alloc_semaphore("blank")
    with nc.Block() as block:

        @block.gpsimd
        def _(pool):
            pool.memset(ident[:, :], 0.0).then_inc(blank, 1)
            pool.wait_ge(blank, 1)
            pool.affine_select(out=ident[:, :], in_=ident[:, :], compare_op=ALU.not_equal, fill=1.0, base=0,
                               pattern=[[-1, P]], channel_multiplier=1)
    return {"x": x, "ident": ident}


def attend_channels(nc, res, src, ctx_in, mask, maskT, wq4, wk4, wv, bq4, bk4, bv, consts, gate):
    x_sb = res["x"]
    with ExitStack() as stack:
        s = Scope(nc, stack, "a")
        ctx_sb = s.sb("ctx", [P, BATCHES, DIM])
        tm = s.sb("tm", [P, BATCHES, DIM])
        km = s.sb("km", [P, BATCHES, DIM])
        smT = s.sb("smT", [P, 2 * BATCHES])
        wraw = s.sb("wraw", [P, 2 * 512 + P])
        wh = s.sb("wh", [P, 2 * 512 + P], F32R)
        wl = s.sb("wl", [P, 2 * 512 + P], F32R)
        bcol = s.sb("bcol", [P, 2 * A_TILES])
        bias = s.sb("bias", [P, 2 * A_TILES])
        bvb = s.sb("bvb", [P, P])
        cst = s.sb("cst", [P, 8])
        g = s.sb("g", [P, 1])
        tg = s.sb("tg", [P, 1])
        stats = s.sb("stats", [P, BATCHES, 6])
        mv = s.sb("mv", [P, BATCHES, 2])
        var = s.sb("var", [P, BATCHES])
        half = s.sb("half", [P, BATCHES])
        zero = s.sb("zero", [P, DIM])
        rstd = s.sb("rstd", [P, BATCHES])
        xn = s.sb("xn", [P, DIM])
        xh = s.sb("xh", [P, DIM], F32R)
        xl = s.sb("xl", [P, DIM], F32R)
        ch = s.sb("ch", [P, DIM], F32R)
        cl = s.sb("cl", [P, DIM], F32R)
        full = s.sb("full", [P, 2, A_TILES, DIM])
        hi = s.sb("hi", [P, 2, A_TILES, DIM], F32R)
        qs = s.sb("qs", [P, 2, A_TILES, DIM], F32R)
        ks = s.sb("ks", [P, 2, A_TILES, DIM], F32R)
        vT = s.sb("vT", [P, 2, 2, A_HEADS, A_ROWS])
        vf = s.sb("vf", [P, P])
        mx = s.sb("mx", [P, 2, 2, A_HEADS])
        mT = s.sb("mT", [A_HEADS, 2, DIM], F32R)
        PR = 8
        prob = s.sb("prob", [P, PR, 2, DIM])
        osb = s.sb("osb", [P, 2, A_TILES, DIM])
        num = s.sb("num", [P, 2, DIM])
        den = s.sb("den", [P, 2, DIM])
        rden = s.sb("rden", [P, DIM])
        tgm = s.sb("tgm", [P, BATCHES, DIM])
        add = s.sb("add", [P, DIM])
        ident = res["ident"]
        proj = s.ps("proj", [P, A_TILES, DIM])
        s1 = [s.ps(f"s1_{k}", [P, 2, DIM]) for k in range(2)]
        s2 = [s.ps(f"s2_{k}", [P, 2, DIM]) for k in range(2)]
        out = s.ps("out", [P, A_TILES, DIM])

        ld_w, ld_x = s.sem("ld_w"), s.sem("ld_x")
        w_split, setup = s.sem("w_split"), s.sem("setup")
        v_own, p_own, a_own = s.sem("v_own"), s.sem("p_own"), s.sem("a_own")
        stats_ready, xn_ready = s.sem("stats_ready"), s.sem("xn_ready")
        parts_ready = s.sem("parts_ready")
        q_psum, k_psum, v_psum = s.sem("q_psum"), s.sem("k_psum"), s.sem("v_psum")
        q_full, k_full, v_full = s.sem("q_full"), s.sem("k_full"), s.sem("v_full")
        q_hi, k_hi = s.sem("q_hi"), s.sem("k_hi")
        q_stack, k_stack = s.sem("q_stack"), s.sem("k_stack")
        s1_psum, max_ready = s.sem("s1_psum"), s.sem("max_ready")
        mT_psum, mT_ready, m_in = s.sem("mT_psum"), s.sem("mT_ready"), s.sem("m_in")
        s2_psum, prob_ready = s.sem("s2_psum"), s.sem("prob_ready")
        out_psum, out_copied = s.sem("out_psum"), s.sem("out_copied")
        sent = [s.sem(f"sent{p}") for p in range(2)]
        moved = [s.sem(f"moved{p}") for p in range(2)]
        heads = nc.dram_tensor("a_heads", (2, 2, P, DIM), F32, kind="Internal").ap()
        rstd_ready, ln_own, vf_ready = s.sem("rstd_ready"), s.sem("ln_own"), s.sem("vf_ready")
        rden_ready = s.sem("rden_ready")
        x_done, tg_ready, tgm_ready = s.sem("x_done"), s.sem("tg_ready"), s.sem("tgm_ready")
        STEPS = BATCHES
        UNITS = A_HEADS

        with nc.Block() as block:

            @block.sync
            def _(sp):
                for h in range(2):
                    b = slice(8 * h, 8 * h + 8)
                    sp.dma_start(x_sb[:, b, :], src[b].rearrange("b p n -> p b n")).then_inc(ld_x, 16)
                sp.dma_start(wraw[:, 0:512], wq4).then_inc(ld_w, 16)
                sp.dma_start(wraw[:, 512:1024], wk4).then_inc(ld_w, 16)
                sp.dma_start(wraw[:, 1024:1152], wv).then_inc(ld_w, 16)
                sp.dma_start(bcol[:, 0:4], bq4).then_inc(ld_w, 16)
                sp.dma_start(bcol[:, 4:8], bk4).then_inc(ld_w, 16)
                sp.dma_start(bvb[:, :], bv.broadcast_to([P, P])).then_inc(ld_w, 16)
                sp.dma_start(cst[:, :], consts).then_inc(ld_w, 16)
                sp.dma_start(g[:, :], gate.broadcast_to([P, 1])).then_inc(ld_w, 16)
                sp.dma_start(smT[:, :], maskT).then_inc(ld_w, 16)
                for b in range(BATCHES):
                    sp.dma_start(tm[:, b, :], mask[b:b + 1, :].broadcast_to([P, DIM])).then_inc(ld_w, 16)
                for h in range(2):
                    b = slice(8 * h, 8 * h + 8)
                    sp.dma_start(ctx_sb[:, b, :], ctx_in[b].rearrange("b p n -> p b n")).then_inc(ld_x, 16)

                def maxima(n, p):
                    settled(sp, mT_ready, n + 1, (ld_w, 16 * (9 + BATCHES)))
                    for r in range(A_SLOTS):
                        row = A_ROWS * r + 27
                        sp.dma_start(qs[row:row + 1, p, :, :].bitcast(F32),
                                     mT[A_TILES * r:A_TILES * r + A_TILES, p, :].bitcast(F32)).then_inc(m_in, 16)

                def body(i, p):
                    n = i * 2 + p
                    if not (isinstance(n, int) and n + 1 >= STEPS):
                        maxima(n + 1, 1 - p)
                    settled(sp, out_copied, n + 1, (ld_w, 16 * (9 + BATCHES)))
                    for r in range(A_SLOTS):
                        a = A_ROWS * r
                        for part in range(2):
                            sp.dma_start(heads[p, part].rearrange("(r j d) t -> r d j t", r=A_SLOTS, j=A_TILES)[r],
                                         osb[a + A_HD * part:a + A_HD * part + A_HD, p, :, :])\
                              .then_inc(sent[p], 16)
                    settled(sp, sent[p], 128 * (i + 1), (ld_w, 16 * (9 + BATCHES)))
                    settled(sp, x_done, 3 * (n - 1), (ld_w, 16 * (9 + BATCHES)))
                    sp.dma_start(num[:, p, :], heads[p, 0]).then_inc(moved[p], 16)
                    sp.dma_start(den[:, p, :], heads[p, 1]).then_inc(moved[p], 16)

                maxima(0, 0)
                pairs(sp, STEPS, body)

            @block.gpsimd
            def _(pool):
                pool.memset(half[:, :], -0.5).then_inc(p_own, 1)
                pool.memset(zero[:, :], 0.0).then_inc(p_own, 1)
                pool.memset(vT[:, :, :, :, :], 0.0).then_inc(p_own, 1)
                pool.wait_ge(p_own, 3)
                pool.memset(vT[:, :, :, :, A_HD:2 * A_HD], 1.0).then_inc(setup, 1)

                def prologue(n):
                    pool.wait_ge(xn_ready, n + 1)
                    after(pool, v_psum, n)
                    pool.tensor_tensor(xh[:, :], xn[:, :], zero[:, :], ALU.add).then_inc(p_own, 1)
                    pool.tensor_copy(ch[:, :], ctx_sb[:, ds(n, 1), :]).then_inc(p_own, 1)
                    pool.wait_ge(p_own, 2 * n + 5)
                    pool.tensor_tensor(xl[:, :], xn[:, :], xh[:, :].bitcast(F32), ALU.subtract)\
                        .then_inc(parts_ready, 1)
                    pool.tensor_tensor(cl[:, :], ctx_sb[:, ds(n, 1), :], ch[:, :].bitcast(F32), ALU.subtract)\
                        .then_inc(parts_ready, 1)

                def finish(n, i, p):
                    pool.wait_ge(rden_ready, n + 1)
                    after(pool, x_done, 3 * n)
                    pool.tensor_tensor(add[:, :], num[:, p, :], rden[:, :], ALU.mult).then_inc(x_done, 1)
                    pool.wait_ge(x_done, 3 * n + 1)
                    pool.tensor_tensor(add[:, :], add[:, :], tgm[:, ds(n, 1), :], ALU.mult).then_inc(x_done, 1)
                    pool.wait_ge(x_done, 3 * n + 2)
                    pool.tensor_tensor(x_sb[:, ds(n, 1), :], x_sb[:, ds(n, 1), :], add[:, :], ALU.add)\
                        .then_inc(x_done, 1)

                def body(i, p):
                    n = i * 2 + p
                    if not (isinstance(n, int) and n + 2 >= STEPS):
                        prologue(n + 2)
                    if not (isinstance(n, int) and n == 0):
                        finish(n - 1, i - 1 + p, 1 - p)

                pool.wait_ge(tgm_ready, 1)
                pool.wait_ge(stats_ready, 1)
                pool.tensor_tensor(rstd[:, :], var[:, :], half[:, :], ALU.pow).then_inc(rstd_ready, 1)
                pool.wait_ge(ld_x, 64)
                prologue(0)
                prologue(1)
                pairs(pool, STEPS, body)
                finish(STEPS - 1, STEPS // 2 - 1, 1)

            @block.scalar
            def _(act):
                act.wait_ge(ld_w, 16 * (9 + BATCHES))
                act.activation(wh[:, :], wraw[:, :], ACT.Copy).then_inc(w_split, 1)
                act.activation(tg[:, :], g[:, :], ACT.Tanh).then_inc(tg_ready, 1)
                act.wait_ge(tg_ready, 1)
                act.activation(tgm[:, :, :], tm[:, :, :], ACT.Copy, scale=tg[:, 0:1]).then_inc(tgm_ready, 1)

                def evacuate(n, kind):
                    full_s, hi_s = ((q_full, q_hi), (k_full, k_hi))[kind]
                    act.wait_ge(full_s, A_TILES * (n + 1))
                    act.activation(hi[:, kind, :, :], full[:, kind, :, :], ACT.Copy).then_inc(hi_s, 1)

                def body(i, p):
                    n = i * 2 + p
                    for u in range(UNITS):
                        if u % A_SLOTS == 0:
                            after(act, out_psum, n * A_TILES + u // A_SLOTS + 1 - PR // A_SLOTS)
                        act.wait_ge(s2_psum, n * UNITS + u + 1)
                        act.activation(prob[:, u % PR, :, :], s2[u % 2][:, :, :], ACT.Exp,
                                       scale=1.0 / A_ROOT).then_inc(prob_ready, 1)
                    if not (isinstance(n, int) and n + 2 >= STEPS):
                        evacuate(n + 2, 0)
                        evacuate(n + 2, 1)
                    act.wait_ge(out_psum, (n + 1) * A_TILES)
                    after(act, x_done, 3 * (n - 1))
                    act.activation(osb[:, p, :, :], out[:, :, :], ACT.Copy).then_inc(out_copied, 1)

                for n in range(2):
                    evacuate(n, 0)
                    evacuate(n, 1)
                pairs(act, STEPS, body)

            @block.tensor
            def _(pe):
                pe.wait_ge(w_split, 2)

                def project(n, kind):
                    if kind == 0:
                        pe.wait_ge(parts_ready, 2 * n + 2)
                        after(pe, v_full, 2 * n)
                    else:
                        pe.wait_ge(q_full, A_TILES * (n + 1))
                    h, l, done = ((xh, xl, q_psum), (ch, cl, k_psum))[kind]
                    for j in range(A_TILES):
                        w = slice(512 * kind + P * j, 512 * kind + P * j + P)
                        if kind == 0 and j == 2:
                            after(pe, mT_ready, n)
                        pe.matmul(proj[:, j, :], wh[:, w], h[:, :], start=True, stop=False)
                        pe.matmul(proj[:, j, :], wh[:, w], l[:, :], start=False, stop=False)
                        mm = pe.matmul(proj[:, j, :], wl[:, w], h[:, :], start=False, stop=True)
                        if j % 2:
                            mm.then_inc(done, 1)

                def project_v(n):
                    pe.wait_ge(k_full, A_TILES * (n + 1))
                    w = slice(1024, 1152)
                    for t in range(2):
                        c = slice(P * t, P * t + P)
                        o = proj[:, t, 0:P]
                        pe.matmul(o, ch[:, c], wh[:, w], start=True, stop=False)
                        pe.matmul(o, ch[:, c], wl[:, w], start=False, stop=False)
                        mm = pe.matmul(o, cl[:, c], wh[:, w], start=False, stop=True)
                    mm.then_inc(v_psum, 1)

                def first_scores(n, p, u):
                    j, r = divmod(u, A_SLOTS)
                    rows = slice(A_ROWS * r, A_ROWS * r + A_ROWS)
                    if u == 0:
                        pe.wait_ge(q_stack, n + 1)
                        pe.wait_ge(k_stack, n + 1)
                    after(pe, max_ready, n * UNITS + u - 1)
                    for t in range(2):
                        mm = pe.matmul(s1[u % 2][:, t, :], qs[rows, p, j, P * t:P * t + P], ks[rows, p, j, :],
                                       start=True, stop=True)
                    mm.then_inc(s1_psum, 1)

                def turn_maxima(n, p):
                    pe.wait_ge(max_ready, (n + 1) * UNITS)
                    pe.wait_ge(v_full, 2 * (n + 1))
                    for t in range(2):
                        mm = pe.transpose(proj[0:A_HEADS, 2, P * t:P * t + P], mx[:, p, t, :], ident[:, :])
                    mm.then_inc(mT_psum, 1)

                def second_scores(n, p, u):
                    j, r = divmod(u, A_SLOTS)
                    rows = slice(A_ROWS * r, A_ROWS * r + A_ROWS)
                    if u == 0:
                        pe.wait_ge(m_in, 64 * (n + 1))
                    after(pe, prob_ready, n * UNITS + u - 1)
                    for t in range(2):
                        mm = pe.matmul(s2[u % 2][:, t, :], ks[rows, p, j, P * t:P * t + P], qs[rows, p, j, :],
                                       start=True, stop=True)
                    mm.then_inc(s2_psum, 1)

                def weigh(n, p, j):
                    pe.wait_ge(prob_ready, n * UNITS + A_SLOTS * (j + 1))
                    if j == 0:
                        pe.wait_ge(v_full, 2 * (n + 1))
                        after(pe, out_copied, n)
                    for t in range(2):
                        for r in range(A_SLOTS):
                            mm = pe.matmul(out[A_ROWS * r:A_ROWS * r + A_ROWS, j, :],
                                           vT[:, p, t, A_TILES * r + j, :],
                                           prob[:, (A_SLOTS * j + r) % PR, t, :], start=(t == 0), stop=(t == 1),
                                           skip_group_check=True)
                    mm.then_inc(out_psum, 1)

                def body(i, p):
                    n = i * 2 + p
                    more = not (isinstance(n, int) and n + 1 >= STEPS)
                    for u in range(UNITS):
                        second_scores(n, p, u)
                        if u >= 2 and (u - 2) % A_SLOTS == A_SLOTS - 1:
                            weigh(n, p, (u - 2) // A_SLOTS)
                        if more and u == 0:
                            project_v(n + 1)
                        if more and 3 <= u < 11:
                            first_scores(n + 1, 1 - p, 2 * u - 6)
                            first_scores(n + 1, 1 - p, 2 * u - 5)
                        if more and u == 12:
                            turn_maxima(n + 1, 1 - p)
                        if u in (13, 14) and not (isinstance(n, int) and n + 2 >= STEPS):
                            project(n + 2, u - 13)
                    weigh(n, p, A_TILES - 1)

                project(0, 0)
                project(0, 1)
                project_v(0)
                for u in range(UNITS):
                    first_scores(0, 0, u)
                turn_maxima(0, 0)
                project(1, 0)
                project(1, 1)
                pairs(pe, STEPS, body)

            @block.vector
            def _(dve):
                dve.wait_ge(ld_x, 64)
                for b in range(BATCHES):
                    dve.bn_stats(stats[:, b, :], x_sb[:, b, :]).then_inc(ln_own, 1)
                for b in range(BATCHES):
                    dve.wait_ge(ln_own, b + 1)
                    dve.bn_aggr(mv[:, b, :], stats[:, b, :]).then_inc(ln_own, 1)
                dve.wait_ge(ln_own, 2 * BATCHES)
                dve.tensor_scalar(var[:, :], mv[:, :, 1], 1e-5, None, ALU.add).then_inc(stats_ready, 1)
                dve.wait_ge(w_split, 1)
                dve.wait_ge(ld_w, 16 * (9 + BATCHES))
                dve.wait_ge(setup, 1)
                dve.tensor_tensor(wl[:, :], wraw[:, :], wh[:, :].bitcast(F32), ALU.subtract).then_inc(w_split, 1)
                dve.tensor_scalar(bias[:, 0:4], bcol[:, 0:4], cst[:, 4:5], None, ALU.add)
                dve.tensor_scalar(bias[:, 4:8], bcol[:, 4:8], cst[:, 5:6], None, ALU.add)
                dve.tensor_scalar(km[:, :, :], tm[:, :, :], cst[:, 2:3], cst[:, 3:4], ALU.mult, ALU.add)\
                   .then_inc(v_own, 1)
                dve.wait_ge(v_own, 1)

                def layernorm(n):
                    after(dve, parts_ready, 2 * n)
                    dve.tensor_scalar(xn[:, :], x_sb[:, ds(n, 1), :], mv[:, ds(n, 1), 0:1], rstd[:, ds(n, 1)],
                                      ALU.subtract, ALU.mult).then_inc(xn_ready, 1)

                def read_projection(n, kind):
                    psum_s, full_s = ((q_psum, q_full), (k_psum, k_full))[kind]
                    m = (tm, km)[kind]
                    after(dve, (q_stack, k_stack)[kind], n)
                    for j in range(A_TILES):
                        dve.wait_ge(psum_s, 2 * n + j // 2 + 1)
                        dve.scalar_tensor_tensor(full[:, kind, j, :], proj[:, j, :],
                                                 bias[:, 4 * kind + j:4 * kind + j + 1], m[:, ds(n, 1), :],
                                                 ALU.add, ALU.mult).then_inc(full_s, 1)

                def stack_parts(n, p, kind):
                    hi_s, stack_s = ((q_hi, q_stack), (k_hi, k_stack))[kind]
                    t = (qs, ks)[kind]
                    dve.wait_ge(hi_s, n + 1)
                    after(dve, s2_psum, UNITS * (n - 1))
                    dve.scalar_tensor_tensor(t[:, p, :, :], hi[:, kind, :, :].bitcast(F32), cst[:, kind:kind + 1],
                                             full[:, kind, :, :], ALU.mult, ALU.add).then_inc(stack_s, 1)

                def read_v(n, p):
                    dve.wait_ge(v_psum, n + 1)
                    after(dve, out_psum, A_TILES * (n - 1))
                    for t in range(2):
                        after(dve, v_full, 2 * n + t)
                        dve.tensor_tensor(vf[:, :], proj[:, t, 0:P], bvb[:, :], ALU.add).then_inc(vf_ready, 1)
                        dve.wait_ge(vf_ready, 2 * n + t + 1)
                        dve.tensor_scalar(vT[:, p, t, :, 0:A_HD], vf[:, :].rearrange("p (h d) -> p h d", h=A_HEADS),
                                          smT[:, ds(n * 2 + t, 1)], None, ALU.mult).then_inc(v_full, 1)

                def take_max(n, p, u):
                    dve.wait_ge(s1_psum, n * UNITS + u + 1)
                    h = A_TILES * (u % A_SLOTS) + u // A_SLOTS
                    dve.tensor_reduce(mx[:, p, :, h], s1[u % 2][:, :, :], AX.X, ALU.max).then_inc(max_ready, 1)

                def read_maxima(n, p):
                    dve.wait_ge(mT_psum, n + 1)
                    dve.tensor_scalar(mT[:, p, :], proj[0:A_HEADS, 2, :], -1.0, None, ALU.mult).then_inc(mT_ready, 1)

                def invert(n, i, p):
                    dve.wait_ge(moved[p], 32 * (i + 1))
                    after(dve, x_done, 3 * (n - 1) + 1)
                    dve.reciprocal(rden[:, :], den[:, p, :]).then_inc(rden_ready, 1)

                def body(i, p):
                    n = i * 2 + p
                    more = not (isinstance(n, int) and n + 2 >= STEPS)
                    if isinstance(n, int) and n + 1 >= STEPS:
                        invert(n - 1, i - 1 + p, 1 - p)
                        invert(n, i, p)
                        return
                    stack_parts(n + 1, 1 - p, 0)
                    stack_parts(n + 1, 1 - p, 1)
                    read_v(n + 1, 1 - p)
                    if more:
                        layernorm(n + 2)
                    for u in range(UNITS):
                        take_max(n + 1, 1 - p, u)
                        if u == 13 and not (isinstance(n, int) and n == 0):
                            invert(n - 1, i - 1 + p, 1 - p)
                    read_maxima(n + 1, 1 - p)
                    if more:
                        read_projection(n + 2, 0)
                        read_projection(n + 2, 1)

                dve.wait_ge(rstd_ready, 1)
                layernorm(0)
                read_projection(0, 0)
                read_projection(0, 1)
                stack_parts(0, 0, 0)
                stack_parts(0, 0, 1)
                read_v(0, 0)
                layernorm(1)
                for u in range(UNITS):
                    take_max(0, 0, u)
                read_maxima(0, 0)
                read_projection(1, 0)
                read_projection(1, 1)
                pairs(dve, STEPS, body)


def bit_linear_ffn(nc, res, gate_w, val_w, out_w, gate_b, val_b, out_b, gate):
    x_sb, ident = res["x"], res["ident"]
    HID = 4 * DIM
    HT = HID // P
    HALF = HID // 2
    with ExitStack() as stack:
        s = Scope(nc, stack, "b")
        raw = s.sb("raw", [P, 3, KT * HID])
        tmp = s.sb("tmp", [P, 2, KT * HID])
        wq = s.sb("wq", [P, 3, KT * HID], BF16)
        bb = s.sb("bb", [P, 2, HID])
        obb = s.sb("obb", [P, DIM])
        g = s.sb("g", [P, 1])
        tg = s.sb("tg", [P, 1])
        identb = s.sb("identb", [P, P], BF16)
        ones = s.sb("ones", [P, P])
        wabs = s.sb("wabs", [P, 3])
        gw = s.sb("gw", [P, 3])
        rgw = s.sb("rgw", [P, 3])
        gw127 = s.sb("gw127", [P, 3])
        stats = s.sb("stats", [P, BATCHES, 6])
        mv = s.sb("mv", [P, BATCHES, 2])
        var = s.sb("var", [P, BATCHES])
        half = s.sb("half", [P, BATCHES])
        rstd = s.sb("rstd", [P, BATCHES])
        xn = s.sb("xn", [P, BATCHES, DIM])
        gx = s.sb("gx", [P, BATCHES])
        rx = s.sb("rx", [P, BATCHES])
        sx = s.sb("sx", [P, BATCHES])
        sc = s.sb("sc", [P, BATCHES, 2])
        xr = s.sb("xr", [P, DIM])
        xq = s.sb("xq", [P, 2, DIM], BF16)
        xqT = s.sb("xqT", [P, 2, KT, P], BF16)
        gt = s.sb("gt", [P, HID])
        gs = s.sb("gs", [P, HID])
        vt = s.sb("vt", [P, HID])
        h = s.sb("h", [P, HID])
        gh = s.sb("gh", [P, 4])
        hr = s.sb("hr", [P, HID])
        hq = s.sb("hq", [P, HID], BF16)
        hqT = s.sb("hqT", [P, HT, P], BF16)
        so = s.sb("so", [P, 2])
        y = s.sb("y", [P, DIM])
        gv = [s.ps(f"gv{k}", [P, HALF]) for k in range(4)]
        hT_ps = s.ps("hT", [P, HT, P], BF16)
        xT_ps = s.ps("xT", [P, KT, P], BF16)
        o_ps = s.ps("o", [P, DIM])
        w_ps = s.ps("w", [P, 4])

        ld_w, ld_b = s.sem("ld_w"), s.sem("ld_b")
        consts_ready, tanh_ready = s.sem("consts_ready"), s.sem("tanh_ready")
        own = s.sem("own")
        stats_ready, rstd_ready = s.sem("stats_ready"), s.sem("rstd_ready")
        wabs_ready, wabs_psum, weights_ready = s.sem("wabs_ready"), s.sem("wabs_psum"), s.sem("weights_ready")
        xr_ready, xq_ready = s.sem("xr_ready"), s.sem("xq_ready")
        xT_psum, xT_ready = s.sem("xT_psum"), s.sem("xT_ready")
        gv_psum, gt_ready, silu_ready, vt_ready = s.sem("gv_psum"), s.sem("gt_ready"), s.sem("silu_ready"), s.sem("vt_ready")
        h_own, hq_ready = s.sem("h_own"), s.sem("hq_ready")
        hT_psum, hT_ready = s.sem("hT_psum"), s.sem("hT_ready")
        o_psum, y_ready, x_done = s.sem("o_psum"), s.sem("y_ready"), s.sem("x_done")
        H_OWN = 7

        def following(n, k):
            return not (isinstance(n, int) and n + k >= BATCHES)

        with nc.Block() as block:

            @block.sync
            def _(sp):
                for k, w in enumerate((gate_w, val_w, out_w)):
                    sp.dma_start(raw[:, k, :], w).then_inc(ld_w, 16)
                sp.dma_start(bb[:, 0, :], gate_b.broadcast_to([P, HID])).then_inc(ld_b, 16)
                sp.dma_start(bb[:, 1, :], val_b.broadcast_to([P, HID])).then_inc(ld_b, 16)
                sp.dma_start(obb[:, :], out_b.broadcast_to([P, DIM])).then_inc(ld_b, 16)
                sp.dma_start(g[:, :], gate.broadcast_to([P, 1])).then_inc(ld_b, 16)

            @block.gpsimd
            def _(pool):
                pool.memset(half[:, :], -0.5).then_inc(consts_ready, 1)
                pool.memset(ones[:, :], 1.0).then_inc(consts_ready, 1)
                pool.tensor_copy(identb[:, :], ident[:, :]).then_inc(consts_ready, 1)
                pool.wait_ge(consts_ready, 3)
                pool.wait_ge(stats_ready, 1)
                pool.tensor_tensor(rstd[:, :], var[:, :], half[:, :], ALU.pow).then_inc(rstd_ready, 1)

            @block.scalar
            def _(act):
                act.wait_ge(ld_b, 64)
                act.activation(tg[:, :], g[:, :], ACT.Tanh).then_inc(tanh_ready, 1)

                def turned_x(n, p):
                    act.wait_ge(xT_psum, n + 1)
                    act.activation(xqT[:, p, :, :], xT_ps[:, :, :], ACT.Copy).then_inc(xT_ready, 1)

                def silu(n, c):
                    act.wait_ge(gt_ready, 2 * n + c + 1)
                    act.activation(gs[:, HALF * c:HALF * c + HALF], gt[:, HALF * c:HALF * c + HALF], ACT.Silu)\
                        .then_inc(silu_ready, 1)

                def body(i, p):
                    n = i * 2 + p
                    if following(n, 1):
                        silu(n + 1, 0)
                    act.wait_ge(hT_psum, n + 1)
                    act.activation(hqT[:, :, :], hT_ps[:, :, :], ACT.Copy).then_inc(hT_ready, 1)
                    if following(n, 1):
                        silu(n + 1, 1)
                    if following(n, 2):
                        turned_x(n + 2, p)

                turned_x(0, 0)
                silu(0, 0)
                silu(0, 1)
                turned_x(1, 1)
                pairs(act, BATCHES, body)

            @block.tensor
            def _(pe):
                pe.wait_ge(consts_ready, 3)
                pe.wait_ge(wabs_ready, 3)
                pe.matmul(w_ps[:, 0:3], ones[:, :], wabs[:, :], start=True, stop=True).then_inc(wabs_psum, 1)

                def turn_x(n, p):
                    pe.wait_ge(xq_ready, n + 1)
                    after(pe, xT_ready, n)
                    for k in range(KT):
                        mm = pe.transpose(xT_ps[:, k, :], xq[:, p, P * k:P * k + P], identb[:, :])
                    mm.then_inc(xT_psum, 1)

                def gate_and_value(n, p):
                    pe.wait_ge(xT_ready, n + 1)
                    for c in range(4):
                        w, half_ = c // 2, c % 2
                        after(pe, (gt_ready, vt_ready)[w], 2 * n + half_ - 1)
                        for k in range(KT):
                            col = HID * k + HALF * half_
                            mm = pe.matmul(gv[c][:, :], xqT[:, p, k, :], wq[:, w, col:col + HALF],
                                           start=(k == 0), stop=(k == KT - 1))
                        mm.then_inc(gv_psum, 1)

                def turn_h(n):
                    pe.wait_ge(hq_ready, n + 1)
                    after(pe, hT_ready, n)
                    for k in range(HT):
                        mm = pe.transpose(hT_ps[:, k, :], hq[:, P * k:P * k + P], identb[:, :])
                    mm.then_inc(hT_psum, 1)

                def project(n):
                    pe.wait_ge(hT_ready, n + 1)
                    after(pe, y_ready, n)
                    for k in range(HT):
                        mm = pe.matmul(o_ps[:, :], hqT[:, k, :], wq[:, 2, DIM * k:DIM * k + DIM],
                                       start=(k == 0), stop=(k == HT - 1))
                    mm.then_inc(o_psum, 1)

                def body(i, p):
                    n = i * 2 + p
                    if following(n, 1):
                        gate_and_value(n + 1, 1 - p)
                    turn_h(n)
                    project(n)
                    if following(n, 2):
                        turn_x(n + 2, p)

                turn_x(0, 0)
                pe.wait_ge(weights_ready, 3)
                gate_and_value(0, 0)
                turn_x(1, 1)
                pairs(pe, BATCHES, body)

            @block.vector
            def _(dve):
                n_own = [0]

                def chained(ins):
                    n_own[0] += 1
                    ins.then_inc(own, 1)
                    dve.wait_ge(own, n_own[0])

                for b in range(BATCHES):
                    dve.bn_stats(stats[:, b, :], x_sb[:, b, :]).then_inc(own, 1)
                n_own[0] = BATCHES
                dve.wait_ge(own, n_own[0])
                for b in range(BATCHES):
                    dve.bn_aggr(mv[:, b, :], stats[:, b, :]).then_inc(own, 1)
                n_own[0] += BATCHES
                dve.wait_ge(own, n_own[0])
                dve.tensor_scalar(var[:, :], mv[:, :, 1], 1e-5, None, ALU.add).then_inc(stats_ready, 1)
                dve.wait_ge(rstd_ready, 1)
                for b in range(BATCHES):
                    dve.tensor_scalar(xn[:, b, :], x_sb[:, b, :], mv[:, b, 0:1], rstd[:, b:b + 1],
                                      ALU.subtract, ALU.mult).then_inc(own, 1)
                n_own[0] += BATCHES
                dve.wait_ge(own, n_own[0])
                chained(dve.tensor_reduce(gx[:, :], xn[:, :, :], AX.X, ALU.max, apply_absolute_value=True))
                chained(dve.tensor_scalar(gx[:, :], gx[:, :], 1e-5, None, ALU.max))
                chained(dve.reciprocal(rx[:, :], gx[:, :]))
                chained(dve.tensor_scalar(sx[:, :], rx[:, :], 127.0, None, ALU.mult))

                def quantise_x(n, p):
                    after(dve, xq_ready, n)
                    dve.tensor_scalar(xr[:, :], xn[:, ds(n, 1), :], sx[:, ds(n, 1)], ROUND, ALU.mult, ALU.add)\
                       .then_inc(xr_ready, 1)
                    dve.wait_ge(xr_ready, n + 1)
                    after(dve, xT_psum, n - 1)
                    dve.tensor_scalar(xq[:, p, :], xr[:, :], ROUND, 127.0, ALU.subtract, ALU.min)\
                       .then_inc(xq_ready, 1)

                for n in range(2):
                    if n == 1:
                        dve.wait_ge(ld_w, 48)
                        for k in range(3):
                            dve.tensor_reduce(wabs[:, k:k + 1], raw[:, k, :], AX.X, ALU.add,
                                              apply_absolute_value=True).then_inc(wabs_ready, 1)
                        dve.wait_ge(wabs_psum, 1)
                        chained(dve.tensor_scalar(gw[:, :], w_ps[:, 0:3], 1.0 / (DIM * HID), 1e-5, ALU.mult, ALU.max))
                        chained(dve.reciprocal(rgw[:, :], gw[:, :]))
                        chained(dve.tensor_scalar(gw127[:, :], gw[:, :], 1.0 / 127.0, None, ALU.mult))
                        for w in range(2):
                            chained(dve.tensor_scalar(sc[:, :, w], gx[:, :], gw127[:, w:w + 1], None, ALU.mult))
                        for k in range(3):
                            chained(dve.tensor_scalar(tmp[:, 0, :], raw[:, k, :], rgw[:, k:k + 1], ROUND,
                                                      ALU.mult, ALU.add))
                            chained(dve.tensor_scalar(tmp[:, 1, :], tmp[:, 0, :], ROUND, 1.0, ALU.subtract, ALU.min))
                            dve.tensor_scalar(wq[:, k, :], tmp[:, 1, :], -1.0, None, ALU.max)\
                               .then_inc(weights_ready, 1)
                            dve.wait_ge(weights_ready, k + 1)
                    quantise_x(n, n % 2)
                dve.wait_ge(ld_b, 64)
                dve.wait_ge(tanh_ready, 1)

                def hidden(n):
                    base = H_OWN * n
                    for c in range(4):
                        w, half_ = c // 2, c % 2
                        cols = slice(HALF * half_, HALF * half_ + HALF)
                        dve.wait_ge(gv_psum, 4 * n + c + 1)
                        if w == 0:
                            after(dve, silu_ready, 2 * n + half_ - 1)
                        dve.scalar_tensor_tensor((gt, vt)[w][:, cols], gv[c][:, :], sc[:, ds(n, 1), w:w + 1],
                                                 bb[:, w, cols], ALU.mult, ALU.add)\
                           .then_inc((gt_ready, vt_ready)[w], 1)
                    dve.wait_ge(silu_ready, 2 * n + 2)
                    dve.wait_ge(vt_ready, 2 * n + 2)
                    dve.tensor_tensor(h[:, :], gs[:, :], vt[:, :], ALU.mult).then_inc(h_own, 1)
                    dve.wait_ge(h_own, base + 1)
                    dve.tensor_reduce(gh[:, 0:1], h[:, :], AX.X, ALU.max, apply_absolute_value=True).then_inc(h_own, 1)
                    dve.wait_ge(h_own, base + 2)
                    dve.tensor_scalar(gh[:, 1:2], gh[:, 0:1], 1e-5, None, ALU.max).then_inc(h_own, 1)
                    dve.wait_ge(h_own, base + 3)
                    dve.reciprocal(gh[:, 2:3], gh[:, 1:2]).then_inc(h_own, 1)
                    dve.wait_ge(h_own, base + 4)
                    dve.tensor_scalar(gh[:, 3:4], gh[:, 2:3], 127.0, None, ALU.mult).then_inc(h_own, 1)
                    dve.wait_ge(h_own, base + 5)
                    dve.tensor_scalar(hr[:, :], h[:, :], gh[:, 3:4], ROUND, ALU.mult, ALU.add).then_inc(h_own, 1)
                    dve.wait_ge(h_own, base + 6)
                    after(dve, hT_psum, n)
                    dve.tensor_scalar(hq[:, :], hr[:, :], ROUND, 127.0, ALU.subtract, ALU.min).then_inc(hq_ready, 1)

                def scale_out(n, p):
                    dve.tensor_scalar(so[:, p:p + 1], gh[:, 1:2], gw127[:, 2:3], None, ALU.mult).then_inc(h_own, 1)

                def finish(n, p):
                    dve.wait_ge(h_own, H_OWN * (n + 1))
                    dve.wait_ge(o_psum, n + 1)
                    after(dve, x_done, n)
                    dve.scalar_tensor_tensor(y[:, :], o_ps[:, :], so[:, p:p + 1], obb[:, :], ALU.mult, ALU.add)\
                       .then_inc(y_ready, 1)
                    dve.wait_ge(y_ready, n + 1)
                    dve.scalar_tensor_tensor(x_sb[:, ds(n, 1), :], y[:, :], tg[:, 0:1], x_sb[:, ds(n, 1), :],
                                             ALU.mult, ALU.add).then_inc(x_done, 1)

                def body(i, p):
                    n = i * 2 + p
                    if following(n, 2):
                        quantise_x(n + 2, p)
                    if following(n, 1):
                        hidden(n + 1)
                        scale_out(n + 1, 1 - p)
                    finish(n, p)

                hidden(0)
                scale_out(0, 0)
                pairs(dve, BATCHES, body)
                dve.wait_ge(x_done, BATCHES)

HEADS, HD = 16, 128
INNER = HEADS * HD
GB = 4
GROUPS = BATCHES // GB
QUADS = HEADS // 4
GT = GB * TOKENS
UNITS = GROUPS * 4


def prepare_tokens(nc, x_sb, ident, xn, xTh, xTl, eps, weight=None, centre=False):
    with ExitStack() as stack:
        s = Scope(nc, stack, f"{xTh.name}_norm")
        stats = s.sb("stats", [P, BATCHES, 6])
        mv = s.sb("mv", [P, BATCHES, 2])
        var = s.sb("var", [P, BATCHES])
        half = s.sb("half", [P, BATCHES])
        rstd = s.sb("rstd", [P, BATCHES])
        wb = s.sb("wb", [P, DIM])
        turned = [s.ps(f"turned{k}", [P, KT, 2, P]) for k in range(4)]
        ld, consts, own = s.sem("ld"), s.sem("consts"), s.sem("own")
        var_ready, rstd_ready, xn_ready = s.sem("var_ready"), s.sem("rstd_ready"), s.sem("xn_ready")
        turned_psum, hi_ready, lo_ready = s.sem("turned_psum"), s.sem("hi_ready"), s.sem("lo_ready")
        PAIRS = BATCHES // 2

        with nc.Block() as block:
            if weight is not None:
                @block.sync
                def _(sp):
                    sp.dma_start(wb[:, :], weight.broadcast_to([P, DIM])).then_inc(ld, 16)

            ROUNDS = 2 if centre else 1

            @block.gpsimd
            def _(pool):
                pool.memset(half[:, :], -0.5).then_inc(consts, 1)
                pool.wait_ge(consts, 1)
                for n in range(ROUNDS):
                    pool.wait_ge(var_ready, n + 1)
                    pool.tensor_tensor(rstd[:, :], var[:, :], half[:, :], ALU.pow).then_inc(rstd_ready, 1)

            @block.tensor
            def _(pe):
                for m in range(PAIRS):
                    pe.wait_ge(xn_ready, 2 * m + 2)
                    after(pe, lo_ready, m - 3)
                    for b in range(2):
                        for k in range(KT):
                            mm = pe.transpose(turned[m % 4][:, k, b, :], xn[:, 2 * m + b, P * k:P * k + P], ident[:, :])
                    mm.then_inc(turned_psum, 1)

            @block.scalar
            def _(act):
                for m in range(PAIRS):
                    act.wait_ge(turned_psum, m + 1)
                    act.activation(xTh[:, :, 2 * P * m:2 * P * m + 2 * P],
                                   turned[m % 4][:, :, :, :].rearrange("p k b t -> p k (b t)"), ACT.Copy)\
                        .then_inc(hi_ready, 1)

            @block.vector
            def _(dve):
                def statistics(n):
                    for b in range(BATCHES):
                        dve.bn_stats(stats[:, b, :], x_sb[:, b, :]).then_inc(own, 1)
                    dve.wait_ge(own, n + BATCHES)
                    for b in range(BATCHES):
                        dve.bn_aggr(mv[:, b, :], stats[:, b, :]).then_inc(own, 1)
                    dve.wait_ge(own, n + 2 * BATCHES)

                counted = 0
                if centre:
                    statistics(0)
                    dve.tensor_scalar(var[:, :], mv[:, :, 1], 1e-5, None, ALU.add).then_inc(var_ready, 1)
                    dve.wait_ge(rstd_ready, 1)
                    for b in range(BATCHES):
                        dve.tensor_scalar(x_sb[:, b, :], x_sb[:, b, :], mv[:, b, 0:1], rstd[:, b:b + 1],
                                          ALU.subtract, ALU.mult).then_inc(own, 1)
                    counted = 3 * BATCHES
                    dve.wait_ge(own, counted)
                statistics(counted)
                if weight is None:
                    dve.tensor_scalar(var[:, :], mv[:, :, 1], eps, None, ALU.add).then_inc(var_ready, 1)
                else:
                    dve.tensor_tensor(var[:, :], mv[:, :, 0], mv[:, :, 0], ALU.mult).then_inc(own, 1)
                    dve.wait_ge(own, counted + 2 * BATCHES + 1)
                    dve.scalar_tensor_tensor(var[:, :], var[:, :], eps, mv[:, :, 1], ALU.add, ALU.add)\
                       .then_inc(var_ready, 1)
                    dve.wait_ge(ld, 16)
                dve.wait_ge(rstd_ready, ROUNDS)

                def normalise(b):
                    if weight is None:
                        dve.tensor_scalar(xn[:, b, :], x_sb[:, b, :], mv[:, b, 0:1], rstd[:, b:b + 1],
                                          ALU.subtract, ALU.mult).then_inc(xn_ready, 1)
                    else:
                        dve.scalar_tensor_tensor(xn[:, b, :], x_sb[:, b, :], rstd[:, b:b + 1], wb[:, :],
                                                 ALU.mult, ALU.mult).then_inc(xn_ready, 1)

                for b in range(4):
                    normalise(b)
                for m in range(PAIRS):
                    if m < PAIRS - 2:
                        normalise(2 * m + 4)
                        normalise(2 * m + 5)
                    dve.wait_ge(hi_ready, m + 1)
                    cols = slice(2 * P * m, 2 * P * m + 2 * P)
                    dve.tensor_tensor(xTl[:, :, cols], turned[m % 4][:, :, :, :].rearrange("p k b t -> p k (b t)"),
                                      xTh[:, :, cols].bitcast(F32), ALU.subtract).then_inc(lo_ready, 1)


def row_norms(nc, ident, xn, xTh, xTl, cTh, cTl, rqs, nrqs, rkb, ctx_in, ctxT, wqT, wkT):
    with ExitStack() as stack:
        s = Scope(nc, stack, "r")
        GW = DIM + 2
        wT = s.sb("wT", [P, 2, HEADS, GW])
        ctx_sb = s.sb("ctx", [P, BATCHES, DIM])
        raw = s.sb("raw", [P, KT, BATCHES * TOKENS])
        gh = s.sb("gh", [P, 2, KT, DIM], F32R)
        gl = s.sb("gl", [P, 2, KT, DIM], F32R)
        row = s.sb("row", [1, 2, GW])
        one = s.sb("one", [1, P])
        onesq = s.sb("onesq", [P, P])
        half = s.sb("half", [P, 2, BATCHES])
        ssq = s.sb("ssq", [P, 2, BATCHES])
        bb = s.sb("bb", [P, 2, BATCHES])
        ms = s.sb("ms", [P, 2, BATCHES])
        rr = s.sb("rr", [P, 2, BATCHES])
        junk = s.sb("junk", [P, DIM])
        diag = s.sb("diag", [P, 2, P])
        g_ps = [s.ps(f"g{k}", [P, GW]) for k in range(2)]
        row_ps = s.ps("row_ps", [1, GW])
        y_ps = [s.ps(f"y{k}", [P, GW]) for k in range(2)]
        b_ps = [s.ps(f"b{k}", [P, P]) for k in range(2)]

        ld_w, ld_c, ld_ct = s.sem("ld_w"), s.sem("ld_c"), s.sem("ld_ct")
        consts, own = s.sem("consts"), s.sem("own")
        g_psum, row_psum, g_hi, g_lo, row_ready = (s.sem(n) for n in ("g_psum", "row_psum", "g_hi", "g_lo", "row_ready"))
        c_hi, c_lo = s.sem("c_hi"), s.sem("c_lo")
        y_psum, y_read, ms_ready, rr_ready = (s.sem(n) for n in ("y_psum", "y_read", "ms_ready", "rr_ready"))
        diag_ready, b_psum, rkb_ready = s.sem("diag_ready"), s.sem("b_psum"), s.sem("rkb_ready")

        with nc.Block() as block:

            @block.sync
            def _(sp):
                sp.dma_start(wT[:, 0, :, :], wqT).then_inc(ld_w, 16)
                sp.dma_start(wT[:, 1, :, :], wkT).then_inc(ld_w, 16)
                sp.dma_start(raw[:, :, :], ctxT).then_inc(ld_ct, 16)
                sp.dma_start(ctx_sb[:, :, :], ctx_in.rearrange("b p n -> p b n")).then_inc(ld_c, 16)

            @block.gpsimd
            def _(pool):
                pool.memset(half[:, :, :], -0.5).then_inc(consts, 1)
                pool.memset(one[:, :], 1.0).then_inc(consts, 1)
                pool.memset(onesq[:, :], 1.0).then_inc(consts, 1)
                pool.wait_ge(consts, 3)
                pool.wait_ge(ms_ready, 1)
                pool.tensor_tensor(rr[:, :, :], ms[:, :, :], half[:, :, :], ALU.pow).then_inc(rr_ready, 1)

            @block.scalar
            def _(act):
                for w in range(2):
                    for k in range(KT):
                        act.wait_ge(g_psum, KT * w + k + 1)
                        act.activation(gh[:, w, k, :], g_ps[k][:, 0:DIM], ACT.Copy).then_inc(g_hi, 1)
                    act.wait_ge(row_psum, w + 1)
                    act.activation(row[:, w, 0:DIM], row_ps[:, 0:DIM], ACT.Copy, scale=2.0).then_inc(row_ready, 1)
                    act.activation(row[:, w, DIM:GW], row_ps[:, DIM:GW], ACT.Copy).then_inc(row_ready, 1)
                    if w == 0:
                        act.wait_ge(ld_ct, 16)
                        act.activation(cTh[:, :, :], raw[:, :, :], ACT.Copy).then_inc(c_hi, 1)
                for b in range(BATCHES):
                    act.wait_ge(b_psum, b + 1)
                    act.activation(rkb[:, b, :], b_ps[b % 2][:, :], ACT.Copy).then_inc(rkb_ready, 1)

            @block.tensor
            def _(pe):
                pe.wait_ge(consts, 3)
                pe.wait_ge(ld_w, 32)
                for w in range(2):
                    for k in range(KT):
                        after(pe, g_lo, KT * (w - 1) + k + 1)
                        for h in range(HEADS):
                            mm = pe.matmul(g_ps[k][:, 0:DIM], wT[:, w, h, P * k:P * k + P], wT[:, w, h, 0:DIM],
                                           start=(h == 0), stop=(h == HEADS - 1))
                        mm.then_inc(g_psum, 1)
                    after(pe, row_ready, 2 * w)
                    for h in range(HEADS):
                        mm = pe.matmul(row_ps[:, :], wT[:, w, h, DIM:DIM + 1], wT[:, w, h, :],
                                       start=(h == 0), stop=(h == HEADS - 1))
                    mm.then_inc(row_psum, 1)
                n = 0
                for w in range(2):
                    th, tl = ((xTh, xTl), (cTh, cTl))[w]
                    pe.wait_ge(g_lo, KT * (w + 1))
                    pe.wait_ge(row_ready, 2 * (w + 1))
                    if w == 1:
                        pe.wait_ge(c_lo, 1)
                    for b in range(BATCHES):
                        y = y_ps[n % 2]
                        cols = slice(P * b, P * b + P)
                        after(pe, y_read, 2 * (n - 1))
                        pe.matmul(y[:, :], one[:, :], row[:, w, :], start=True, stop=False, skip_group_check=True)
                        for k in range(KT):
                            pe.matmul(y[:, 0:DIM], th[:, k, cols], gh[:, w, k, :], start=False, stop=False,
                                      skip_group_check=True)
                            pe.matmul(y[:, 0:DIM], th[:, k, cols], gl[:, w, k, :], start=False, stop=False,
                                      skip_group_check=True)
                            mm = pe.matmul(y[:, 0:DIM], tl[:, k, cols], gh[:, w, k, :], start=False,
                                           stop=(k == KT - 1), skip_group_check=True)
                        mm.then_inc(y_psum, 1)
                        n += 1
                for b in range(BATCHES):
                    pe.wait_ge(diag_ready, b + 1)
                    after(pe, rkb_ready, b - 1)
                    pe.matmul(b_ps[b % 2][:, :], onesq[:, :], diag[:, b % 2, :], start=True, stop=True).then_inc(b_psum, 1)

            @block.vector
            def _(dve):
                for w in range(2):
                    for k in range(KT):
                        dve.wait_ge(g_hi, KT * w + k + 1)
                        dve.tensor_tensor(gl[:, w, k, :], g_ps[k][:, 0:DIM], gh[:, w, k, :].bitcast(F32), ALU.subtract)\
                           .then_inc(g_lo, 1)
                dve.wait_ge(c_hi, 1)
                dve.tensor_tensor(cTl[:, :, :], raw[:, :, :], cTh[:, :, :].bitcast(F32), ALU.subtract).then_inc(c_lo, 1)
                dve.wait_ge(ld_c, 16)
                n = 0
                for w in range(2):
                    t = (xn, ctx_sb)[w]
                    for b in range(BATCHES):
                        dve.wait_ge(y_psum, n + 1)
                        after(dve, y_read, 2 * n)
                        dve.tensor_tensor_reduce(junk[:, :], y_ps[n % 2][:, 0:DIM], t[:, b, :], 1.0, 0.0, ALU.mult,
                                                 ALU.add, ssq[:, w, b:b + 1]).then_inc(y_read, 1)
                        dve.tensor_copy(bb[:, w, b:b + 1], y_ps[n % 2][:, DIM:DIM + 1]).then_inc(y_read, 1)
                        n += 1
                dve.wait_ge(y_read, 2 * n)
                dve.tensor_tensor(ms[:, :, :], ssq[:, :, :], bb[:, :, :], ALU.add).then_inc(own, 1)
                dve.wait_ge(own, 1)
                dve.tensor_scalar(ms[:, :, :], ms[:, :, :], 1.0 / INNER, 0.0, ALU.mult, ALU.max).then_inc(own, 1)
                dve.wait_ge(own, 2)
                dve.tensor_scalar(ms[:, :, :], ms[:, :, :], 1e-6, None, ALU.add).then_inc(ms_ready, 1)
                dve.wait_ge(rr_ready, 1)
                dve.tensor_scalar(rqs[:, :], rr[:, 0, :], float(HD) ** -0.5, None, ALU.mult).then_inc(own, 1)
                dve.tensor_scalar(nrqs[:, :], rr[:, 0, :], -float(HD) ** -0.5, None, ALU.mult).then_inc(own, 1)
                for b in range(BATCHES):
                    after(dve, b_psum, b - 1)
                    dve.tensor_scalar(diag[:, b % 2, :], ident[:, :], rr[:, 1, b:b + 1], None, ALU.mult)\
                       .then_inc(diag_ready, 1)
                dve.wait_ge(own, 4)


def attend_tokens(nc, tag, x_sb, ident, q_parts, kv_parts, w, cols, gate, rowmul, rqs, nrqs, key_norm):
    normed = cols is not None
    QC = 4 * HD
    with ExitStack() as stack:
        s = Scope(nc, stack, tag)
        xTh, xTl = q_parts
        cTh, cTl = kv_parts
        raw_qk = s.sb("raw_qk", [P, 2, KT, QC])
        raw_vo = s.sb("raw_vo", [P, KT * QC])
        wqkv_h = s.sb("wqkv_h", [P, 3, KT, QC], F32R)
        wqkv_l = s.sb("wqkv_l", [P, 3, KT, QC], F32R)
        wo_h = s.sb("wo_h", [P, 4, DIM], F32R)
        wo_l = s.sb("wo_l", [P, 4, DIM], F32R)
        qk_h = s.sb("qk_h", [P, 2, 2, GT], F32R)
        qk_l = s.sb("qk_l", [P, 2, 2, GT], F32R)
        v_h = s.sb("v_h", [P, 2, GB, QC], F32R)
        v_l = s.sb("v_l", [P, 2, GB, QC], F32R)
        prob = s.sb("prob", [P, 2, GB, TOKENS])
        pT_h = s.sb("pT_h", [P, 2, GB, TOKENS], F32R)
        pT_l = s.sb("pT_l", [P, 2, GB, TOKENS], F32R)
        oT_h = s.sb("oT_h", [P, 2, GB, TOKENS], F32R)
        oT_l = s.sb("oT_l", [P, 2, GB, TOKENS], F32R)
        mx = s.sb("mx", [P, 2, GB])
        nb = s.sb("nb", [P, 2, GB])
        sums = s.sb("sums", [P, 2, GB])
        rsum = s.sb("rsum", [P, 2, GB])
        if normed:
            knorm = s.sb("knorm", [P, 2, QC])
            allb = s.sb("allb", [P, 5, HEADS])
            bqk = s.sb("bqk", [P, 2, 4])
            bv = s.sb("bv", [P, 4])
            g = s.sb("g", [P, 1])
            tg = s.sb("tg", [P, 1])
        qk_ps = [s.ps(f"qk{k}", [P, GT]) for k in range(2)]
        v_ps = s.ps("v", [P, QC])
        s_ps = s.ps("s", [P, GB, TOKENS])
        pT_ps = s.ps("pT", [P, GB, TOKENS])
        oT_ps = s.ps("oT", [P, GB, TOKENS])
        acc = s.ps("acc", [P, GB, DIM])

        ld_qk, ld_v, ld_o, ld_b = s.sem("ld_qk"), s.sem("ld_v"), s.sem("ld_o"), s.sem("ld_b")
        bias_copied, half_scaled, tanh_ready = s.sem("bias_copied"), s.sem("half_scaled"), s.sem("tanh_ready")
        kw_scaled, ow_scaled = s.sem("kw_scaled"), s.sem("ow_scaled")
        wqk_hi, wqk_lo, wv_hi, wv_lo, wo_hi, wo_lo = (
            s.sem(n) for n in ("wqk_hi", "wqk_lo", "wv_hi", "wv_lo", "wo_hi", "wo_lo"))
        qk_psum, qk_hi, qk_lo = (s.sem(n) for n in ("qk_psum", "qk_hi", "qk_lo"))
        v_psum, v_hi, v_lo = (s.sem(n) for n in ("v_psum", "v_hi", "v_lo"))
        s_psum, s_read, mx_ready, nb_ready = (s.sem(n) for n in ("s_psum", "s_read", "mx_ready", "nb_ready"))
        exp_ready, rsum_ready, prob_ready = (s.sem(n) for n in ("exp_ready", "rsum_ready", "prob_ready"))
        pT_psum, pT_hi, pT_lo = (s.sem(n) for n in ("pT_psum", "pT_hi", "pT_lo"))
        oT_psum, oT_hi, oT_lo = (s.sem(n) for n in ("oT_psum", "oT_hi", "oT_lo"))
        acc_psum, x_added = s.sem("acc_psum"), s.sem("x_added")

        def quads(eng, body):
            body(0)
            with eng.Fori(1, QUADS - 1) as i:
                body(i)
            body(QUADS - 1)

        def known(t):
            return not isinstance(t, int) or 0 <= t < UNITS * QUADS

        def v_turns(k, last):
            if k == 14:
                return []
            turns = [divmod(n + 2, GB) for n in ((14, 15) if k == 15 else (k,))]
            return [(g, b) for g, b in turns if not (last and g == GROUPS)]

        def v_count(i, g, b):
            return (i * 4 + g) * 4 + b + 1

        with nc.Block() as block:

            @block.sync
            def _(sp):
                if normed:
                    sp.dma_start(allb[:, :, :], cols).then_inc(ld_b, 16)
                    sp.dma_start(g[:, :], gate.broadcast_to([P, 1])).then_inc(ld_b, 16)

                def load(i):
                    c = ds(i * QC, QC)
                    after(sp, wqk_lo, i * 4)
                    for k in range(2):
                        sp.dma_start(raw_qk[:, k, :, :], w[k][:, :, c]).then_inc(ld_qk, 16)
                        if normed:
                            sp.dma_start(knorm[:, k, :], key_norm[k][:, c].broadcast_to([P, QC])).then_inc(ld_qk, 16)
                    after(sp, wo_lo, i * 4)
                    sp.dma_start(raw_vo[:, :].rearrange("p (k c) -> p k c", k=KT), w[2][:, :, c]).then_inc(ld_v, 16)
                    sp.wait_ge(wv_lo, i + 1)
                    sp.dma_start(raw_vo[:, :].rearrange("p (h c) -> p h c", h=4), w[3][:, ds(i * 4, 4), :])\
                      .then_inc(ld_o, 16)

                load(0)
                with sp.Fori(1, QUADS) as i:
                    load(i)

            def split_qk_turn(k):
                return k - 12 if k >= 12 else None

            def split_o_turn(k):
                return k - 1 if 1 <= k <= 4 else None

            LD_QK = 64 if normed else 32

            @block.scalar
            def _(act):
                if normed:
                    act.wait_ge(ld_b, 32)
                    act.activation(tg[:, :], g[:, :], ACT.Tanh).then_inc(tanh_ready, 1)

                def split_qk(i, h):
                    if normed:
                        act.wait_ge(kw_scaled, i * 4 + h + 1)
                    else:
                        act.wait_ge(ld_qk, LD_QK * (i + 1))
                    after(act, qk_psum, 2 * (i * 16 - 4 + h + 1))
                    c = slice(HD * h, HD * h + HD)
                    act.activation(wqkv_h[:, 0:2, :, c], raw_qk[:, :, :, c], ACT.Copy).then_inc(wqk_hi, 1)

                def split_v(i):
                    act.wait_ge(ld_v, 16 * (i + 1))
                    after(act, v_psum, i * 16)
                    act.activation(wqkv_h[:, 2, :, :], raw_vo[:, :].rearrange("p (k c) -> p k c", k=KT), ACT.Copy)\
                        .then_inc(wv_hi, 1)

                def split_o(i, h):
                    if normed:
                        act.wait_ge(ow_scaled, i * 4 + h + 1)
                    else:
                        act.wait_ge(ld_o, 16 * (i + 1))
                    after(act, acc_psum, i * 16 - 4 + h + 1)
                    act.activation(wo_h[:, h, :], raw_vo[:, DIM * h:DIM * h + DIM], ACT.Copy).then_inc(wo_hi, 1)

                def round_qk(t, h, k):
                    act.wait_ge(qk_psum, 2 * t + k + 1)
                    after(act, s_psum, t - 1)
                    o, i_ = qk_h[:, h % 2, k, :], qk_ps[k][:, :]
                    if normed:
                        ins = act.activation(o, i_, ACT.Identity, bias=bqk[:, k, h:h + 1])
                    else:
                        ins = act.activation(o, i_, ACT.Copy)
                    ins.then_inc(qk_hi, 1)

                def round_v(n, g, b):
                    act.wait_ge(v_psum, n)
                    after(act, oT_psum, (n - b - 1) - 4)
                    act.activation(v_h[:, g % 2, b, :], v_ps[:, :], ACT.Copy).then_inc(v_hi, 1)

                def exponentials(t, k):
                    g_, p = k // 4, k % 2
                    act.wait_ge(nb_ready, t + 1)
                    for b in range(GB):
                        r = GB * g_ + b
                        ins = act.activation(prob[:, p, b, :], prob[:, p, b, :], ACT.Exp, bias=nb[:, p, b:b + 1],
                                             scale=rqs[:, r:r + 1], accum_out=sums[:, p, b:b + 1])
                    ins.then_inc(exp_ready, 1)

                def round_pT(t, k):
                    act.wait_ge(pT_psum, t + 1)
                    after(act, oT_psum, t - 1)
                    act.activation(pT_h[:, k % 2, :, :], pT_ps[:, :, :], ACT.Copy).then_inc(pT_hi, 1)

                def round_oT(t, k):
                    act.wait_ge(oT_psum, t + 1)
                    after(act, acc_psum, t - 1)
                    if normed:
                        ins = act.activation(oT_h[:, k % 2, :, :], oT_ps[:, :, :], ACT.Identity,
                                             bias=bv[:, k % 4:k % 4 + 1])
                    else:
                        ins = act.activation(oT_h[:, k % 2, :, :], oT_ps[:, :, :], ACT.Copy)
                    ins.then_inc(oT_hi, 1)

                def body(i):
                    last = isinstance(i, int) and i == QUADS - 1
                    for k in range(16):
                        t = i * 16 + k
                        if known(t + 1):
                            round_qk(t + 1, (k + 1) % 4, 0)
                        exponentials(t, k)
                        if known(t - 1):
                            round_pT(t - 1, k - 1)
                        if known(t + 1):
                            round_qk(t + 1, (k + 1) % 4, 1)
                        if k == 14 and not last:
                            split_v(i + 1)
                        if known(t - 2):
                            round_oT(t - 2, k - 2)
                        if split_o_turn(k) is not None:
                            split_o(i, split_o_turn(k))
                        for g_, b in v_turns(k, last):
                            round_v(v_count(i, g_, b), g_, b)
                        if split_qk_turn(k) is not None and not last:
                            split_qk(i + 1, split_qk_turn(k))

                split_v(0)
                for h in range(4):
                    split_qk(0, h)
                round_qk(0, 0, 0)
                round_qk(0, 0, 1)
                for b in range(2):
                    round_v(v_count(0, 0, b), 0, b)
                quads(act, body)
                n = 16 * QUADS
                round_pT(n - 1, 15)
                round_oT(n - 2, 14)
                round_oT(n - 1, 15)

            @block.gpsimd
            def _(pool):
                def body(i):
                    for k in range(16):
                        t = i * 16 + k
                        pool.wait_ge(rsum_ready, t + 1)
                        pool.tensor_tensor(prob[:, k % 2, :, :], prob[:, k % 2, :, :],
                                           rsum[:, k % 2, :].unsqueeze(2).broadcast_to([P, GB, TOKENS]), ALU.mult)\
                            .then_inc(prob_ready, 1)

                with pool.Fori(0, QUADS) as i:
                    body(i)

            @block.tensor
            def _(pe):
                def product(out, ah, al, bh, bl, start, stop):
                    pe.matmul(out, ah, bh, start=start, stop=False)
                    pe.matmul(out, ah, bl, start=False, stop=False)
                    return pe.matmul(out, al, bh, start=False, stop=stop)

                def project_qk(t, g_, h, k):
                    th, tl = ((xTh, xTl), (cTh, cTl))[k]
                    after(pe, qk_lo, 2 * (t - 1) + k + 1)
                    c, tok = slice(HD * h, HD * h + HD), slice(GT * g_, GT * g_ + GT)
                    for kt in range(KT):
                        mm = product(qk_ps[k][:, :], wqkv_h[:, k, kt, c], wqkv_l[:, k, kt, c],
                                     th[:, kt, tok], tl[:, kt, tok], kt == 0, kt == KT - 1)
                    mm.then_inc(qk_psum, 1)

                def project_v(n, g_, b):
                    after(pe, v_lo, n - 1)
                    tok = slice(P * (GB * g_ + b), P * (GB * g_ + b) + P)
                    for kt in range(KT):
                        mm = product(v_ps[:, :], cTh[:, kt, tok], cTl[:, kt, tok], wqkv_h[:, 2, kt, :],
                                     wqkv_l[:, 2, kt, :], kt == 0, kt == KT - 1)
                    mm.then_inc(v_psum, 1)

                def scores(t, k):
                    pe.wait_ge(qk_lo, 2 * t + 2)
                    after(pe, s_read, t)
                    p = k % 2
                    for b in range(GB):
                        tok = slice(P * b, P * b + P)
                        mm = product(s_ps[:, b, :], qk_h[:, p, 0, tok], qk_l[:, p, 0, tok],
                                     qk_h[:, p, 1, tok], qk_l[:, p, 1, tok], True, True)
                    mm.then_inc(s_psum, 1)

                def turn_probs(t, k):
                    pe.wait_ge(prob_ready, t + 1)
                    after(pe, pT_lo, t)
                    for b in range(GB):
                        mm = pe.transpose(pT_ps[:, b, :], prob[:, k % 2, b, :], ident[:, :])
                    mm.then_inc(pT_psum, 1)

                def weigh(t, k):
                    g_, h, p = (k // 4) % 4, k % 4, k % 2
                    pe.wait_ge(pT_lo, t + 1)
                    if h == 0:
                        pe.wait_ge(v_lo, t + 4)
                    after(pe, oT_lo, t)
                    c = slice(HD * h, HD * h + HD)
                    for b in range(GB):
                        mm = product(oT_ps[:, b, :], v_h[:, g_ % 2, b, c], v_l[:, g_ % 2, b, c],
                                     pT_h[:, p, b, :], pT_l[:, p, b, :], True, True)
                    mm.then_inc(oT_psum, 1)

                def body(i):
                    last = isinstance(i, int) and i == QUADS - 1
                    for k in range(16):
                        t = i * 16 + k
                        g1, h1 = ((k + 1) // 4) % 4, (k + 1) % 4
                        scores(t, k)
                        if known(t + 1):
                            if k == 15:
                                pe.wait_ge(wqk_lo, i * 4 + 5)
                            elif g1 == 0:
                                pe.wait_ge(wqk_lo, i * 4 + h1 + 1)
                            project_qk(t + 1, g1, h1, 0)
                        if known(t - 1):
                            turn_probs(t - 1, k - 1)
                        if known(t + 1):
                            project_qk(t + 1, g1, h1, 1)
                        if known(t - 2):
                            weigh(t - 2, k - 2)
                        for g_, b in v_turns(k, last):
                            if g_ == GROUPS and b == 0:
                                pe.wait_ge(wv_lo, i + 2)
                            project_v(v_count(i, g_, b), g_ % GROUPS, b)
                        if known(t - 3):
                            out_turn(i, k)

                def out_turn(i, k):
                    t, h, p = i * 16 + (k - 3), (k - 3) % 4, (k - 3) % 2
                    pe.wait_ge(oT_lo, t + 1)
                    if h == 0:
                        after(pe, x_added, i * 4 + (k - 3) // 4)
                    if 3 <= k < 7:
                        pe.wait_ge(wo_lo, i * 4 + h + 1)
                    for b in range(GB):
                        ah, al, bh, bl = oT_h[:, p, b, :], oT_l[:, p, b, :], wo_h[:, h, :], wo_l[:, h, :]
                        pe.matmul(acc[:, b, :], ah, bh, start=(h == 0 and b % 2 == 0), stop=False, skip_group_check=True)
                        pe.matmul(acc[:, b, :], ah, bl, start=False, stop=False, skip_group_check=True)
                        mm = pe.matmul(acc[:, b, :], al, bh, start=False, stop=(h == 3), skip_group_check=True)
                    mm.then_inc(acc_psum, 1)

                pe.wait_ge(wv_lo, 1)
                pe.wait_ge(wqk_lo, 1)
                project_qk(0, 0, 0, 0)
                project_qk(0, 0, 0, 1)
                for b in range(2):
                    project_v(v_count(0, 0, b), 0, b)
                quads(pe, body)
                n = 16 * QUADS
                turn_probs(n - 1, 15)
                weigh(n - 2, 14)
                out_turn(QUADS, 0)
                weigh(n - 1, 15)
                out_turn(QUADS, 1)
                out_turn(QUADS, 2)

            @block.vector
            def _(dve):
                def copy_bias(i, h):
                    n = i * 4 + h
                    after(dve, qk_lo, 2 * (i * 16 - 4 + h + 1))
                    dve.tensor_scalar(bqk[:, 0, h:h + 1], allb[:, 0, ds(n, 1)], 1.0, None, ALU.mult)
                    dve.tensor_scalar(bqk[:, 1, h:h + 1], allb[:, 1, ds(n, 1)], allb[:, 3, ds(n, 1)],
                                      allb[:, 4, ds(n, 1)], ALU.mult, ALU.mult).then_inc(bias_copied, 1)

                def scale_k(i, h):
                    if h == 0:
                        dve.wait_ge(ld_qk, LD_QK * (i + 1))
                    c = slice(HD * h, HD * h + HD)
                    for n in range(2):
                        for kt in range(KT):
                            ins = dve.tensor_tensor(raw_qk[:, 1, kt, c], raw_qk[:, 1, kt, c], knorm[:, n, c], ALU.mult)
                            if n == 0:
                                ins.then_inc(half_scaled, 1)
                        if n == 0:
                            dve.wait_ge(half_scaled, i * 8 + 2 * h + 2)
                    ins.then_inc(kw_scaled, 1)

                def split_qk(i, h):
                    dve.wait_ge(wqk_hi, i * 4 + h + 1)
                    c = slice(HD * h, HD * h + HD)
                    for kt in range(KT):
                        ins = dve.tensor_tensor(wqkv_l[:, 0:2, kt, c], raw_qk[:, :, kt, c],
                                                wqkv_h[:, 0:2, kt, c].bitcast(F32), ALU.subtract)
                    ins.then_inc(wqk_lo, 1)

                def prepare_qk(i, h):
                    if normed:
                        copy_bias(i, h)
                    split_qk(i, h)

                def split_v(i):
                    dve.wait_ge(wv_hi, i + 1)
                    dve.tensor_tensor(wqkv_l[:, 2, :, :], raw_vo[:, :].rearrange("p (k c) -> p k c", k=KT),
                                      wqkv_h[:, 2, :, :].bitcast(F32), ALU.subtract).then_inc(wv_lo, 1)

                def split_o(i, h):
                    c = slice(DIM * h, DIM * h + DIM)
                    if normed:
                        dve.wait_ge(ld_o, 16 * (i + 1))
                        after(dve, oT_lo, i * 16 - 4 + h + 1)
                        dve.tensor_scalar(bv[:, h:h + 1], allb[:, 2, ds(i * 4 + h, 1)], 1.0, None, ALU.mult)
                        dve.tensor_scalar(raw_vo[:, c], raw_vo[:, c], tg[:, 0:1], None, ALU.mult).then_inc(ow_scaled, 1)
                    dve.wait_ge(wo_hi, i * 4 + h + 1)
                    dve.tensor_tensor(wo_l[:, h, :], raw_vo[:, c], wo_h[:, h, :].bitcast(F32), ALU.subtract)\
                       .then_inc(wo_lo, 1)

                def rest(out, psum, hi, bias, sem):
                    if normed and bias is not None:
                        dve.scalar_tensor_tensor(out, psum, bias, hi.bitcast(F32), ALU.add, ALU.subtract).then_inc(sem, 1)
                    else:
                        dve.tensor_tensor(out, psum, hi.bitcast(F32), ALU.subtract).then_inc(sem, 1)

                def rest_qk(t, h, k):
                    dve.wait_ge(qk_hi, 2 * t + k + 1)
                    rest(qk_l[:, h % 2, k, :], qk_ps[k][:, :], qk_h[:, h % 2, k, :],
                         bqk[:, k, h:h + 1] if normed else None, qk_lo)

                def rest_v(n, g_, b):
                    dve.wait_ge(v_hi, n)
                    rest(v_l[:, g_ % 2, b, :], v_ps[:, :], v_h[:, g_ % 2, b, :], None, v_lo)

                def shift(t, k):
                    g_, p = k // 4, k % 2
                    dve.wait_ge(s_psum, t + 1)
                    after(dve, pT_psum, t - 1)
                    m = rowmul[:, GB * g_:GB * g_ + GB, :] if normed else rowmul[:, :, :]
                    dve.tensor_tensor(prob[:, p, :, :], s_ps[:, :, :], m, ALU.mult if normed else ALU.add)\
                       .then_inc(s_read, 1)
                    dve.wait_ge(s_read, t + 1)
                    dve.tensor_reduce(mx[:, p, :], prob[:, p, :, :], AX.X, ALU.max).then_inc(mx_ready, 1)
                    dve.wait_ge(mx_ready, t + 1)
                    dve.tensor_tensor(nb[:, p, :], mx[:, p, :], nrqs[:, GB * g_:GB * g_ + GB], ALU.mult)\
                       .then_inc(nb_ready, 1)

                def invert_sums(t, k):
                    dve.wait_ge(exp_ready, t + 1)
                    dve.reciprocal(rsum[:, k % 2, :], sums[:, k % 2, :]).then_inc(rsum_ready, 1)

                def rest_pT(t, k):
                    dve.wait_ge(pT_hi, t + 1)
                    rest(pT_l[:, k % 2, :, :], pT_ps[:, :, :], pT_h[:, k % 2, :, :], None, pT_lo)

                def rest_oT(t, k):
                    dve.wait_ge(oT_hi, t + 1)
                    rest(oT_l[:, k % 2, :, :], oT_ps[:, :, :], oT_h[:, k % 2, :, :],
                         bv[:, k % 4:k % 4 + 1] if normed else None, oT_lo)

                def add_group(i, k):
                    g_ = ((k - 3) // 4) % 4
                    dve.wait_ge(acc_psum, i * 16 + (k - 3) + 1)
                    b = slice(GB * g_, GB * g_ + GB)
                    dve.tensor_tensor(x_sb[:, b, :], x_sb[:, b, :], acc[:, :, :], ALU.add).then_inc(x_added, 1)

                def body(i):
                    last = isinstance(i, int) and i == QUADS - 1
                    for k in range(16):
                        t = i * 16 + k
                        shift(t, k)
                        if known(t + 1):
                            rest_qk(t + 1, (k + 1) % 4, 0)
                        invert_sums(t, k)
                        if known(t - 1):
                            rest_pT(t - 1, k - 1)
                        if known(t + 1):
                            rest_qk(t + 1, (k + 1) % 4, 1)
                        if k == 14 and not last:
                            split_v(i + 1)
                        if known(t - 2):
                            rest_oT(t - 2, k - 2)
                        if split_o_turn(k) is not None:
                            split_o(i, split_o_turn(k))
                        for g_, b in v_turns(k, last):
                            rest_v(v_count(i, g_, b), g_, b)
                        if k % 4 == 2 and known(t - 3):
                            add_group(i, k)
                        if normed and 8 <= k < 12 and not last:
                            scale_k(i + 1, k - 8)
                        if split_qk_turn(k) is not None and not last:
                            prepare_qk(i + 1, split_qk_turn(k))

                if normed:
                    dve.wait_ge(ld_b, 32)
                    dve.wait_ge(tanh_ready, 1)
                split_v(0)
                for h in range(4):
                    if normed:
                        scale_k(0, h)
                    prepare_qk(0, h)
                rest_qk(0, 0, 0)
                rest_qk(0, 0, 1)
                for b in range(2):
                    rest_v(v_count(0, 0, b), 0, b)
                quads(dve, body)
                n = 16 * QUADS
                rest_pT(n - 1, 15)
                rest_oT(n - 2, 14)
                rest_oT(n - 1, 15)
                add_group(QUADS, 2)
                dve.wait_ge(x_added, GROUPS * QUADS)


def text_free_attention(nc, res, ctx_in, ctxT, wqT, wkT, w, cols, key_norm, out_b, gate):
    x_sb, ident = res["x"], res["ident"]
    with ExitStack() as stack:
        s = Scope(nc, stack, "c")
        xTh = s.sb("xTh", [P, KT, BATCHES * TOKENS], F32R)
        xTl = s.sb("xTl", [P, KT, BATCHES * TOKENS], F32R)
        cTh = s.sb("cTh", [P, KT, BATCHES * TOKENS], F32R)
        cTl = s.sb("cTl", [P, KT, BATCHES * TOKENS], F32R)
        rkb = s.sb("rkb", [P, BATCHES, TOKENS])
        rqs = s.sb("rqs", [P, BATCHES])
        nrqs = s.sb("nrqs", [P, BATCHES])
        with nc.sbuf_tensor("c_xn", [P, BATCHES, DIM], F32) as xn:
            prepare_tokens(nc, x_sb, ident, xn, xTh, xTl, 1e-5)
            row_norms(nc, ident, xn, xTh, xTl, cTh, cTl, rqs, nrqs, rkb, ctx_in, ctxT, wqT, wkT)
            add_bias(nc, x_sb, out_b, gate)
        attend_tokens(nc, "ca", x_sb, ident, (xTh, xTl), (cTh, cTl), w, cols, gate, rkb, rqs, nrqs, key_norm)


def add_bias(nc, x_sb, out_b, gate):
    with ExitStack() as stack:
        s = Scope(nc, stack, "cb")
        ob = s.sb("ob", [P, DIM])
        g = s.sb("g", [P, 1])
        tg = s.sb("tg", [P, 1])
        ld, tanh_ready, ob_ready, x_done = s.sem("ld"), s.sem("tanh_ready"), s.sem("ob_ready"), s.sem("x_done")
        with nc.Block() as block:

            @block.sync
            def _(sp):
                sp.dma_start(ob[:, :], out_b.broadcast_to([P, DIM])).then_inc(ld, 16)
                sp.dma_start(g[:, :], gate.broadcast_to([P, 1])).then_inc(ld, 16)

            @block.scalar
            def _(act):
                act.wait_ge(ld, 32)
                act.activation(tg[:, :], g[:, :], ACT.Tanh).then_inc(tanh_ready, 1)

            @block.vector
            def _(dve):
                dve.wait_ge(tanh_ready, 1)
                dve.tensor_scalar(ob[:, :], ob[:, :], tg[:, 0:1], None, ALU.mult).then_inc(ob_ready, 1)
                dve.wait_ge(ob_ready, 1)
                for b in range(BATCHES):
                    dve.tensor_tensor(x_sb[:, b, :], x_sb[:, b, :], ob[:, :], ALU.add).then_inc(x_done, 1)
                dve.wait_ge(x_done, BATCHES)

EXPERTS, EXPERT_HID, SHARED_HID, TOPK = 16, 176, 352, 4
M_TILES = -(-(EXPERTS * EXPERT_HID + SHARED_HID) // P)
CHUNKS = 5
CT = M_TILES // CHUNKS
KINDS = EXPERTS + 1
M_UNITS = GROUPS * CT
QHD = 192


def route(nc, ident, xTh, xTl, gate_w, wTh, wTl):
    PAD = EXPERTS + 4
    with ExitStack() as stack:
        s = Scope(nc, stack, "e")
        raw = s.sb("raw", [P, KT, EXPERTS])
        gh = s.sb("gh", [P, KT, EXPERTS], F32R)
        gl = s.sb("gl", [P, KT, EXPERTS], F32R)
        mx = s.sb("mx", [P, BATCHES])
        sh = s.sb("sh", [P, BATCHES, EXPERTS])
        e = s.sb("e", [P, BATCHES, PAD])
        top = s.sb("top", [P, BATCHES, 8])
        rep = s.sb("rep", [P, BATCHES, PAD])
        den = s.sb("den", [P, BATCHES])
        rden = s.sb("rden", [P, BATCHES])
        sel = s.sb("sel", [P, BATCHES, EXPERTS])
        weight = s.sb("weight", [P, BATCHES, KINDS])
        l_ps = s.ps("l", [P, BATCHES, EXPERTS])
        t_ps = [s.ps(f"t{k}", [KINDS, GT]) for k in range(GROUPS)]
        ld, g_hi, g_lo, l_psum = s.sem("ld"), s.sem("g_hi"), s.sem("g_lo"), s.sem("l_psum")
        consts, own, shifted, exp_ready = s.sem("consts"), s.sem("own"), s.sem("shifted"), s.sem("exp_ready")
        weight_ready, t_psum, t_hi, t_lo = s.sem("weight_ready"), s.sem("t_psum"), s.sem("t_hi"), s.sem("t_lo")
        with nc.Block() as block:

            @block.sync
            def _(sp):
                sp.dma_start(raw[:, :, :], gate_w).then_inc(ld, 16)

            @block.gpsimd
            def _(pool):
                pool.memset(e[:, :, EXPERTS:PAD], -1.0).then_inc(consts, 1)
                pool.memset(weight[:, :, EXPERTS:KINDS], 1.0).then_inc(consts, 1)

            @block.scalar
            def _(act):
                act.wait_ge(ld, 16)
                act.activation(gh[:, :, :], raw[:, :, :], ACT.Copy).then_inc(g_hi, 1)
                act.wait_ge(shifted, 1)
                act.activation(e[:, :, 0:EXPERTS], sh[:, :, :], ACT.Exp).then_inc(exp_ready, 1)
                for g in range(GROUPS):
                    act.wait_ge(t_psum, g + 1)
                    act.activation(wTh[:, GT * g:GT * g + GT], t_ps[g][:, :], ACT.Copy).then_inc(t_hi, 1)

            @block.tensor
            def _(pe):
                pe.wait_ge(g_lo, 1)
                for b in range(BATCHES):
                    tok = slice(P * b, P * b + P)
                    for k in range(KT):
                        pe.matmul(l_ps[:, b, :], xTh[:, k, tok], gh[:, k, :], start=(k == 0), stop=False)
                        pe.matmul(l_ps[:, b, :], xTh[:, k, tok], gl[:, k, :], start=False, stop=False)
                        mm = pe.matmul(l_ps[:, b, :], xTl[:, k, tok], gh[:, k, :], start=False, stop=(k == KT - 1))
                mm.then_inc(l_psum, 1)
                pe.wait_ge(weight_ready, 1)
                for g in range(GROUPS):
                    for b in range(GB):
                        mm = pe.transpose(t_ps[g][:, P * b:P * b + P], weight[:, GB * g + b, :], ident[:, :])
                    mm.then_inc(t_psum, 1)

            @block.vector
            def _(dve):
                count = [0]

                def chained(ins):
                    count[0] += 1
                    ins.then_inc(own, 1)
                    dve.wait_ge(own, count[0])

                dve.wait_ge(g_hi, 1)
                dve.tensor_tensor(gl[:, :, :], raw[:, :, :], gh[:, :, :].bitcast(F32), ALU.subtract).then_inc(g_lo, 1)
                dve.wait_ge(l_psum, 1)
                chained(dve.tensor_reduce(mx[:, :], l_ps[:, :, :], AX.X, ALU.max))
                dve.tensor_tensor(sh[:, :, :], l_ps[:, :, :], mx[:, :].unsqueeze(2).broadcast_to([P, BATCHES, EXPERTS]),
                                  ALU.subtract).then_inc(shifted, 1)
                dve.wait_ge(exp_ready, 1)
                dve.wait_ge(consts, 2)
                for b in range(BATCHES):
                    ins = dve.max(top[:, b, :], e[:, b, 0:EXPERTS])
                chained(ins)
                chained(dve.tensor_reduce(den[:, :], top[:, :, 0:TOPK], AX.X, ALU.add))
                chained(dve.memset(top[:, :, TOPK:8], -1.0))
                for b in range(BATCHES):
                    ins = dve.match_replace(rep[:, b, :], top[:, b, :], e[:, b, :], -2.0)
                chained(ins)
                chained(dve.reciprocal(rden[:, :], den[:, :]))
                chained(dve.scalar_tensor_tensor(sel[:, :, :], rep[:, :, 0:EXPERTS], -1.5, e[:, :, 0:EXPERTS],
                                                 ALU.is_lt, ALU.mult))
                dve.tensor_tensor(weight[:, :, 0:EXPERTS], sel[:, :, :],
                                  rden[:, :].unsqueeze(2).broadcast_to([P, BATCHES, EXPERTS]), ALU.mult)\
                   .then_inc(weight_ready, 1)
                for g in range(GROUPS):
                    dve.wait_ge(t_hi, g + 1)
                    cols = slice(GT * g, GT * g + GT)
                    dve.tensor_tensor(wTl[:, cols], t_ps[g][:, :], wTh[:, cols].bitcast(F32), ALU.subtract)\
                       .then_inc(t_lo, 1)
                dve.wait_ge(t_lo, GROUPS)


def experts(nc, x_sb, xTh, xTl, wTh, wTl, gu_w, down_w, spread):
    with ExitStack() as stack:
        s = Scope(nc, stack, "m")
        CC = CT * P
        raw_gu = s.sb("raw_gu", [P, 2, KT, CC])
        raw_d = s.sb("raw_d", [P, CT, DIM])
        raw_s = s.sb("raw_s", [KINDS, CC])
        gu_h = s.sb("gu_h", [P, 2, KT, CC], F32R)
        gu_l = s.sb("gu_l", [P, 2, KT, CC], F32R)
        d_h = s.sb("d_h", [P, CT, DIM], F32R)
        d_l = s.sb("d_l", [P, CT, DIM], F32R)
        sp_h = s.sb("sp_h", [KINDS, CC], F32R)
        silu = s.sb("silu", [P, 2, GT])
        prod = s.sb("prod", [P, 2, GT])
        hid = s.sb("hid", [P, 2, GT])
        hid_h = s.sb("hid_h", [P, 2, GT], F32R)
        hid_l = s.sb("hid_l", [P, 2, GT], F32R)
        g_ps = [s.ps(f"g{k}", [P, GT]) for k in range(2)]
        u_ps = [s.ps(f"u{k}", [P, GT]) for k in range(2)]
        w_ps = [s.ps(f"w{k}", [P, GT]) for k in range(2)]
        acc = s.ps("acc", [P, GB, DIM])
        ld_gu, ld_d = s.sem("ld_gu"), s.sem("ld_d")
        gu_hi, gu_lo, d_hi, d_lo = s.sem("gu_hi"), s.sem("gu_lo"), s.sem("d_hi"), s.sem("d_lo")
        g_psum, u_psum, w_psum = s.sem("g_psum"), s.sem("u_psum"), s.sem("w_psum")
        silu_ready, prod_ready, hid_ready = s.sem("silu_ready"), s.sem("prod_ready"), s.sem("hid_ready")
        hid_hi, hid_lo, acc_psum, x_added = s.sem("hid_hi"), s.sem("hid_lo"), s.sem("acc_psum"), s.sem("x_added")

        def chunks(eng, body):
            body(0)
            with eng.Fori(1, CHUNKS - 1) as i:
                body(i)
            body(CHUNKS - 1)

        def gu_turn(i, k):
            if k == 0 and not (isinstance(i, int) and i == 0):
                return i, 4
            if k >= 16 and not (isinstance(i, int) and i == CHUNKS - 1):
                return i + 1, k - 16
            return None

        def d_turn(i, k):
            if k < 3 and not (isinstance(i, int) and i == 0):
                return i, k + 2
            if k >= 18 and not (isinstance(i, int) and i == CHUNKS - 1):
                return i + 1, k - 18
            return None

        def known(t):
            return not isinstance(t, int) or t >= 0

        with nc.Block() as block:

            @block.sync
            def _(sp):
                def load(i):
                    c = ds(i * CC, CC)
                    after(sp, gu_lo, i * CT)
                    for n in range(2):
                        sp.dma_start(raw_gu[:, n, :, :], gu_w[:, n, :, c]).then_inc(ld_gu, 16)
                    sp.dma_start(raw_s[:, :], spread[:, c]).then_inc(ld_gu, 16)
                    after(sp, d_lo, i * CT)
                    sp.dma_start(raw_d[:, :, :], down_w[:, ds(i * CT, CT), :]).then_inc(ld_d, 16)

                load(0)
                with sp.Fori(1, CHUNKS) as i:
                    load(i)

            @block.scalar
            def _(act):
                def split_gu(i, j):
                    act.wait_ge(ld_gu, 48 * (i + 1))
                    after(act, w_psum, i * M_UNITS - CT + j + 1)
                    c = slice(P * j, P * j + P)
                    act.activation(sp_h[:, c], raw_s[:, c], ACT.Copy).then_inc(gu_hi, 1)
                    for n in range(2):
                        ins = act.activation(gu_h[:, n, :, c], raw_gu[:, n, :, c], ACT.Copy)
                    ins.then_inc(gu_hi, 1)

                def split_d(i, j):
                    act.wait_ge(ld_d, 16 * (i + 1))
                    after(act, acc_psum, i * M_UNITS - CT + j + 1)
                    act.activation(d_h[:, j, :], raw_d[:, j, :], ACT.Copy).then_inc(d_hi, 1)

                def gates(t, k):
                    act.wait_ge(g_psum, t + 1)
                    after(act, prod_ready, t - 1)
                    act.activation(silu[:, k % 2, :], g_ps[k % 2][:, :], ACT.Silu).then_inc(silu_ready, 1)

                def round_hid(t, k):
                    act.wait_ge(hid_ready, t + 1)
                    after(act, acc_psum, t - 1)
                    act.activation(hid_h[:, k % 2, :], hid[:, k % 2, :], ACT.Copy).then_inc(hid_hi, 1)

                def body(i):
                    for k in range(M_UNITS):
                        t = i * M_UNITS + k
                        gates(t, k)
                        if gu_turn(i, k):
                            split_gu(*gu_turn(i, k))
                        if d_turn(i, k):
                            split_d(*d_turn(i, k))
                        if known(t - 1):
                            round_hid(t - 1, k - 1)

                for j in range(CT):
                    split_gu(0, j)
                for j in range(CT):
                    split_d(0, j)
                chunks(act, body)
                round_hid(CHUNKS * M_UNITS - 1, M_UNITS - 1)

            @block.tensor
            def _(pe):
                def gates_and_values(i, k):
                    t, (g_, j), p = i * M_UNITS + k, divmod(k, CT), k % 2
                    if g_ == 0:
                        pe.wait_ge(gu_lo, i * CT + j + 1)
                    c, tok = slice(P * j, P * j + P), slice(GT * g_, GT * g_ + GT)
                    for n, ps, free, done in ((0, g_ps, silu_ready, g_psum), (1, u_ps, prod_ready, u_psum)):
                        after(pe, free, t - 1)
                        for kt in range(KT):
                            h, l = gu_h[:, n, kt, c], gu_l[:, n, kt, c]
                            pe.matmul(ps[p][:, :], h, xTh[:, kt, tok], start=(kt == 0), stop=False)
                            pe.matmul(ps[p][:, :], h, xTl[:, kt, tok], start=False, stop=False)
                            mm = pe.matmul(ps[p][:, :], l, xTh[:, kt, tok], start=False, stop=(kt == KT - 1))
                        mm.then_inc(done, 1)
                    after(pe, hid_ready, t - 1)
                    pe.matmul(w_ps[p][:, :], sp_h[:, c], wTh[:, tok], start=True, stop=False)
                    pe.matmul(w_ps[p][:, :], sp_h[:, c], wTl[:, tok], start=False, stop=True).then_inc(w_psum, 1)

                def down(i, k):
                    t, (g_, j), p = i * M_UNITS + k, divmod(k % M_UNITS, CT), k % 2
                    pe.wait_ge(hid_lo, t + 1)
                    if g_ == 0:
                        pe.wait_ge(d_lo, i * CT + j + 1)
                    if j == 0:
                        after(pe, x_added, i * GROUPS + g_)
                    for b in range(GB):
                        ah, al = (a[:, p, P * b:P * b + P] for a in (hid_h, hid_l))
                        pe.matmul(acc[:, b, :], ah, d_h[:, j, :], start=(j == 0 and b % 2 == 0), stop=False,
                                  skip_group_check=True)
                        pe.matmul(acc[:, b, :], ah, d_l[:, j, :], start=False, stop=False, skip_group_check=True)
                        mm = pe.matmul(acc[:, b, :], al, d_h[:, j, :], start=False, stop=(j == CT - 1),
                                       skip_group_check=True)
                    mm.then_inc(acc_psum, 1)

                def body(i):
                    for k in range(M_UNITS):
                        gates_and_values(i, k)
                        if known(i * M_UNITS + k - 2):
                            down(i, k - 2)

                chunks(pe, body)
                down(CHUNKS, -2)
                down(CHUNKS, -1)

            @block.vector
            def _(dve):
                def split_gu(i, j):
                    dve.wait_ge(gu_hi, 2 * (i * CT + j + 1))
                    c = slice(P * j, P * j + P)
                    for n in range(2):
                        ins = dve.tensor_tensor(gu_l[:, n, :, c], raw_gu[:, n, :, c], gu_h[:, n, :, c].bitcast(F32),
                                                ALU.subtract)
                    ins.then_inc(gu_lo, 1)

                def split_d(i, j):
                    dve.wait_ge(d_hi, i * CT + j + 1)
                    dve.tensor_tensor(d_l[:, j, :], raw_d[:, j, :], d_h[:, j, :].bitcast(F32), ALU.subtract)\
                       .then_inc(d_lo, 1)

                def hidden(t, k):
                    p = k % 2
                    dve.wait_ge(silu_ready, t + 1)
                    dve.wait_ge(u_psum, t + 1)
                    dve.tensor_tensor(prod[:, p, :], silu[:, p, :], u_ps[p][:, :], ALU.mult).then_inc(prod_ready, 1)
                    dve.wait_ge(prod_ready, t + 1)
                    dve.wait_ge(w_psum, t + 1)
                    dve.tensor_tensor(hid[:, p, :], prod[:, p, :], w_ps[p][:, :], ALU.mult).then_inc(hid_ready, 1)

                def rest_hid(t, k):
                    p = k % 2
                    dve.wait_ge(hid_hi, t + 1)
                    dve.tensor_tensor(hid_l[:, p, :], hid[:, p, :], hid_h[:, p, :].bitcast(F32), ALU.subtract)\
                       .then_inc(hid_lo, 1)

                def add_group(i, k):
                    g_ = (k % M_UNITS) // CT
                    dve.wait_ge(acc_psum, i * M_UNITS + k + 1)
                    b = slice(GB * g_, GB * g_ + GB)
                    dve.tensor_tensor(x_sb[:, b, :], x_sb[:, b, :], acc[:, :, :], ALU.add).then_inc(x_added, 1)

                def body(i):
                    for k in range(M_UNITS):
                        t = i * M_UNITS + k
                        if known(t - 1):
                            rest_hid(t - 1, k - 1)
                        if gu_turn(i, k):
                            split_gu(*gu_turn(i, k))
                        if d_turn(i, k):
                            split_d(*d_turn(i, k))
                        hidden(t, k)
                        if k % CT == 1 and known(t - 2):
                            add_group(i, k - 2)

                for j in range(CT):
                    split_gu(0, j)
                for j in range(CT):
                    split_d(0, j)
                chunks(dve, body)
                rest_hid(CHUNKS * M_UNITS - 1, M_UNITS - 1)
                add_group(CHUNKS, -1)
                dve.wait_ge(x_added, CHUNKS * GROUPS)


def expert_layer(nc, res, w, ln1, gate_w, ln2, gu_w, down_w, spread, gate, out):
    x_sb, ident = res["x"], res["ident"]
    before = nc.dram_tensor("x_before", (BATCHES, TOKENS, DIM), F32, kind="Internal").ap()
    with ExitStack() as stack:
        s = Scope(nc, stack, "d")
        xTh = s.sb("xTh", [P, KT, BATCHES * TOKENS], F32R)
        xTl = s.sb("xTl", [P, KT, BATCHES * TOKENS], F32R)
        scale = float(QHD) ** -0.5
        with ExitStack() as inner:
            s1 = Scope(nc, inner, "d1")
            causal = s1.sb("causal", [P, GB, TOKENS])
            rqs = s1.sb("rqs", [P, BATCHES])
            nrqs = s1.sb("nrqs", [P, BATCHES])
            saved, blank = s1.sem("saved"), s1.sem("blank")
            with nc.Block() as block:

                @block.sync
                def _(sp):
                    sp.dma_start(before.rearrange("b p n -> p b n"), x_sb[:, :, :]).then_inc(saved, 16)
                    sp.wait_ge(saved, 16)

                @block.gpsimd
                def _(pool):
                    pool.memset(causal[:, :, :], 0.0).then_inc(blank, 1)
                    pool.memset(rqs[:, :], scale).then_inc(blank, 1)
                    pool.memset(nrqs[:, :], -scale).then_inc(blank, 1)
                    pool.wait_ge(blank, 3)
                    pool.affine_select(out=causal[:, :, :], in_=causal[:, :, :], compare_op=ALU.is_ge,
                                       fill=-1.0e9 / scale, base=0, pattern=[[0, GB], [-1, TOKENS]],
                                       channel_multiplier=1).then_inc(blank, 1)

            with nc.sbuf_tensor("d_xn1", [P, BATCHES, DIM], F32) as xn:
                prepare_tokens(nc, x_sb, ident, xn, xTh, xTl, 1e-6, ln1, centre=True)
            attend_tokens(nc, "da", x_sb, ident, (xTh, xTl), (xTh, xTl), w, None, None, causal, rqs, nrqs, None)
        wTh = s.sb("wTh", [KINDS, BATCHES * TOKENS], F32R)
        wTl = s.sb("wTl", [KINDS, BATCHES * TOKENS], F32R)
        yTh = s.sb("yTh", [P, KT, BATCHES * TOKENS], F32R)
        yTl = s.sb("yTl", [P, KT, BATCHES * TOKENS], F32R)
        with nc.sbuf_tensor("d_xn2", [P, BATCHES, DIM], F32) as xn:
            prepare_tokens(nc, x_sb, ident, xn, yTh, yTl, 1e-6, ln2)
        route(nc, ident, yTh, yTl, gate_w, wTh, wTl)
        experts(nc, x_sb, yTh, yTl, wTh, wTl, gu_w, down_w, spread)
        finish(nc, x_sb, before, gate, out)


def finish(nc, x_sb, before, gate, out):
    with ExitStack() as stack:
        s = Scope(nc, stack, "f")
        x0 = s.sb("x0", [P, BATCHES, DIM])
        g = s.sb("g", [P, 1])
        tg = s.sb("tg", [P, 1])
        ld_g, tanh_ready, x_ready, sent = s.sem("ld_g"), s.sem("tanh_ready"), s.sem("x_ready"), s.sem("sent")
        ld_x = [s.sem(f"ld_x{g}") for g in range(GROUPS)]
        with nc.Block() as block:

            @block.sync
            def _(sp):
                sp.dma_start(g[:, :], gate.broadcast_to([P, 1])).then_inc(ld_g, 16)
                for n in range(GROUPS):
                    b = slice(GB * n, GB * n + GB)
                    sp.dma_start(x0[:, b, :], before[b].rearrange("b p n -> p b n")).then_inc(ld_x[n], 16)
                for n in range(GROUPS):
                    b = slice(GB * n, GB * n + GB)
                    sp.wait_ge(x_ready, n + 1)
                    sp.dma_start(out[b].rearrange("b p n -> p b n"), x_sb[:, b, :]).then_inc(sent, 16)
                sp.wait_ge(sent, 16 * GROUPS)

            @block.scalar
            def _(act):
                act.wait_ge(ld_g, 16)
                act.activation(tg[:, :], g[:, :], ACT.Tanh).then_inc(tanh_ready, 1)

            @block.vector
            def _(dve):
                dve.wait_ge(tanh_ready, 1)
                for n in range(GROUPS):
                    b = slice(GB * n, GB * n + GB)
                    dve.wait_ge(ld_x[n], 16)
                    dve.scalar_tensor_tensor(x_sb[:, b, :], x_sb[:, b, :], tg[:, 0:1], x0[:, b, :], ALU.mult, ALU.add)\
                       .then_inc(x_ready, 1)


def gated_layers(nc, io, out):
    with ExitStack() as stack:
        res = make_resident(nc, stack, io)
        attend_channels(nc, res, io["x"], io["ctx"], io["mask"], io["maskT"], io["a_wq4"], io["a_wk4"], io["a_wv"],
                        io["a_bq4"], io["a_bk4"], io["a_bv"], io["a_consts"], io["g_xattn"][0:1, 0:1])
        bit_linear_ffn(nc, res, io["b_gate_w"], io["b_val_w"], io["b_out_w"], io["b_gate_b"], io["b_val_b"],
                       io["b_out_b"], io["g_ffn"][0:1, 0:1])
        text_free_attention(nc, res, io["ctx"], io["ctxT"], io["c_wqT"], io["c_wkT"],
                            (io["c_wq"], io["c_wk"], io["c_wv"], io["c_wo"]), io["c_cols"],
                            (io["c_nq"], io["c_nk"]), io["c_ob"], io["g_xattn"][0:1, 1:2])
        expert_layer(nc, res, (io["d_wq"], io["d_wk"], io["d_wv"], io["d_wo"]), io["d_ln1"], io["d_gate_w"],
                     io["d_ln2"], io["d_gu_w"], io["d_down_w"], io["d_spread"], io["g_ffn"][0:1, 1:2], out)


def lay_out(inputs):
    f = {n: np.ascontiguousarray(v) for n, v in inputs.items()}
    out = {"x": f["x"], "ctx": f["ctx_2048"], "mask": f["mask_Bx1x2048_fk1"][:, 0, :]}
    out["maskT"] = out["mask"].reshape(BATCHES, 2, P).transpose(2, 0, 1).reshape(P, 2 * BATCHES)
    out["g_xattn"], out["g_ffn"] = f["g_xattn"][None, :], f["g_ffn"][None, :]

    def strips(rows):
        w = np.zeros((A_TILES, A_SLOTS, A_ROWS) + rows.shape[1:], rows.dtype)
        for j in range(A_TILES):
            for r in range(A_SLOTS):
                h = A_TILES * r + j
                for k in range(3):
                    w[j, r, A_HD * k:A_HD * k + A_HD] = rows[A_HD * h:A_HD * h + A_HD]
        return w.reshape((A_TILES * P,) + rows.shape[1:])

    out["a_wq4"], out["a_wk4"] = strips(f["L0_xattn_Wq"]).T, strips(f["L0_xattn_Wk"]).T
    out["a_wv"], out["a_bv"] = f["L0_xattn_Wv"].T, f["L0_xattn_bv"][None, :]
    out["a_bq4"] = strips(f["L0_xattn_bq"]).reshape(A_TILES, P).T
    out["a_bk4"] = strips(f["L0_xattn_bk"]).reshape(A_TILES, P).T
    c = np.zeros((A_ROWS, 8), np.float32)
    c[[*range(16, 24), 26], 0] = -1.0
    c[[*range(8, 16), 25], 1] = -1.0
    c[:, 2] = 1.0
    c[24:27, 2], c[24:27, 3], c[24:27, 5] = -1.0, 1.0, 1.0
    c[24:27, 4] = -NEG * A_ROOT
    c[27, 2], c[27, 3], c[27, 5] = 0.0, 1.0, 1.0
    out["a_consts"] = np.tile(c, (A_SLOTS, 1))

    def stationary(w):
        return w.T.reshape(-1, P, w.shape[0]).transpose(1, 0, 2).reshape(P, -1)

    for n in ("gate", "val", "out"):
        out[f"b_{n}_w"] = stationary(f[f"L0_ffn_{n}_w"])
        out[f"b_{n}_b"] = f[f"L0_ffn_{n}_b"][None, :]

    def by_heads(w, b):
        t = np.zeros((P, HEADS, DIM + 2), w.dtype)
        t[:, :, :DIM] = w.T.reshape(HEADS, P, DIM).transpose(1, 0, 2)
        t[:, :, DIM] = b.reshape(HEADS, P).T
        return t

    def tokens_last(a):
        return a.transpose(2, 0, 1).reshape(KT, P, -1).transpose(1, 0, 2)

    pre = "L1_xattn_"
    out["ctxT"] = tokens_last(out["ctx"])
    out["c_wqT"], out["c_wkT"] = by_heads(f[pre + "q_w"], f[pre + "q_b"]), by_heads(f[pre + "ki_w"], f[pre + "ki_b"])
    for n, m in (("q", "q_w"), ("k", "ki_w"), ("v", "vi_w")):
        out[f"c_w{n}"] = f[pre + m].reshape(KT, P, INNER).transpose(1, 0, 2)
    out["c_wo"] = f[pre + "o_w"].reshape(HEADS, P, DIM).transpose(1, 0, 2)
    out["c_cols"] = np.stack([f[pre + n].reshape(HEADS, P).T for n in ("q_b", "ki_b", "vi_b", "nq_s", "nki_s")], 1)
    out["c_nq"], out["c_nk"], out["c_ob"] = (f[pre + n][None, :] for n in ("nq_s", "nki_s", "o_b"))

    def natural(w):
        return w.T.reshape(KT, P, -1).transpose(1, 0, 2)

    pre = "L1_ffn_"
    out["d_wq"] = natural(f[pre + "q_w"].reshape(HEADS, QHD, DIM)[:, :HD].reshape(INNER, DIM))
    out["d_wk"], out["d_wv"] = natural(f[pre + "kv_w"][:INNER]), natural(f[pre + "kv_w"][INNER:2 * INNER])
    out["d_wo"] = f[pre + "o_w"].T.reshape(HEADS, P, DIM).transpose(1, 0, 2)
    out["d_ln1"], out["d_ln2"] = f[pre + "ln1_w"][None, :], f[pre + "ln2_w"][None, :]
    out["d_gate_w"] = natural(f[pre + "gate_w"])

    w1, sh = f[pre + "w1"], f[pre + "sh_gu_w"]
    gu = np.zeros((2, M_TILES * P, DIM), w1.dtype)
    down = np.zeros((M_TILES * P, DIM), w1.dtype)
    split = EXPERTS * EXPERT_HID
    for n in range(2):
        gu[n, :split] = w1[:, EXPERT_HID * n:EXPERT_HID * n + EXPERT_HID].reshape(split, DIM)
        gu[n, split:split + SHARED_HID] = sh[SHARED_HID * n:SHARED_HID * n + SHARED_HID]
    down[:split] = f[pre + "w2"].transpose(0, 2, 1).reshape(split, DIM)
    down[split:split + SHARED_HID] = f[pre + "sh_down_w"].T
    out["d_gu_w"] = gu.transpose(2, 0, 1).reshape(KT, P, 2, M_TILES * P).transpose(1, 2, 0, 3)
    out["d_down_w"] = down.reshape(M_TILES, P, DIM).transpose(1, 0, 2)
    owner = np.minimum(np.arange(M_TILES * P) // EXPERT_HID, EXPERTS)
    out["d_spread"] = (owner[None, :] == np.arange(KINDS)[:, None]).astype(np.float32)
    return {n: np.ascontiguousarray(v) for n, v in out.items()}


def kernel(**inputs):
    import concourse.bacc as bacc
    from concourse.bass_utils import run_bass_kernel_spmd

    nc = bacc.Bacc("TRN2", target_bir_lowering=False, num_devices=1)
    arrays = lay_out(inputs)
    io = {n: nc.dram_tensor(f"in_{n}", a.shape, mybir.dt.from_np(a.dtype), kind="ExternalInput").ap()
          for n, a in arrays.items()}
    out = nc.dram_tensor("out_x", (BATCHES, TOKENS, DIM), F32, kind="ExternalOutput").ap()
    gated_layers(nc, io, out)
    r = run_bass_kernel_spmd(nc, [{f"in_{n}": a for n, a in arrays.items()}], core_ids=[0])
    return r.results[0]["out_x"]
```

```python
import numpy as np
from contextlib import ExitStack

import concourse.bass as bass
from concourse import mybir
from concourse.bass import ds

F32 = mybir.dt.float32
F32R = mybir.dt.float32r
BF16 = mybir.dt.bfloat16
ALU = mybir.AluOpType
ACT = mybir.ActivationFunctionType
AX = mybir.AxisListType

P = 128
BATCHES, TOKENS, DIM = 16, 128, 256
KT = DIM // P
NEG = 1.0e6

A_HEADS, A_HD = 16, 8
A_SLOTS = 4
A_TILES = A_HEADS // A_SLOTS
A_ROWS = P // A_SLOTS
A_ROOT = float(A_HD) ** 0.5

ROUND = 12582912.0


class Scope:

    def __init__(self, nc, stack, tag):
        self.nc, self.stack, self.tag, self.sems = nc, stack, tag, []
        stack.callback(self.release)

    def release(self):
        if self.sems:
            self.nc.clear_and_free_semaphores(self.sems)
            self.nc.all_engine_barrier()

    def sb(self, name, shape, dt=F32):
        return self.stack.enter_context(self.nc.sbuf_tensor(f"{self.tag}_{name}", shape, dt))

    def ps(self, name, shape, dt=F32):
        return self.stack.enter_context(self.nc.psum_tensor(f"{self.tag}_{name}", shape, dt))

    def sem(self, name):
        self.sems.append(self.nc.alloc_semaphore(f"{self.tag}_{name}"))
        return self.sems[-1]


def after(eng, sem, value):
    if not (isinstance(value, int) and value <= 0):
        eng.wait_ge(sem, value)


def settled(eng, sem, value, met):
    eng.wait_ge(*met)
    after(eng, sem, value)


def pairs(eng, count, body):
    for p in range(2):
        body(0, p)
    with eng.Fori(1, count // 2 - 1) as i:
        for p in range(2):
            body(i, p)
    for p in range(2):
        body(count // 2 - 1, p)



def make_resident(nc, stack, io):
    x = stack.enter_context(nc.sbuf_tensor("x_sb", [P, BATCHES, DIM], F32))
    ident = stack.enter_context(nc.sbuf_tensor("ident", [P, P], F32))
    blank = nc.alloc_semaphore("blank")
    with nc.Block() as block:

        @block.gpsimd
        def _(pool):
            pool.memset(ident[:, :], 0.0).then_inc(blank, 1)
            pool.wait_ge(blank, 1)
            pool.affine_select(out=ident[:, :], in_=ident[:, :], compare_op=ALU.not_equal, fill=1.0, base=0,
                               pattern=[[-1, P]], channel_multiplier=1)
    return {"x": x, "ident": ident}


def attend_channels(nc, res, src, ctx_in, mask, maskT, wq4, wk4, wv, bq4, bk4, bv, consts, gate):
    x_sb = res["x"]
    with ExitStack() as stack:
        s = Scope(nc, stack, "a")
        ctx_sb = s.sb("ctx", [P, BATCHES, DIM])
        tm = s.sb("tm", [P, BATCHES, DIM])
        km = s.sb("km", [P, BATCHES, DIM])
        smT = s.sb("smT", [P, 2 * BATCHES])
        wraw = s.sb("wraw", [P, 2 * 512 + P])
        wh = s.sb("wh", [P, 2 * 512 + P], F32R)
        wl = s.sb("wl", [P, 2 * 512 + P], F32R)
        bcol = s.sb("bcol", [P, 2 * A_TILES])
        bias = s.sb("bias", [P, 2 * A_TILES])
        bvb = s.sb("bvb", [P, P])
        cst = s.sb("cst", [P, 8])
        g = s.sb("g", [P, 1])
        tg = s.sb("tg", [P, 1])
        stats = s.sb("stats", [P, BATCHES, 6])
        mv = s.sb("mv", [P, BATCHES, 2])
        var = s.sb("var", [P, BATCHES])
        half = s.sb("half", [P, BATCHES])
        zero = s.sb("zero", [P, DIM])
        rstd = s.sb("rstd", [P, BATCHES])
        xn = s.sb("xn", [P, DIM])
        xh = s.sb("xh", [P, DIM], F32R)
        xl = s.sb("xl", [P, DIM], F32R)
        ch = s.sb("ch", [P, DIM], F32R)
        cl = s.sb("cl", [P, DIM], F32R)
        full = s.sb("full", [P, 2, A_TILES, DIM])
        hi = s.sb("hi", [P, 2, A_TILES, DIM], F32R)
        qs = s.sb("qs", [P, 2, A_TILES, DIM], F32R)
        ks = s.sb("ks", [P, 2, A_TILES, DIM], F32R)
        vT = s.sb("vT", [P, 2, 2, A_HEADS, A_ROWS])
        vf = s.sb("vf", [P, P])
        mx = s.sb("mx", [P, 2, 2, A_HEADS])
        mT = s.sb("mT", [A_HEADS, 2, DIM], F32R)
        PR = 8
        prob = s.sb("prob", [P, PR, 2, DIM])
        osb = s.sb("osb", [P, 2, A_TILES, DIM])
        num = s.sb("num", [P, 2, DIM])
        den = s.sb("den", [P, 2, DIM])
        rden = s.sb("rden", [P, DIM])
        tgm = s.sb("tgm", [P, BATCHES, DIM])
        add = s.sb("add", [P, DIM])
        ident = res["ident"]
        proj = s.ps("proj", [P, A_TILES, DIM])
        s1 = [s.ps(f"s1_{k}", [P, 2, DIM]) for k in range(2)]
        s2 = [s.ps(f"s2_{k}", [P, 2, DIM]) for k in range(2)]
        out = s.ps("out", [P, A_TILES, DIM])

        ld_w, ld_x, ld_c = s.sem("ld_w"), s.sem("ld_x"), s.sem("ld_c")
        w_split, setup = s.sem("w_split"), s.sem("setup")
        v_own, p_own = s.sem("v_own"), s.sem("p_own")
        stats_ready, xn_ready = s.sem("stats_ready"), s.sem("xn_ready")
        parts_ready = s.sem("parts_ready")
        q_psum, k_psum, v_psum = s.sem("q_psum"), s.sem("k_psum"), s.sem("v_psum")
        q_full, k_full, v_full = s.sem("q_full"), s.sem("k_full"), s.sem("v_full")
        q_hi, k_hi = s.sem("q_hi"), s.sem("k_hi")
        q_stack, k_stack = s.sem("q_stack"), s.sem("k_stack")
        s1_psum, max_ready = s.sem("s1_psum"), s.sem("max_ready")
        mT_psum, mT_ready, m_in = s.sem("mT_psum"), s.sem("mT_ready"), s.sem("m_in")
        s2_psum, prob_ready = s.sem("s2_psum"), s.sem("prob_ready")
        out_psum, out_copied = s.sem("out_psum"), s.sem("out_copied")
        sent = [s.sem(f"sent{p}") for p in range(2)]
        moved = [s.sem(f"moved{p}") for p in range(2)]
        heads = nc.dram_tensor("a_heads", (2, 2, P, DIM), F32, kind="Internal").ap()
        rstd_ready, ln_own, vf_ready = s.sem("rstd_ready"), s.sem("ln_own"), s.sem("vf_ready")
        rden_ready = s.sem("rden_ready")
        x_done, tg_ready, tgm_ready = s.sem("x_done"), s.sem("tg_ready"), s.sem("tgm_ready")
        STEPS = BATCHES
        UNITS = A_HEADS

        with nc.Block() as block:

            @block.sync
            def _(sp):
                for h in range(2):
                    b = slice(8 * h, 8 * h + 8)
                    sp.dma_start(x_sb[:, b, :], src[b].rearrange("b p n -> p b n")).then_inc(ld_x, 16)
                sp.dma_start(wraw[:, 0:512], wq4).then_inc(ld_w, 16)
                sp.dma_start(wraw[:, 512:1024], wk4).then_inc(ld_w, 16)
                sp.dma_start(wraw[:, 1024:1152], wv).then_inc(ld_w, 16)
                sp.dma_start(bcol[:, 0:4], bq4).then_inc(ld_w, 16)
                sp.dma_start(bcol[:, 4:8], bk4).then_inc(ld_w, 16)
                sp.dma_start(bvb[:, :], bv.broadcast_to([P, P])).then_inc(ld_w, 16)
                sp.dma_start(cst[:, :], consts).then_inc(ld_w, 16)
                sp.dma_start(g[:, :], gate.broadcast_to([P, 1])).then_inc(ld_w, 16)
                sp.dma_start(smT[:, :], maskT).then_inc(ld_w, 16)
                sp.dma_start(tm[:, :, :].rearrange("p b n -> p (b n)"), mask.broadcast_to([P, BATCHES * DIM]))\
                    .then_inc(ld_w, 16)
                for h in range(2):
                    b = slice(8 * h, 8 * h + 8)
                    sp.dma_start(ctx_sb[:, b, :], ctx_in[b].rearrange("b p n -> p b n")).then_inc(ld_c, 16)

                def maxima(n, p):
                    settled(sp, mT_ready, n + 1, (ld_w, 16 * 10))
                    for r in range(A_SLOTS):
                        row = A_ROWS * r + 27
                        sp.dma_start(qs[row:row + 1, p, :, :].bitcast(F32),
                                     mT[A_TILES * r:A_TILES * r + A_TILES, p, :].bitcast(F32)).then_inc(m_in, 16)

                def body(i, p):
                    n = i * 2 + p
                    if not (isinstance(n, int) and n + 1 >= STEPS):
                        maxima(n + 1, 1 - p)
                    settled(sp, out_copied, n + 1, (ld_w, 16 * 10))
                    for r in range(A_SLOTS):
                        a = A_ROWS * r
                        for part in range(2):
                            sp.dma_start(heads[p, part].rearrange("(r j d) t -> r d j t", r=A_SLOTS, j=A_TILES)[r],
                                         osb[a + A_HD * part:a + A_HD * part + A_HD, p, :, :])\
                              .then_inc(sent[p], 16)
                    settled(sp, sent[p], 128 * (i + 1), (ld_w, 16 * 10))
                    settled(sp, x_done, 3 * (n - 1), (ld_w, 16 * 10))
                    sp.dma_start(num[:, p, :], heads[p, 0]).then_inc(moved[p], 16)
                    sp.dma_start(den[:, p, :], heads[p, 1]).then_inc(moved[p], 16)

                maxima(0, 0)
                pairs(sp, STEPS, body)

            @block.gpsimd
            def _(pool):
                pool.memset(half[:, :], -0.5).then_inc(p_own, 1)
                pool.memset(zero[:, :], 0.0).then_inc(p_own, 1)
                pool.memset(vT[:, :, :, :, :], 0.0).then_inc(p_own, 1)
                pool.wait_ge(p_own, 3)
                pool.memset(vT[:, :, :, :, A_HD:2 * A_HD], 1.0).then_inc(setup, 1)

                def prologue(n):
                    pool.wait_ge(xn_ready, n + 1)
                    after(pool, v_psum, n)
                    pool.tensor_tensor(xh[:, :], xn[:, :], zero[:, :], ALU.add).then_inc(p_own, 1)
                    pool.tensor_copy(ch[:, :], ctx_sb[:, ds(n, 1), :]).then_inc(p_own, 1)
                    pool.wait_ge(p_own, 2 * n + 5)
                    pool.tensor_tensor(xl[:, :], xn[:, :], xh[:, :].bitcast(F32), ALU.subtract)\
                        .then_inc(parts_ready, 1)
                    pool.tensor_tensor(cl[:, :], ctx_sb[:, ds(n, 1), :], ch[:, :].bitcast(F32), ALU.subtract)\
                        .then_inc(parts_ready, 1)

                def finish(n, i, p):
                    pool.wait_ge(rden_ready, n + 1)
                    after(pool, x_done, 3 * n)
                    pool.tensor_tensor(add[:, :], num[:, p, :], rden[:, :], ALU.mult).then_inc(x_done, 1)
                    pool.wait_ge(x_done, 3 * n + 1)
                    pool.tensor_tensor(add[:, :], add[:, :], tgm[:, ds(n, 1), :], ALU.mult).then_inc(x_done, 1)
                    pool.wait_ge(x_done, 3 * n + 2)
                    pool.tensor_tensor(x_sb[:, ds(n, 1), :], x_sb[:, ds(n, 1), :], add[:, :], ALU.add)\
                        .then_inc(x_done, 1)

                def body(i, p):
                    n = i * 2 + p
                    if not (isinstance(n, int) and n + 2 >= STEPS):
                        prologue(n + 2)
                    if not (isinstance(n, int) and n == 0):
                        finish(n - 1, i - 1 + p, 1 - p)

                pool.wait_ge(stats_ready, 1)
                pool.tensor_tensor(rstd[:, :], var[:, :], half[:, :], ALU.pow).then_inc(rstd_ready, 1)
                pool.wait_ge(ld_c, 32)
                prologue(0)
                prologue(1)
                pool.wait_ge(tgm_ready, 1)
                pairs(pool, STEPS, body)
                finish(STEPS - 1, STEPS // 2 - 1, 1)

            @block.scalar
            def _(act):
                act.wait_ge(ld_w, 16 * 10)
                act.activation(wh[:, :], wraw[:, :], ACT.Copy).then_inc(w_split, 1)
                act.activation(tg[:, :], g[:, :], ACT.Tanh).then_inc(tg_ready, 1)
                act.wait_ge(tg_ready, 1)
                act.activation(tgm[:, :, :], tm[:, :, :], ACT.Copy, scale=tg[:, 0:1]).then_inc(tgm_ready, 1)

                def evacuate(n, kind):
                    full_s, hi_s = ((q_full, q_hi), (k_full, k_hi))[kind]
                    act.wait_ge(full_s, A_TILES * (n + 1))
                    act.activation(hi[:, kind, :, :], full[:, kind, :, :], ACT.Copy).then_inc(hi_s, 1)

                def body(i, p):
                    n = i * 2 + p
                    for u in range(UNITS):
                        if u % A_SLOTS == 0:
                            after(act, out_psum, n * A_TILES + u // A_SLOTS + 1 - PR // A_SLOTS)
                        act.wait_ge(s2_psum, n * UNITS + u + 1)
                        act.activation(prob[:, u % PR, :, :], s2[u % 2][:, :, :], ACT.Exp,
                                       scale=1.0 / A_ROOT).then_inc(prob_ready, 1)
                        if u in (9, 12) and not (isinstance(n, int) and n + 2 >= STEPS):
                            evacuate(n + 2, u // 3 - 3)
                    act.wait_ge(out_psum, (n + 1) * A_TILES)
                    after(act, x_done, 3 * (n - 1))
                    act.activation(osb[:, p, :, :], out[:, :, :], ACT.Copy).then_inc(out_copied, 1)

                for n in range(2):
                    evacuate(n, 0)
                    evacuate(n, 1)
                pairs(act, STEPS, body)

            @block.tensor
            def _(pe):
                pe.wait_ge(w_split, 2)

                def project(n, kind):
                    if kind == 0:
                        pe.wait_ge(parts_ready, 2 * n + 2)
                        after(pe, v_full, 2 * n)
                    else:
                        pe.wait_ge(q_full, A_TILES * (n + 1))
                    h, l, done = ((xh, xl, q_psum), (ch, cl, k_psum))[kind]
                    for j in range(A_TILES):
                        w = slice(512 * kind + P * j, 512 * kind + P * j + P)
                        if kind == 0 and j == 2:
                            after(pe, mT_ready, n - 1)
                        pe.matmul(proj[:, j, :], wh[:, w], h[:, :], start=True, stop=False)
                        pe.matmul(proj[:, j, :], wh[:, w], l[:, :], start=False, stop=False)
                        mm = pe.matmul(proj[:, j, :], wl[:, w], h[:, :], start=False, stop=True)
                        if j % 2:
                            mm.then_inc(done, 1)

                def project_v(n):
                    pe.wait_ge(k_full, A_TILES * (n + 1))
                    w = slice(1024, 1152)
                    for t in range(2):
                        c = slice(P * t, P * t + P)
                        o = proj[:, t, 0:P]
                        pe.matmul(o, ch[:, c], wh[:, w], start=True, stop=False)
                        pe.matmul(o, ch[:, c], wl[:, w], start=False, stop=False)
                        mm = pe.matmul(o, cl[:, c], wh[:, w], start=False, stop=True)
                    mm.then_inc(v_psum, 1)

                def first_scores(n, p, u):
                    j, r = divmod(u, A_SLOTS)
                    rows = slice(A_ROWS * r, A_ROWS * r + A_ROWS)
                    if u == 0:
                        pe.wait_ge(q_stack, n + 1)
                        pe.wait_ge(k_stack, n + 1)
                    after(pe, max_ready, n * UNITS + u - 1)
                    for t in range(2):
                        mm = pe.matmul(s1[u % 2][:, t, :], qs[rows, p, j, P * t:P * t + P], ks[rows, p, j, :],
                                       start=True, stop=True)
                    mm.then_inc(s1_psum, 1)

                def turn_maxima(n, p, last):
                    pe.wait_ge(max_ready, (n + 1) * UNITS)
                    pe.wait_ge(k_full, A_TILES * (n + (1 if last else 2)))
                    for t in range(2):
                        mm = pe.transpose(proj[0:A_HEADS, 2, P * t:P * t + P], mx[:, p, t, :], ident[:, :])
                    mm.then_inc(mT_psum, 1)

                def second_scores(n, p, u):
                    j, r = divmod(u, A_SLOTS)
                    rows = slice(A_ROWS * r, A_ROWS * r + A_ROWS)
                    if u == 0:
                        pe.wait_ge(m_in, 64 * (n + 1))
                    after(pe, prob_ready, n * UNITS + u - 1)
                    for t in range(2):
                        mm = pe.matmul(s2[u % 2][:, t, :], ks[rows, p, j, P * t:P * t + P], qs[rows, p, j, :],
                                       start=True, stop=True)
                    mm.then_inc(s2_psum, 1)

                def weigh(n, p, j):
                    pe.wait_ge(prob_ready, n * UNITS + A_SLOTS * (j + 1))
                    if j == 0:
                        pe.wait_ge(v_full, 2 * (n + 1))
                        after(pe, out_copied, n)
                    for t in range(2):
                        for r in range(A_SLOTS):
                            mm = pe.matmul(out[A_ROWS * r:A_ROWS * r + A_ROWS, j, :],
                                           vT[:, p, t, A_TILES * r + j, :],
                                           prob[:, (A_SLOTS * j + r) % PR, t, :], start=(t == 0), stop=(t == 1),
                                           skip_group_check=True)
                    mm.then_inc(out_psum, 1)

                def body(i, p):
                    n = i * 2 + p
                    more = not (isinstance(n, int) and n + 1 >= STEPS)
                    for u in range(UNITS):
                        if more and 4 <= u < 12:
                            first_scores(n + 1, 1 - p, 2 * u - 8)
                        second_scores(n, p, u)
                        if more and 4 <= u < 12:
                            first_scores(n + 1, 1 - p, 2 * u - 7)
                        if u >= 2 and (u - 2) % A_SLOTS == A_SLOTS - 1:
                            weigh(n, p, (u - 2) // A_SLOTS)
                        if more and u == 0:
                            project_v(n + 1)
                        if u in (6, 8) and not (isinstance(n, int) and n + 2 >= STEPS):
                            project(n + 2, u // 2 - 3)
                        if more and u == 13:
                            turn_maxima(n + 1, 1 - p, isinstance(n, int) and n + 2 >= STEPS)
                    weigh(n, p, A_TILES - 1)

                project(0, 0)
                project(0, 1)
                project_v(0)
                for u in range(UNITS):
                    first_scores(0, 0, u)
                    if u in (7, 11):
                        project(1, u // 4 - 1)
                turn_maxima(0, 0, False)
                pairs(pe, STEPS, body)

            @block.vector
            def _(dve):
                dve.wait_ge(ld_x, 32)
                for b in range(BATCHES):
                    dve.bn_stats(stats[:, b, :], x_sb[:, b, :]).then_inc(ln_own, 1)
                for b in range(BATCHES):
                    dve.wait_ge(ln_own, b + 1)
                    dve.bn_aggr(mv[:, b, :], stats[:, b, :]).then_inc(ln_own, 1)
                dve.wait_ge(ln_own, 2 * BATCHES)
                dve.tensor_scalar(var[:, :], mv[:, :, 1], 1e-5, None, ALU.add).then_inc(stats_ready, 1)
                dve.wait_ge(w_split, 1)
                dve.wait_ge(ld_w, 16 * 10)
                dve.wait_ge(setup, 1)
                dve.tensor_tensor(wl[:, :], wraw[:, :], wh[:, :].bitcast(F32), ALU.subtract).then_inc(w_split, 1)
                dve.tensor_scalar(bias[:, 0:4], bcol[:, 0:4], cst[:, 4:5], None, ALU.add)
                dve.tensor_scalar(bias[:, 4:8], bcol[:, 4:8], cst[:, 5:6], None, ALU.add)

                def layernorm(n):
                    after(dve, parts_ready, 2 * n)
                    dve.tensor_scalar(xn[:, :], x_sb[:, ds(n, 1), :], mv[:, ds(n, 1), 0:1], rstd[:, ds(n, 1)],
                                      ALU.subtract, ALU.mult).then_inc(xn_ready, 1)

                def read_projection(n, kind):
                    psum_s, full_s = ((q_psum, q_full), (k_psum, k_full))[kind]
                    m = (tm, km)[kind]
                    after(dve, (q_stack, k_stack)[kind], n)
                    for j in range(A_TILES):
                        dve.wait_ge(psum_s, 2 * n + j // 2 + 1)
                        dve.scalar_tensor_tensor(full[:, kind, j, :], proj[:, j, :],
                                                 bias[:, 4 * kind + j:4 * kind + j + 1], m[:, ds(n, 1), :],
                                                 ALU.add, ALU.mult).then_inc(full_s, 1)

                def stack_parts(n, p, kind):
                    hi_s, stack_s = ((q_hi, q_stack), (k_hi, k_stack))[kind]
                    t = (qs, ks)[kind]
                    dve.wait_ge(hi_s, n + 1)
                    after(dve, s2_psum, UNITS * (n - 1))
                    dve.scalar_tensor_tensor(t[:, p, :, :], hi[:, kind, :, :].bitcast(F32), cst[:, kind:kind + 1],
                                             full[:, kind, :, :], ALU.mult, ALU.add).then_inc(stack_s, 1)

                def read_v(n, p):
                    dve.wait_ge(v_psum, n + 1)
                    after(dve, out_psum, A_TILES * (n - 1))
                    for t in range(2):
                        after(dve, v_full, 2 * n + t)
                        dve.tensor_tensor(vf[:, :], proj[:, t, 0:P], bvb[:, :], ALU.add).then_inc(vf_ready, 1)
                        dve.wait_ge(vf_ready, 2 * n + t + 1)
                        dve.tensor_scalar(vT[:, p, t, :, 0:A_HD], vf[:, :].rearrange("p (h d) -> p h d", h=A_HEADS),
                                          smT[:, ds(n * 2 + t, 1)], None, ALU.mult).then_inc(v_full, 1)

                def take_max(n, p, u):
                    dve.wait_ge(s1_psum, n * UNITS + u + 1)
                    h = A_TILES * (u % A_SLOTS) + u // A_SLOTS
                    dve.tensor_reduce(mx[:, p, :, h], s1[u % 2][:, :, :], AX.X, ALU.max).then_inc(max_ready, 1)

                def read_maxima(n, p):
                    dve.wait_ge(mT_psum, n + 1)
                    dve.tensor_scalar(mT[:, p, :], proj[0:A_HEADS, 2, :], -1.0, None, ALU.mult).then_inc(mT_ready, 1)

                def invert(n, i, p):
                    dve.wait_ge(moved[p], 32 * (i + 1))
                    after(dve, x_done, 3 * (n - 1) + 1)
                    dve.reciprocal(rden[:, :], den[:, p, :]).then_inc(rden_ready, 1)

                def body(i, p):
                    n = i * 2 + p
                    more = not (isinstance(n, int) and n + 2 >= STEPS)
                    if isinstance(n, int) and n + 1 >= STEPS:
                        invert(n - 1, i - 1 + p, 1 - p)
                        invert(n, i, p)
                        return
                    stack_parts(n + 1, 1 - p, 0)
                    stack_parts(n + 1, 1 - p, 1)
                    read_v(n + 1, 1 - p)
                    if more:
                        layernorm(n + 2)
                    for u in range(UNITS):
                        take_max(n + 1, 1 - p, u)
                        if more and u in (5, 9):
                            read_projection(n + 2, (u - 5) // 4)
                        if u == 13 and not (isinstance(n, int) and n == 0):
                            invert(n - 1, i - 1 + p, 1 - p)
                    read_maxima(n + 1, 1 - p)

                dve.wait_ge(rstd_ready, 1)
                layernorm(0)
                dve.tensor_scalar(km[:, :, :], tm[:, :, :], cst[:, 2:3], cst[:, 3:4], ALU.mult, ALU.add)\
                   .then_inc(v_own, 1)
                dve.wait_ge(v_own, 1)
                read_projection(0, 0)
                read_projection(0, 1)
                stack_parts(0, 0, 0)
                stack_parts(0, 0, 1)
                read_v(0, 0)
                layernorm(1)
                for u in range(UNITS):
                    take_max(0, 0, u)
                    if u in (7, 11):
                        read_projection(1, u // 4 - 1)
                read_maxima(0, 0)
                pairs(dve, STEPS, body)


def bit_linear_ffn(nc, res, gate_w, val_w, out_w, gate_b, val_b, out_b, gate):
    x_sb, ident = res["x"], res["ident"]
    HID = 4 * DIM
    HT = HID // P
    HALF = HID // 2
    with ExitStack() as stack:
        s = Scope(nc, stack, "b")
        raw = s.sb("raw", [P, 3, KT * HID])
        tmp = s.sb("tmp", [P, 3, KT * HID])
        junk = s.sb("junk", [P, KT * HID])
        back = s.sb("back", [P, 1])
        wq = s.sb("wq", [P, 3, KT * HID], BF16)
        bb = s.sb("bb", [P, 2, HID])
        obb = s.sb("obb", [P, DIM])
        g = s.sb("g", [P, 1])
        tg = s.sb("tg", [P, 1])
        identb = s.sb("identb", [P, P], BF16)
        ones = s.sb("ones", [P, P])
        wabs = s.sb("wabs", [P, 3])
        gw = s.sb("gw", [P, 3])
        rgw = s.sb("rgw", [P, 3])
        gw127 = s.sb("gw127", [P, 3])
        stats = s.sb("stats", [P, BATCHES, 6])
        mv = s.sb("mv", [P, BATCHES, 2])
        var = s.sb("var", [P, BATCHES])
        half = s.sb("half", [P, BATCHES])
        rstd = s.sb("rstd", [P, BATCHES])
        xn = s.sb("xn", [P, BATCHES, DIM])
        gx = s.sb("gx", [P, BATCHES])
        rx = s.sb("rx", [P, BATCHES])
        sx = s.sb("sx", [P, BATCHES])
        sc = s.sb("sc", [P, BATCHES, 2])
        xr = s.sb("xr", [P, DIM])
        xq = s.sb("xq", [P, 2, DIM], BF16)
        xqT = s.sb("xqT", [P, 2, KT, P], BF16)
        gt = s.sb("gt", [P, HID])
        gs = s.sb("gs", [P, HID])
        vt = s.sb("vt", [P, HID])
        h = s.sb("h", [P, HID])
        gh = s.sb("gh", [P, 4])
        hr = s.sb("hr", [P, HID])
        hq = s.sb("hq", [P, HID], BF16)
        hqT = s.sb("hqT", [P, HT, P], BF16)
        so = s.sb("so", [P, 2])
        y = s.sb("y", [P, DIM])
        gv = [s.ps(f"gv{k}", [P, HALF]) for k in range(4)]
        hT_ps = s.ps("hT", [P, HT, P], BF16)
        xT_ps = s.ps("xT", [P, KT, P], BF16)
        o_ps = s.ps("o", [P, DIM])
        w_ps = s.ps("w", [P, 4])

        ld_w, ld_b = s.sem("ld_w"), s.sem("ld_b")
        consts_ready, tanh_ready = s.sem("consts_ready"), s.sem("tanh_ready")
        own = s.sem("own")
        stats_ready, rstd_ready = s.sem("stats_ready"), s.sem("rstd_ready")
        wabs_ready, wabs_psum, weights_ready = s.sem("wabs_ready"), s.sem("wabs_psum"), s.sem("weights_ready")
        rounded = s.sem("rounded")
        xr_ready, xq_ready = s.sem("xr_ready"), s.sem("xq_ready")
        xT_psum, xT_ready = s.sem("xT_psum"), s.sem("xT_ready")
        gv_psum, gt_ready, silu_ready, vt_ready = s.sem("gv_psum"), s.sem("gt_ready"), s.sem("silu_ready"), s.sem("vt_ready")
        h_ready, h_own, hq_ready = s.sem("h_ready"), s.sem("h_own"), s.sem("hq_ready")
        hT_psum, hT_ready = s.sem("hT_psum"), s.sem("hT_ready")
        o_psum, y_ready, x_done = s.sem("o_psum"), s.sem("y_ready"), s.sem("x_done")
        H_OWN = 6

        def following(n, k):
            return not (isinstance(n, int) and n + k >= BATCHES)

        with nc.Block() as block:

            @block.sync
            def _(sp):
                for k, w in enumerate((gate_w, val_w, out_w)):
                    sp.dma_start(raw[:, k, :], w).then_inc(ld_w, 16)
                sp.dma_start(bb[:, 0, :], gate_b.broadcast_to([P, HID])).then_inc(ld_b, 16)
                sp.dma_start(bb[:, 1, :], val_b.broadcast_to([P, HID])).then_inc(ld_b, 16)
                sp.dma_start(obb[:, :], out_b.broadcast_to([P, DIM])).then_inc(ld_b, 16)
                sp.dma_start(g[:, :], gate.broadcast_to([P, 1])).then_inc(ld_b, 16)

            @block.gpsimd
            def _(pool):
                pool.memset(half[:, :], -0.5).then_inc(consts_ready, 1)
                pool.memset(ones[:, :], 1.0).then_inc(consts_ready, 1)
                pool.memset(back[:, :], -ROUND).then_inc(consts_ready, 1)
                pool.tensor_copy(identb[:, :], ident[:, :]).then_inc(consts_ready, 1)
                pool.wait_ge(consts_ready, 4)
                pool.wait_ge(stats_ready, 1)
                pool.tensor_tensor(rstd[:, :], var[:, :], half[:, :], ALU.pow).then_inc(rstd_ready, 1)

                def multiply(i, p):
                    n = i * 2 + p
                    for c in range(2):
                        cols = slice(HALF * c, HALF * c + HALF)
                        pool.wait_ge(vt_ready, 2 * n + c + 1)
                        pool.wait_ge(silu_ready, 2 * n + c + 1)
                        after(pool, hq_ready, n)
                        pool.tensor_tensor(h[:, cols], gs[:, cols], vt[:, cols], ALU.mult).then_inc(h_ready, 1)

                pairs(pool, BATCHES, multiply)

            @block.scalar
            def _(act):
                act.wait_ge(ld_w, 48)
                for k in range(3):
                    after(act, wabs_ready, k)
                    act.activation(junk[:, :], raw[:, k, :], ACT.Abs, accum_out=wabs[:, k:k + 1]).then_inc(wabs_ready, 1)
                act.wait_ge(ld_b, 64)
                act.activation(tg[:, :], g[:, :], ACT.Tanh).then_inc(tanh_ready, 1)
                act.wait_ge(consts_ready, 4)
                for k in range(3):
                    act.wait_ge(rounded, k + 1)
                    act.activation(wq[:, k, :], tmp[:, 1 + k % 2, :], ACT.Identity, bias=back[:, 0:1])\
                        .then_inc(weights_ready, 1)

                def turned_x(n, p):
                    act.wait_ge(xT_psum, n + 1)
                    act.activation(xqT[:, p, :, :], xT_ps[:, :, :], ACT.Copy).then_inc(xT_ready, 1)

                def silu(n, c):
                    act.wait_ge(gt_ready, 2 * n + c + 1)
                    after(act, h_ready, 2 * n + c - 1)
                    act.activation(gs[:, HALF * c:HALF * c + HALF], gt[:, HALF * c:HALF * c + HALF], ACT.Silu)\
                        .then_inc(silu_ready, 1)

                def body(i, p):
                    n = i * 2 + p
                    if following(n, 2):
                        turned_x(n + 2, p)
                    act.wait_ge(hT_psum, n + 1)
                    act.activation(hqT[:, :, :], hT_ps[:, :, :], ACT.Copy).then_inc(hT_ready, 1)
                    if following(n, 2):
                        silu(n + 2, 0)
                        silu(n + 2, 1)

                turned_x(0, 0)
                silu(0, 0)
                silu(0, 1)
                turned_x(1, 1)
                silu(1, 0)
                silu(1, 1)
                pairs(act, BATCHES, body)

            @block.tensor
            def _(pe):
                pe.wait_ge(consts_ready, 4)
                pe.wait_ge(wabs_ready, 3)
                pe.matmul(w_ps[:, 0:3], ones[:, :], wabs[:, :], start=True, stop=True).then_inc(wabs_psum, 1)

                def turn_x(n, p):
                    pe.wait_ge(xq_ready, n + 1)
                    after(pe, xT_ready, n)
                    for k in range(KT):
                        mm = pe.transpose(xT_ps[:, k, :], xq[:, p, P * k:P * k + P], identb[:, :])
                    mm.then_inc(xT_psum, 1)

                def gate_and_value(n, p):
                    pe.wait_ge(xT_ready, n + 1)
                    for c in range(4):
                        w, half_ = c // 2, c % 2
                        after(pe, (gt_ready, vt_ready)[w], 2 * n + half_ - 1)
                        for k in range(KT):
                            col = HID * k + HALF * half_
                            mm = pe.matmul(gv[c][:, :], xqT[:, p, k, :], wq[:, w, col:col + HALF],
                                           start=(k == 0), stop=(k == KT - 1))
                        mm.then_inc(gv_psum, 1)

                def turn_h(n):
                    pe.wait_ge(hq_ready, n + 1)
                    after(pe, hT_ready, n)
                    for k in range(HT):
                        mm = pe.transpose(hT_ps[:, k, :], hq[:, P * k:P * k + P], identb[:, :])
                    mm.then_inc(hT_psum, 1)

                def project(n):
                    pe.wait_ge(hT_ready, n + 1)
                    after(pe, y_ready, n)
                    for k in range(HT):
                        mm = pe.matmul(o_ps[:, :], hqT[:, k, :], wq[:, 2, DIM * k:DIM * k + DIM],
                                       start=(k == 0), stop=(k == HT - 1))
                    mm.then_inc(o_psum, 1)

                def body(i, p):
                    n = i * 2 + p
                    if following(n, 2):
                        turn_x(n + 2, p)
                    turn_h(n)
                    if following(n, 2):
                        gate_and_value(n + 2, p)
                    project(n)

                turn_x(0, 0)
                pe.wait_ge(weights_ready, 3)
                gate_and_value(0, 0)
                turn_x(1, 1)
                gate_and_value(1, 1)
                pairs(pe, BATCHES, body)

            @block.vector
            def _(dve):
                n_own = [0]

                def chained(ins):
                    n_own[0] += 1
                    ins.then_inc(own, 1)
                    dve.wait_ge(own, n_own[0])

                for b in range(BATCHES):
                    dve.bn_stats(stats[:, b, :], x_sb[:, b, :]).then_inc(own, 1)
                n_own[0] = BATCHES
                dve.wait_ge(own, n_own[0])
                for b in range(BATCHES):
                    dve.bn_aggr(mv[:, b, :], stats[:, b, :]).then_inc(own, 1)
                n_own[0] += BATCHES
                dve.wait_ge(own, n_own[0])
                dve.tensor_scalar(var[:, :], mv[:, :, 1], 1e-5, None, ALU.add).then_inc(stats_ready, 1)
                dve.wait_ge(rstd_ready, 1)
                for b in range(BATCHES):
                    dve.tensor_scalar(xn[:, b, :], x_sb[:, b, :], mv[:, b, 0:1], rstd[:, b:b + 1],
                                      ALU.subtract, ALU.mult).then_inc(own, 1)
                n_own[0] += BATCHES
                dve.wait_ge(own, n_own[0])
                chained(dve.tensor_reduce(gx[:, :], xn[:, :, :], AX.X, ALU.max, apply_absolute_value=True))
                chained(dve.tensor_scalar(gx[:, :], gx[:, :], 1e-5, None, ALU.max))
                chained(dve.reciprocal(rx[:, :], gx[:, :]))
                chained(dve.tensor_scalar(sx[:, :], rx[:, :], 127.0, None, ALU.mult))

                def quantise_x(n, p):
                    after(dve, xq_ready, n)
                    dve.tensor_scalar(xr[:, :], xn[:, ds(n, 1), :], sx[:, ds(n, 1)], ROUND, ALU.mult, ALU.add)\
                       .then_inc(xr_ready, 1)
                    dve.wait_ge(xr_ready, n + 1)
                    after(dve, xT_psum, n - 1)
                    dve.tensor_scalar(xq[:, p, :], xr[:, :], ROUND, 127.0, ALU.subtract, ALU.min)\
                       .then_inc(xq_ready, 1)

                for n in range(2):
                    if n == 1:
                        dve.wait_ge(ld_w, 48)
                        dve.wait_ge(wabs_psum, 1)
                        chained(dve.tensor_scalar(gw[:, :], w_ps[:, 0:3], 1.0 / (DIM * HID), 1e-5, ALU.mult, ALU.max))
                        chained(dve.reciprocal(rgw[:, :], gw[:, :]))
                        chained(dve.tensor_scalar(gw127[:, :], gw[:, :], 1.0 / 127.0, None, ALU.mult))
                        for w in range(2):
                            chained(dve.tensor_scalar(sc[:, :, w], gx[:, :], gw127[:, w:w + 1], None, ALU.mult))
                        for k in range(3):
                            chained(dve.tensor_scalar(tmp[:, 0, :], raw[:, k, :], rgw[:, k:k + 1], -1.0,
                                                      ALU.mult, ALU.max))
                            after(dve, weights_ready, k - 1)
                            dve.tensor_scalar(tmp[:, 1 + k % 2, :], tmp[:, 0, :], 1.0, ROUND, ALU.min, ALU.add)\
                               .then_inc(rounded, 1)
                            dve.wait_ge(rounded, k + 1)
                    quantise_x(n, n % 2)
                dve.wait_ge(ld_b, 64)
                dve.wait_ge(tanh_ready, 1)

                def hidden(n):
                    for c in range(4):
                        w, half_ = c // 2, c % 2
                        cols = slice(HALF * half_, HALF * half_ + HALF)
                        dve.wait_ge(gv_psum, 4 * n + c + 1)
                        after(dve, (silu_ready, h_ready)[w], 2 * n + half_ - 1)
                        dve.scalar_tensor_tensor((gt, vt)[w][:, cols], gv[c][:, :], sc[:, ds(n, 1), w:w + 1],
                                                 bb[:, w, cols], ALU.mult, ALU.add)\
                           .then_inc((gt_ready, vt_ready)[w], 1)

                def quantise_h(n):
                    base = H_OWN * n
                    dve.wait_ge(h_ready, 2 * n + 2)
                    dve.tensor_reduce(gh[:, 0:1], h[:, :], AX.X, ALU.max, apply_absolute_value=True).then_inc(h_own, 1)
                    dve.wait_ge(h_own, base + 1)
                    dve.tensor_scalar(gh[:, 1:2], gh[:, 0:1], 1e-5, None, ALU.max).then_inc(h_own, 1)
                    dve.wait_ge(h_own, base + 2)
                    dve.reciprocal(gh[:, 2:3], gh[:, 1:2]).then_inc(h_own, 1)
                    dve.wait_ge(h_own, base + 3)
                    dve.tensor_scalar(gh[:, 3:4], gh[:, 2:3], 127.0, None, ALU.mult).then_inc(h_own, 1)
                    dve.wait_ge(h_own, base + 4)
                    dve.tensor_scalar(hr[:, :], h[:, :], gh[:, 3:4], ROUND, ALU.mult, ALU.add).then_inc(h_own, 1)
                    dve.wait_ge(h_own, base + 5)
                    after(dve, hT_psum, n)
                    dve.tensor_scalar(hq[:, :], hr[:, :], ROUND, 127.0, ALU.subtract, ALU.min).then_inc(hq_ready, 1)

                def scale_out(n, p):
                    dve.tensor_scalar(so[:, p:p + 1], gh[:, 1:2], gw127[:, 2:3], None, ALU.mult).then_inc(h_own, 1)

                def finish(n, p):
                    dve.wait_ge(h_own, H_OWN * (n + 1))
                    dve.wait_ge(o_psum, n + 1)
                    after(dve, x_done, n)
                    dve.scalar_tensor_tensor(y[:, :], o_ps[:, :], so[:, p:p + 1], obb[:, :], ALU.mult, ALU.add)\
                       .then_inc(y_ready, 1)
                    dve.wait_ge(y_ready, n + 1)
                    dve.scalar_tensor_tensor(x_sb[:, ds(n, 1), :], y[:, :], tg[:, 0:1], x_sb[:, ds(n, 1), :],
                                             ALU.mult, ALU.add).then_inc(x_done, 1)

                def body(i, p):
                    n = i * 2 + p
                    if following(n, 2):
                        quantise_x(n + 2, p)
                    if following(n, 1):
                        quantise_h(n + 1)
                        scale_out(n + 1, 1 - p)
                    if following(n, 2):
                        hidden(n + 2)
                    finish(n, p)

                hidden(0)
                hidden(1)
                quantise_h(0)
                scale_out(0, 0)
                pairs(dve, BATCHES, body)
                dve.wait_ge(x_done, BATCHES)

HEADS, HD = 16, 128
INNER = HEADS * HD
GB = 4
GROUPS = BATCHES // GB
QUADS = HEADS // 4
GT = GB * TOKENS
UNITS = GROUPS * 4


def prepare_tokens(nc, x_sb, ident, xn, xTh, xTl, eps, weight=None, centre=False, fetch=None, saved=None):
    with ExitStack() as stack:
        s = Scope(nc, stack, f"{xTh.name}_norm")
        stats = s.sb("stats", [P, BATCHES, 6])
        mv = s.sb("mv", [P, BATCHES, 2])
        var = s.sb("var", [P, BATCHES])
        half = s.sb("half", [P, BATCHES])
        rstd = s.sb("rstd", [P, BATCHES])
        wb = s.sb("wb", [P, DIM])
        turned = [s.ps(f"turned{k}", [P, KT, 2, P]) for k in range(4)]
        ld, consts, own = s.sem("ld"), s.sem("consts"), s.sem("own")
        var_ready, rstd_ready, xn_ready = s.sem("var_ready"), s.sem("rstd_ready"), s.sem("xn_ready")
        turned_psum, hi_ready, lo_ready = s.sem("turned_psum"), s.sem("hi_ready"), s.sem("lo_ready")
        PAIRS = BATCHES // 2

        with nc.Block() as block:
            @block.sync
            def _(sp):
                if weight is not None:
                    sp.dma_start(wb[:, :], weight.broadcast_to([P, DIM])).then_inc(ld, 16)
                if fetch is not None:
                    fetch(sp)

            ROUNDS = 2 if centre else 1

            @block.gpsimd
            def _(pool):
                pool.memset(half[:, :], -0.5).then_inc(consts, 1)
                pool.wait_ge(consts, 1)
                for n in range(ROUNDS):
                    pool.wait_ge(var_ready, n + 1)
                    pool.tensor_tensor(rstd[:, :], var[:, :], half[:, :], ALU.pow).then_inc(rstd_ready, 1)

            @block.tensor
            def _(pe):
                for m in range(PAIRS):
                    pe.wait_ge(xn_ready, 2 * m + 2)
                    after(pe, lo_ready, m - 3)
                    for b in range(2):
                        for k in range(KT):
                            mm = pe.transpose(turned[m % 4][:, k, b, :], xn[:, 2 * m + b, P * k:P * k + P], ident[:, :])
                    mm.then_inc(turned_psum, 1)

            @block.scalar
            def _(act):
                for m in range(PAIRS):
                    act.wait_ge(turned_psum, m + 1)
                    act.activation(xTh[:, :, 2 * P * m:2 * P * m + 2 * P],
                                   turned[m % 4][:, :, :, :].rearrange("p k b t -> p k (b t)"), ACT.Copy)\
                        .then_inc(hi_ready, 1)

            @block.vector
            def _(dve):
                def statistics(n):
                    for b in range(BATCHES):
                        dve.bn_stats(stats[:, b, :], x_sb[:, b, :]).then_inc(own, 1)
                    dve.wait_ge(own, n + BATCHES)
                    for b in range(BATCHES):
                        dve.bn_aggr(mv[:, b, :], stats[:, b, :]).then_inc(own, 1)
                    dve.wait_ge(own, n + 2 * BATCHES)

                counted = 0
                if centre:
                    statistics(0)
                    dve.tensor_scalar(var[:, :], mv[:, :, 1], 1e-5, None, ALU.add).then_inc(var_ready, 1)
                    dve.wait_ge(rstd_ready, 1)
                    dve.wait_ge(saved, 16)
                    for b in range(BATCHES):
                        dve.tensor_scalar(x_sb[:, b, :], x_sb[:, b, :], mv[:, b, 0:1], rstd[:, b:b + 1],
                                          ALU.subtract, ALU.mult).then_inc(own, 1)
                    counted = 3 * BATCHES
                    dve.wait_ge(own, counted)
                statistics(counted)
                if weight is None:
                    dve.tensor_scalar(var[:, :], mv[:, :, 1], eps, None, ALU.add).then_inc(var_ready, 1)
                else:
                    dve.tensor_tensor(var[:, :], mv[:, :, 0], mv[:, :, 0], ALU.mult).then_inc(own, 1)
                    dve.wait_ge(own, counted + 2 * BATCHES + 1)
                    dve.scalar_tensor_tensor(var[:, :], var[:, :], eps, mv[:, :, 1], ALU.add, ALU.add)\
                       .then_inc(var_ready, 1)
                    dve.wait_ge(ld, 16)
                dve.wait_ge(rstd_ready, ROUNDS)

                def normalise(b):
                    if weight is None:
                        dve.tensor_scalar(xn[:, b, :], x_sb[:, b, :], mv[:, b, 0:1], rstd[:, b:b + 1],
                                          ALU.subtract, ALU.mult).then_inc(xn_ready, 1)
                    else:
                        dve.scalar_tensor_tensor(xn[:, b, :], x_sb[:, b, :], rstd[:, b:b + 1], wb[:, :],
                                                 ALU.mult, ALU.mult).then_inc(xn_ready, 1)

                for b in range(4):
                    normalise(b)
                for m in range(PAIRS):
                    if m < PAIRS - 2:
                        normalise(2 * m + 4)
                        normalise(2 * m + 5)
                    dve.wait_ge(hi_ready, m + 1)
                    cols = slice(2 * P * m, 2 * P * m + 2 * P)
                    dve.tensor_tensor(xTl[:, :, cols], turned[m % 4][:, :, :, :].rearrange("p k b t -> p k (b t)"),
                                      xTh[:, :, cols].bitcast(F32), ALU.subtract).then_inc(lo_ready, 1)


def row_norms(nc, ident, xn, xTh, xTl, cTh, cTl, rqs, nrqs, rkb, wT, ctx_sb, raw, loads, x_sb, ob, g):
    with ExitStack() as stack:
        s = Scope(nc, stack, "r")
        GW = DIM + 2
        ORDER = (1, 0)
        gh = s.sb("gh", [P, 2, KT, GW], F32R)
        gl = s.sb("gl", [P, 2, KT, GW], F32R)
        bsq = s.sb("bsq", [P, 2, HEADS])
        bsum = s.sb("bsum", [P, 2])
        onesq = s.sb("onesq", [P, P])
        half = s.sb("half", [P, 2, BATCHES])
        ssq = s.sb("ssq", [P, 2, BATCHES])
        xb = s.sb("xb", [P, 2, BATCHES])
        bb = s.sb("bb", [P, 2])
        ms = s.sb("ms", [P, 2, BATCHES])
        rr = s.sb("rr", [P, 2, BATCHES])
        junk = s.sb("junk", [P, DIM])
        diag = s.sb("diag", [P, 2, P])
        g_ps = [s.ps(f"g{k}", [P, GW]) for k in range(2)]
        bb_ps = s.ps("bb_ps", [P, 2])
        y_ps = [s.ps(f"y{k}", [P, GW]) for k in range(2)]
        b_ps = [s.ps(f"b{k}", [P, P]) for k in range(2)]

        ld_w, ld_c, ld_ct, ld_b = loads
        tg = s.sb("tg", [P, 1])
        tanh_ready, ob_ready, x_done = s.sem("tanh_ready"), s.sem("ob_ready"), s.sem("x_done")
        consts, own = s.sem("consts"), s.sem("own")
        g_psum, g_hi, g_lo = (s.sem(n) for n in ("g_psum", "g_hi", "g_lo"))
        bsum_ready, bb_psum = s.sem("bsum_ready"), s.sem("bb_psum")
        c_hi, c_lo = s.sem("c_hi"), s.sem("c_lo")
        y_psum, y_read, ms_ready, rr_ready = (s.sem(n) for n in ("y_psum", "y_read", "ms_ready", "rr_ready"))
        diag_ready, b_psum, rkb_ready = s.sem("diag_ready"), s.sem("b_psum"), s.sem("rkb_ready")

        with nc.Block() as block:

            @block.gpsimd
            def _(pool):
                pool.memset(half[:, :, :], -0.5).then_inc(consts, 1)
                pool.memset(onesq[:, :], 1.0).then_inc(consts, 1)
                pool.wait_ge(consts, 2)
                for m, w in enumerate(ORDER):
                    pool.wait_ge(ms_ready, m + 1)
                    pool.tensor_tensor(rr[:, w, :], ms[:, w, :], half[:, w, :], ALU.pow).then_inc(rr_ready, 1)

            @block.scalar
            def _(act):
                act.wait_ge(ld_b, 32)
                act.activation(tg[:, :], g[:, :], ACT.Tanh).then_inc(tanh_ready, 1)
                act.wait_ge(ld_ct, 16)
                act.activation(cTh[:, :, :], raw[:, :, :], ACT.Copy).then_inc(c_hi, 1)
                for n, w in enumerate(ORDER):
                    for k in range(KT):
                        act.wait_ge(g_psum, KT * n + k + 1)
                        act.activation(gh[:, w, k, :], g_ps[k][:, :], ACT.Copy).then_inc(g_hi, 1)
                for b in range(BATCHES):
                    act.wait_ge(b_psum, b + 1)
                    act.activation(rkb[:, b, :], b_ps[b % 2][:, :], ACT.Copy).then_inc(rkb_ready, 1)

            @block.tensor
            def _(pe):
                pe.wait_ge(consts, 2)
                pe.wait_ge(ld_w, 32)
                for n, w in enumerate(ORDER):
                    for k in range(KT):
                        after(pe, g_lo, KT * (n - 1) + k + 1)
                        for h in range(HEADS):
                            mm = pe.matmul(g_ps[k][:, :], wT[:, w, h, P * k:P * k + P], wT[:, w, h, :],
                                           start=(h == 0), stop=(h == HEADS - 1))
                        mm.then_inc(g_psum, 1)
                pe.wait_ge(bsum_ready, 1)
                pe.matmul(bb_ps[:, :], onesq[:, :], bsum[:, :], start=True, stop=True).then_inc(bb_psum, 1)
                n = 0
                for m, w in enumerate(ORDER):
                    th, tl = ((xTh, xTl), (cTh, cTl))[w]
                    pe.wait_ge(g_lo, KT * (m + 1))
                    if w == 1:
                        pe.wait_ge(c_lo, 1)
                    for b in range(BATCHES):
                        y = y_ps[n % 2]
                        cols = slice(P * b, P * b + P)
                        after(pe, y_read, 2 * (n - 1))
                        for k in range(KT):
                            pe.matmul(y[:, :], th[:, k, cols], gh[:, w, k, :], start=(k == 0), stop=False)
                            pe.matmul(y[:, :], th[:, k, cols], gl[:, w, k, :], start=False, stop=False)
                            mm = pe.matmul(y[:, :], tl[:, k, cols], gh[:, w, k, :], start=False, stop=(k == KT - 1))
                        mm.then_inc(y_psum, 1)
                        n += 1
                for b in range(BATCHES):
                    pe.wait_ge(diag_ready, b + 1)
                    after(pe, rkb_ready, b - 1)
                    pe.matmul(b_ps[b % 2][:, :], onesq[:, :], diag[:, b % 2, :], start=True, stop=True).then_inc(b_psum, 1)

            @block.vector
            def _(dve):
                dve.wait_ge(ld_w, 32)
                dve.tensor_tensor(bsq[:, :, :], wT[:, :, :, DIM], wT[:, :, :, DIM], ALU.mult).then_inc(own, 1)
                dve.wait_ge(own, 1)
                dve.tensor_reduce(bsum[:, :], bsq[:, :, :], AX.X, ALU.add).then_inc(bsum_ready, 1)
                dve.wait_ge(tanh_ready, 1)
                dve.tensor_scalar(ob[:, :], ob[:, :], tg[:, 0:1], None, ALU.mult).then_inc(ob_ready, 1)
                dve.wait_ge(ob_ready, 1)
                for b in range(BATCHES):
                    dve.tensor_tensor(x_sb[:, b, :], x_sb[:, b, :], ob[:, :], ALU.add).then_inc(x_done, 1)
                dve.wait_ge(c_hi, 1)
                dve.tensor_tensor(cTl[:, :, :], raw[:, :, :], cTh[:, :, :].bitcast(F32), ALU.subtract).then_inc(c_lo, 1)
                for m, w in enumerate(ORDER):
                    for k in range(KT):
                        dve.wait_ge(g_hi, KT * m + k + 1)
                        dve.tensor_tensor(gl[:, w, k, :], g_ps[k][:, :], gh[:, w, k, :].bitcast(F32), ALU.subtract)\
                           .then_inc(g_lo, 1)
                dve.wait_ge(bb_psum, 1)
                dve.tensor_copy(bb[:, :], bb_ps[:, :]).then_inc(own, 1)
                dve.wait_ge(ld_c, 16)
                for m, w in enumerate(ORDER):
                    t = (xn, ctx_sb)[w]
                    for b in range(BATCHES):
                        n = m * BATCHES + b
                        dve.wait_ge(y_psum, n + 1)
                        after(dve, y_read, 2 * n)
                        dve.tensor_tensor_reduce(junk[:, :], y_ps[n % 2][:, 0:DIM], t[:, b, :], 1.0, 0.0, ALU.mult,
                                                 ALU.add, ssq[:, w, b:b + 1]).then_inc(y_read, 1)
                        dve.tensor_copy(xb[:, w, b:b + 1], y_ps[n % 2][:, DIM:DIM + 1]).then_inc(y_read, 1)
                    dve.wait_ge(y_read, 2 * BATCHES * (m + 1))
                    base = 2 + 3 * m
                    dve.scalar_tensor_tensor(ms[:, w, :], xb[:, w, :], 2.0, ssq[:, w, :], ALU.mult, ALU.add)\
                       .then_inc(own, 1)
                    dve.wait_ge(own, base + 1)
                    dve.tensor_scalar(ms[:, w, :], ms[:, w, :], bb[:, w:w + 1], None, ALU.add).then_inc(own, 1)
                    dve.wait_ge(own, base + 2)
                    dve.tensor_scalar(ms[:, w, :], ms[:, w, :], 1.0 / INNER, 0.0, ALU.mult, ALU.max).then_inc(own, 1)
                    dve.wait_ge(own, base + 3)
                    dve.tensor_scalar(ms[:, w, :], ms[:, w, :], 1e-6, None, ALU.add).then_inc(ms_ready, 1)
                dve.wait_ge(rr_ready, 1)
                for b in range(BATCHES):
                    after(dve, b_psum, b - 1)
                    dve.tensor_scalar(diag[:, b % 2, :], ident[:, :], rr[:, 1, b:b + 1], None, ALU.mult)\
                       .then_inc(diag_ready, 1)
                dve.wait_ge(rr_ready, 2)
                dve.tensor_scalar(rqs[:, :], rr[:, 0, :], float(HD) ** -0.5, None, ALU.mult).then_inc(own, 1)
                dve.tensor_scalar(nrqs[:, :], rr[:, 0, :], -float(HD) ** -0.5, None, ALU.mult).then_inc(own, 1)
                dve.wait_ge(own, 10)
                dve.wait_ge(x_done, BATCHES)


class QuadWeights:

    def __init__(self, nc, stack, tag, w, key_norm):
        s = Scope(nc, stack, tag)
        self.w, self.key_norm = w, key_norm
        self.qk = s.sb("raw_qk", [P, 2, KT, 4 * HD])
        self.vo = s.sb("raw_vo", [P, KT * 4 * HD])
        self.knorm = s.sb("knorm", [P, 2, 4 * HD]) if key_norm else None
        self.ld_qk, self.ld_v = s.sem("ld_qk"), s.sem("ld_v")

    def load_qk(self, sp, i):
        c = ds(i * 4 * HD, 4 * HD)
        for k in range(2):
            sp.dma_start(self.qk[:, k, :, :], self.w[k][:, :, c]).then_inc(self.ld_qk, 16)
            if self.key_norm:
                sp.dma_start(self.knorm[:, k, :], self.key_norm[k][:, c].broadcast_to([P, 4 * HD]))\
                  .then_inc(self.ld_qk, 16)

    def load_v(self, sp, i):
        c = ds(i * 4 * HD, 4 * HD)
        sp.dma_start(self.vo[:, :].rearrange("p (k c) -> p k c", k=KT), self.w[2][:, :, c]).then_inc(self.ld_v, 16)

    def fetch(self, sp):
        self.load_qk(sp, 0)
        self.load_v(sp, 0)


def attend_tokens(nc, tag, x_sb, ident, q_parts, kv_parts, first, cols, gate, rowmul, rqs, nrqs):
    normed = cols is not None
    QC = 4 * HD
    with ExitStack() as stack:
        s = Scope(nc, stack, tag)
        xTh, xTl = q_parts
        cTh, cTl = kv_parts
        raw_qk, raw_vo, knorm, ld_qk, ld_v = first.qk, first.vo, first.knorm, first.ld_qk, first.ld_v
        wqkv_h = s.sb("wqkv_h", [P, 3, KT, QC], F32R)
        wqkv_l = s.sb("wqkv_l", [P, 3, KT, QC], F32R)
        wo_h = s.sb("wo_h", [P, 4, DIM], F32R)
        wo_l = s.sb("wo_l", [P, 4, DIM], F32R)
        qk = s.sb("qk", [P, 2, 2, GT])
        v = s.sb("values", [P, 2, GB, QC])
        prob = s.sb("prob", [P, 2, GB, TOKENS])
        pT = s.sb("turned", [P, 2, GB, TOKENS])
        oT_h = s.sb("oT_h", [P, 2, GB, TOKENS], F32R)
        oT_l = s.sb("oT_l", [P, 2, GB, TOKENS], F32R)
        mx = s.sb("mx", [P, 2, GB])
        nb = s.sb("nb", [P, 2, GB])
        sums = s.sb("sums", [P, 2, GB])
        rsum = s.sb("rsum", [P, 2, GB])
        if normed:
            allb = s.sb("allb", [P, 5, HEADS])
            bqk = s.sb("bqk", [P, 2, 4])
            bv = s.sb("bv", [P, 4])
            g = s.sb("g", [P, 1])
            tg = s.sb("tg", [P, 1])
        qk_ps = [s.ps(f"qk{k}", [P, GT]) for k in range(2)]
        v_ps = s.ps("v", [P, QC])
        s_ps = s.ps("s", [P, GB, TOKENS])
        pT_ps = s.ps("pT", [P, GB, TOKENS])
        oT_ps = s.ps("oT", [P, GB, TOKENS])
        acc = s.ps("acc", [P, GB, DIM])

        ld_o, ld_b = s.sem("ld_o"), s.sem("ld_b")
        bias_copied, half_scaled, tanh_ready = s.sem("bias_copied"), s.sem("half_scaled"), s.sem("tanh_ready")
        kw_scaled, ow_scaled = s.sem("kw_scaled"), s.sem("ow_scaled")
        wqk_hi, wqk_lo, wv_hi, wv_lo, wo_hi, wo_lo = (
            s.sem(n) for n in ("wqk_hi", "wqk_lo", "wv_hi", "wv_lo", "wo_hi", "wo_lo"))
        qk_psum, q_ready, k_ready = (s.sem(n) for n in ("qk_psum", "q_ready", "k_ready"))
        v_psum, v_ready = s.sem("v_psum"), s.sem("v_ready")
        s_psum, s_read, mx_ready, nb_ready = (s.sem(n) for n in ("s_psum", "s_read", "mx_ready", "nb_ready"))
        exp_ready, rsum_ready, prob_ready = (s.sem(n) for n in ("exp_ready", "rsum_ready", "prob_ready"))
        pT_psum, pT_ready = s.sem("pT_psum"), s.sem("pT_ready")
        oT_psum, oT_hi, oT_lo = (s.sem(n) for n in ("oT_psum", "oT_hi", "oT_lo"))
        acc_psum, x_added = s.sem("acc_psum"), s.sem("x_added")

        def quads(eng, body):
            body(0)
            with eng.Fori(1, QUADS - 1) as i:
                body(i)
            body(QUADS - 1)

        def known(t):
            return not isinstance(t, int) or 0 <= t < UNITS * QUADS

        def v_turns(k, last):
            if k == 14:
                return []
            turns = [divmod(n + 2, GB) for n in ((14, 15) if k == 15 else (k,))]
            return [(g, b) for g, b in turns if not (last and g == GROUPS)]

        def v_count(i, g, b):
            return (i * 4 + g) * 4 + b + 1

        with nc.Block() as block:

            @block.sync
            def _(sp):
                if normed:
                    sp.dma_start(allb[:, :, :], cols).then_inc(ld_b, 16)
                    sp.dma_start(g[:, :], gate.broadcast_to([P, 1])).then_inc(ld_b, 16)

                def load(i):
                    if not isinstance(i, int):
                        sp.wait_ge(wqk_lo, i * 4)
                        first.load_qk(sp, i)
                        sp.wait_ge(wo_lo, i * 4)
                        first.load_v(sp, i)
                    sp.wait_ge(wv_lo, i + 1)
                    sp.dma_start(raw_vo[:, :].rearrange("p (h c) -> p h c", h=4), first.w[3][:, ds(i * 4, 4), :])\
                      .then_inc(ld_o, 16)

                load(0)
                with sp.Fori(1, QUADS) as i:
                    load(i)

            def split_qk_turn(i, k):
                if k == 0 and not (isinstance(i, int) and i == 0):
                    return i, 3
                if k in (12, 13, 15) and not (isinstance(i, int) and i == QUADS - 1):
                    return i + 1, {12: 0, 13: 1, 15: 2}[k]
                return None

            def split_o_turn(k):
                return k - 1 if 1 <= k <= 4 else None

            LD_QK = 64 if normed else 32

            @block.scalar
            def _(act):
                if normed:
                    act.wait_ge(ld_b, 32)
                    act.activation(tg[:, :], g[:, :], ACT.Tanh).then_inc(tanh_ready, 1)

                def split_qk(i, h):
                    if normed:
                        act.wait_ge(kw_scaled, i * 4 + h + 1)
                    else:
                        act.wait_ge(ld_qk, LD_QK * (i + 1))
                    after(act, qk_psum, 2 * (i * 16 - 4 + h + 1))
                    c = slice(HD * h, HD * h + HD)
                    act.activation(wqkv_h[:, 0:2, :, c], raw_qk[:, :, :, c], ACT.Copy).then_inc(wqk_hi, 1)

                def split_v(i):
                    act.wait_ge(ld_v, 16 * (i + 1))
                    after(act, v_psum, i * 16)
                    act.activation(wqkv_h[:, 2, :, :], raw_vo[:, :].rearrange("p (k c) -> p k c", k=KT), ACT.Copy)\
                        .then_inc(wv_hi, 1)

                def split_o(i, h):
                    if normed:
                        act.wait_ge(ow_scaled, i * 4 + h + 1)
                    else:
                        act.wait_ge(ld_o, 16 * (i + 1))
                    after(act, acc_psum, i * 16 - 4 + h + 1)
                    act.activation(wo_h[:, h, :], raw_vo[:, DIM * h:DIM * h + DIM], ACT.Copy).then_inc(wo_hi, 1)

                def copy_k(t, h):
                    act.wait_ge(qk_psum, 2 * t + 2)
                    after(act, s_psum, t - 1)
                    o, i_ = qk[:, h % 2, 1, :], qk_ps[1][:, :]
                    if normed:
                        ins = act.activation(o, i_, ACT.Identity, bias=bqk[:, 1, h:h + 1])
                    else:
                        ins = act.activation(o, i_, ACT.Copy)
                    ins.then_inc(k_ready, 1)

                def exponentials(t, k):
                    g_, p = k // 4, k % 2
                    act.wait_ge(nb_ready, t + 1)
                    for b in range(GB):
                        r = GB * g_ + b
                        ins = act.activation(prob[:, p, b, :], prob[:, p, b, :], ACT.Exp, bias=nb[:, p, b:b + 1],
                                             scale=rqs[:, r:r + 1], accum_out=sums[:, p, b:b + 1])
                    ins.then_inc(exp_ready, 1)

                def copy_pT(t, k):
                    act.wait_ge(pT_psum, t + 1)
                    after(act, oT_psum, t - 1)
                    act.activation(pT[:, k % 2, :, :], pT_ps[:, :, :], ACT.Copy).then_inc(pT_ready, 1)

                def round_oT(t, k):
                    act.wait_ge(oT_psum, t + 1)
                    after(act, acc_psum, t - 1)
                    if normed:
                        ins = act.activation(oT_h[:, k % 2, :, :], oT_ps[:, :, :], ACT.Identity,
                                             bias=bv[:, k % 4:k % 4 + 1])
                    else:
                        ins = act.activation(oT_h[:, k % 2, :, :], oT_ps[:, :, :], ACT.Copy)
                    ins.then_inc(oT_hi, 1)

                def body(i):
                    last = isinstance(i, int) and i == QUADS - 1
                    for k in range(16):
                        t = i * 16 + k
                        if k == 14 and not last:
                            split_v(i + 1)
                        exponentials(t, k)
                        if known(t + 1):
                            copy_k(t + 1, (k + 1) % 4)
                        if known(t - 1):
                            copy_pT(t - 1, k - 1)
                        if known(t - 2):
                            round_oT(t - 2, k - 2)
                        if split_o_turn(k) is not None:
                            split_o(i, split_o_turn(k))
                        if split_qk_turn(i, k):
                            split_qk(*split_qk_turn(i, k))

                split_v(0)
                for h in range(4):
                    split_qk(0, h)
                copy_k(0, 0)
                quads(act, body)
                n = 16 * QUADS
                copy_pT(n - 1, 15)
                round_oT(n - 2, 14)
                round_oT(n - 1, 15)

            @block.gpsimd
            def _(pool):
                def split_v(i):
                    pool.wait_ge(wv_hi, i + 1)
                    pool.tensor_tensor(wqkv_l[:, 2, :, :], raw_vo[:, :].rearrange("p (k c) -> p k c", k=KT),
                                       wqkv_h[:, 2, :, :].bitcast(F32), ALU.subtract).then_inc(wv_lo, 1)

                def body(i):
                    for k in range(16):
                        t = i * 16 + k
                        if k == 14 and not (isinstance(i, int) and i == QUADS - 1):
                            split_v(i + 1)
                        pool.wait_ge(rsum_ready, t + 1)
                        pool.tensor_tensor(prob[:, k % 2, :, :], prob[:, k % 2, :, :],
                                           rsum[:, k % 2, :].unsqueeze(2).broadcast_to([P, GB, TOKENS]), ALU.mult)\
                            .then_inc(prob_ready, 1)

                split_v(0)
                quads(pool, body)

            @block.tensor
            def _(pe):
                def product(out, ah, al, bh, bl, start, stop):
                    pe.matmul(out, ah, bh, start=start, stop=False)
                    pe.matmul(out, ah, bl, start=False, stop=False)
                    return pe.matmul(out, al, bh, start=False, stop=stop)

                def project_qk(t, g_, h, k):
                    th, tl = ((xTh, xTl), (cTh, cTl))[k]
                    after(pe, (q_ready, k_ready)[k], t)
                    c, tok = slice(HD * h, HD * h + HD), slice(GT * g_, GT * g_ + GT)
                    for kt in range(KT):
                        mm = product(qk_ps[k][:, :], wqkv_h[:, k, kt, c], wqkv_l[:, k, kt, c],
                                     th[:, kt, tok], tl[:, kt, tok], kt == 0, kt == KT - 1)
                    mm.then_inc(qk_psum, 1)

                def project_v(n, g_, b):
                    after(pe, v_ready, n - 1)
                    tok = slice(P * (GB * g_ + b), P * (GB * g_ + b) + P)
                    for kt in range(KT):
                        mm = product(v_ps[:, :], cTh[:, kt, tok], cTl[:, kt, tok], wqkv_h[:, 2, kt, :],
                                     wqkv_l[:, 2, kt, :], kt == 0, kt == KT - 1)
                    mm.then_inc(v_psum, 1)

                def scores(t, k):
                    pe.wait_ge(q_ready, t + 1)
                    pe.wait_ge(k_ready, t + 1)
                    after(pe, s_read, t)
                    p = k % 2
                    for b in range(GB):
                        tok = slice(P * b, P * b + P)
                        mm = pe.matmul(s_ps[:, b, :], qk[:, p, 0, tok], qk[:, p, 1, tok], start=True, stop=True)
                    mm.then_inc(s_psum, 1)

                def turn_probs(t, k):
                    pe.wait_ge(prob_ready, t + 1)
                    after(pe, pT_ready, t)
                    for b in range(GB):
                        mm = pe.transpose(pT_ps[:, b, :], prob[:, k % 2, b, :], ident[:, :])
                    mm.then_inc(pT_psum, 1)

                def weigh(t, k):
                    g_, h, p = (k // 4) % 4, k % 4, k % 2
                    pe.wait_ge(pT_ready, t + 1)
                    if h == 0:
                        pe.wait_ge(v_ready, t + 4)
                    after(pe, oT_lo, t)
                    c = slice(HD * h, HD * h + HD)
                    for b in range(GB):
                        mm = pe.matmul(oT_ps[:, b, :], v[:, g_ % 2, b, c], pT[:, p, b, :], start=True, stop=True)
                    mm.then_inc(oT_psum, 1)

                def body(i):
                    last = isinstance(i, int) and i == QUADS - 1
                    for k in range(16):
                        t = i * 16 + k
                        g1, h1 = ((k + 1) // 4) % 4, (k + 1) % 4
                        scores(t, k)
                        for g_, b in v_turns(k, last)[:-1]:
                            pe.wait_ge(wv_lo, i + 2)
                            project_v(v_count(i, g_, b), g_ % GROUPS, b)
                        if known(t + 1):
                            if k == 15:
                                pe.wait_ge(wqk_lo, i * 4 + 5)
                            elif g1 == 0:
                                pe.wait_ge(wqk_lo, i * 4 + h1 + 1)
                            project_qk(t + 1, g1, h1, 0)
                        if known(t + 1):
                            project_qk(t + 1, g1, h1, 1)
                        if known(t - 1):
                            turn_probs(t - 1, k - 1)
                        if known(t - 2):
                            weigh(t - 2, k - 2)
                        for g_, b in v_turns(k, last)[-1:]:
                            project_v(v_count(i, g_, b), g_ % GROUPS, b)
                        if known(t - 3):
                            out_turn(i, k)

                def out_turn(i, k):
                    t, h, p = i * 16 + (k - 3), (k - 3) % 4, (k - 3) % 2
                    pe.wait_ge(oT_lo, t + 1)
                    if h == 0:
                        after(pe, x_added, i * 4 + (k - 3) // 4)
                    if 3 <= k < 7:
                        pe.wait_ge(wo_lo, i * 4 + h + 1)
                    for b in range(GB):
                        ah, al, bh, bl = oT_h[:, p, b, :], oT_l[:, p, b, :], wo_h[:, h, :], wo_l[:, h, :]
                        pe.matmul(acc[:, b, :], ah, bh, start=(h == 0 and b % 2 == 0), stop=False, skip_group_check=True)
                        pe.matmul(acc[:, b, :], ah, bl, start=False, stop=False, skip_group_check=True)
                        mm = pe.matmul(acc[:, b, :], al, bh, start=False, stop=(h == 3), skip_group_check=True)
                    mm.then_inc(acc_psum, 1)

                pe.wait_ge(wv_lo, 1)
                pe.wait_ge(wqk_lo, 1)
                project_qk(0, 0, 0, 0)
                project_qk(0, 0, 0, 1)
                for b in range(2):
                    project_v(v_count(0, 0, b), 0, b)
                quads(pe, body)
                n = 16 * QUADS
                turn_probs(n - 1, 15)
                weigh(n - 2, 14)
                out_turn(QUADS, 0)
                weigh(n - 1, 15)
                out_turn(QUADS, 1)
                out_turn(QUADS, 2)

            @block.vector
            def _(dve):
                def copy_bias(i, h):
                    n = i * 4 + h
                    after(dve, q_ready, i * 16 - 4 + h + 1)
                    after(dve, k_ready, i * 16 - 4 + h + 1)
                    dve.tensor_scalar(bqk[:, 0, h:h + 1], allb[:, 0, ds(n, 1)], 1.0, None, ALU.mult)
                    dve.tensor_scalar(bqk[:, 1, h:h + 1], allb[:, 1, ds(n, 1)], allb[:, 3, ds(n, 1)],
                                      allb[:, 4, ds(n, 1)], ALU.mult, ALU.mult).then_inc(bias_copied, 1)

                def scale_k(i, h):
                    if h == 0:
                        dve.wait_ge(ld_qk, LD_QK * (i + 1))
                    c = slice(HD * h, HD * h + HD)
                    for n in range(2):
                        for kt in range(KT):
                            ins = dve.tensor_tensor(raw_qk[:, 1, kt, c], raw_qk[:, 1, kt, c], knorm[:, n, c], ALU.mult)
                            if n == 0:
                                ins.then_inc(half_scaled, 1)
                        if n == 0:
                            dve.wait_ge(half_scaled, i * 8 + 2 * h + 2)
                    ins.then_inc(kw_scaled, 1)

                def split_qk(i, h):
                    dve.wait_ge(wqk_hi, i * 4 + h + 1)
                    c = slice(HD * h, HD * h + HD)
                    for kt in range(KT):
                        ins = dve.tensor_tensor(wqkv_l[:, 0:2, kt, c], raw_qk[:, :, kt, c],
                                                wqkv_h[:, 0:2, kt, c].bitcast(F32), ALU.subtract)
                    ins.then_inc(wqk_lo, 1)

                def prepare_qk(i, h):
                    if normed:
                        copy_bias(i, h)
                    split_qk(i, h)

                def split_o(i, h):
                    c = slice(DIM * h, DIM * h + DIM)
                    if normed:
                        dve.wait_ge(ld_o, 16 * (i + 1))
                        after(dve, oT_lo, i * 16 - 4 + h + 1)
                        dve.tensor_scalar(bv[:, h:h + 1], allb[:, 2, ds(i * 4 + h, 1)], 1.0, None, ALU.mult)
                        dve.tensor_scalar(raw_vo[:, c], raw_vo[:, c], tg[:, 0:1], None, ALU.mult).then_inc(ow_scaled, 1)
                    dve.wait_ge(wo_hi, i * 4 + h + 1)
                    dve.tensor_tensor(wo_l[:, h, :], raw_vo[:, c], wo_h[:, h, :].bitcast(F32), ALU.subtract)\
                       .then_inc(wo_lo, 1)

                def copy_q(t, h):
                    dve.wait_ge(qk_psum, 2 * t + 1)
                    after(dve, s_psum, t - 1)
                    if normed:
                        ins = dve.tensor_scalar(qk[:, h % 2, 0, :], qk_ps[0][:, :], bqk[:, 0, h:h + 1], None, ALU.add)
                    else:
                        ins = dve.tensor_copy(qk[:, h % 2, 0, :], qk_ps[0][:, :])
                    ins.then_inc(q_ready, 1)

                def copy_v(n, g_, b):
                    dve.wait_ge(v_psum, n)
                    after(dve, oT_psum, (n - b - 1) - 4)
                    dve.tensor_copy(v[:, g_ % 2, b, :], v_ps[:, :]).then_inc(v_ready, 1)

                def shift(t, k):
                    g_, p = k // 4, k % 2
                    dve.wait_ge(s_psum, t + 1)
                    after(dve, pT_psum, t - 1)
                    m = rowmul[:, GB * g_:GB * g_ + GB, :] if normed else rowmul[:, :, :]
                    dve.tensor_tensor(prob[:, p, :, :], s_ps[:, :, :], m, ALU.mult if normed else ALU.add)\
                       .then_inc(s_read, 1)
                    dve.wait_ge(s_read, t + 1)
                    dve.tensor_reduce(mx[:, p, :], prob[:, p, :, :], AX.X, ALU.max).then_inc(mx_ready, 1)
                    dve.wait_ge(mx_ready, t + 1)
                    dve.tensor_tensor(nb[:, p, :], mx[:, p, :], nrqs[:, GB * g_:GB * g_ + GB], ALU.mult)\
                       .then_inc(nb_ready, 1)

                def invert_sums(t, k):
                    dve.wait_ge(exp_ready, t + 1)
                    dve.reciprocal(rsum[:, k % 2, :], sums[:, k % 2, :]).then_inc(rsum_ready, 1)

                def rest_oT(t, k):
                    dve.wait_ge(oT_hi, t + 1)
                    o, i_, hi = oT_l[:, k % 2, :, :], oT_ps[:, :, :], oT_h[:, k % 2, :, :].bitcast(F32)
                    if normed:
                        ins = dve.scalar_tensor_tensor(o, i_, bv[:, k % 4:k % 4 + 1], hi, ALU.add, ALU.subtract)
                    else:
                        ins = dve.tensor_tensor(o, i_, hi, ALU.subtract)
                    ins.then_inc(oT_lo, 1)

                def add_group(i, k):
                    g_ = ((k - 3) // 4) % 4
                    dve.wait_ge(acc_psum, i * 16 + (k - 3) + 1)
                    b = slice(GB * g_, GB * g_ + GB)
                    dve.tensor_tensor(x_sb[:, b, :], x_sb[:, b, :], acc[:, :, :], ALU.add).then_inc(x_added, 1)

                def body(i):
                    last = isinstance(i, int) and i == QUADS - 1
                    for k in range(16):
                        t = i * 16 + k
                        shift(t, k)
                        for g_, b in v_turns(k, last)[:-1]:
                            copy_v(v_count(i, g_, b), g_, b)
                        if known(t + 1):
                            copy_q(t + 1, (k + 1) % 4)
                        invert_sums(t, k)
                        if known(t - 2):
                            rest_oT(t - 2, k - 2)
                        if split_o_turn(k) is not None:
                            split_o(i, split_o_turn(k))
                        for g_, b in v_turns(k, last)[-1:]:
                            copy_v(v_count(i, g_, b), g_, b)
                        if k % 4 == 2 and known(t - 3):
                            add_group(i, k)
                        if normed and 8 <= k < 12 and not last:
                            scale_k(i + 1, k - 8)
                        if split_qk_turn(i, k):
                            prepare_qk(*split_qk_turn(i, k))

                if normed:
                    dve.wait_ge(ld_b, 32)
                    dve.wait_ge(tanh_ready, 1)
                for h in range(4):
                    if normed:
                        scale_k(0, h)
                    prepare_qk(0, h)
                copy_q(0, 0)
                for b in range(2):
                    copy_v(v_count(0, 0, b), 0, b)
                quads(dve, body)
                n = 16 * QUADS
                rest_oT(n - 2, 14)
                rest_oT(n - 1, 15)
                add_group(QUADS, 2)
                dve.wait_ge(x_added, GROUPS * QUADS)


def text_free_attention(nc, res, ctx_in, ctxT, wqT, wkT, w, cols, key_norm, out_b, gate):
    x_sb, ident = res["x"], res["ident"]
    with ExitStack() as stack:
        s = Scope(nc, stack, "c")
        xTh = s.sb("xTh", [P, KT, BATCHES * TOKENS], F32R)
        xTl = s.sb("xTl", [P, KT, BATCHES * TOKENS], F32R)
        cTh = s.sb("cTh", [P, KT, BATCHES * TOKENS], F32R)
        cTl = s.sb("cTl", [P, KT, BATCHES * TOKENS], F32R)
        rkb = s.sb("rkb", [P, BATCHES, TOKENS])
        rqs = s.sb("rqs", [P, BATCHES])
        nrqs = s.sb("nrqs", [P, BATCHES])
        first = QuadWeights(nc, stack, "cw", w, key_norm)
        with ExitStack() as inner:
            i = Scope(nc, inner, "ci")
            xn = i.sb("xn", [P, BATCHES, DIM])
            wT = i.sb("wT", [P, 2, HEADS, DIM + 2])
            ctx_sb = i.sb("ctx", [P, BATCHES, DIM])
            raw = i.sb("raw", [P, KT, BATCHES * TOKENS])
            ob = i.sb("ob", [P, DIM])
            g = i.sb("g", [P, 1])
            loads = ld_w, ld_c, ld_ct, ld_b = i.sem("ld_w"), i.sem("ld_c"), i.sem("ld_ct"), i.sem("ld_b")

            def fetch(sp):
                sp.dma_start(wT[:, 0, :, :], wqT).then_inc(ld_w, 16)
                sp.dma_start(wT[:, 1, :, :], wkT).then_inc(ld_w, 16)
                sp.dma_start(raw[:, :, :], ctxT).then_inc(ld_ct, 16)
                sp.dma_start(ctx_sb[:, :, :], ctx_in.rearrange("b p n -> p b n")).then_inc(ld_c, 16)
                sp.dma_start(ob[:, :], out_b.broadcast_to([P, DIM])).then_inc(ld_b, 16)
                sp.dma_start(g[:, :], gate.broadcast_to([P, 1])).then_inc(ld_b, 16)
                first.fetch(sp)

            prepare_tokens(nc, x_sb, ident, xn, xTh, xTl, 1e-5, fetch=fetch)
            row_norms(nc, ident, xn, xTh, xTl, cTh, cTl, rqs, nrqs, rkb, wT, ctx_sb, raw, loads,
                      x_sb, ob, g)
        attend_tokens(nc, "ca", x_sb, ident, (xTh, xTl), (cTh, cTl), first, cols, gate, rkb, rqs, nrqs)

EXPERTS, EXPERT_HID, SHARED_HID, TOPK = 16, 176, 352, 4
M_TILES = -(-(EXPERTS * EXPERT_HID + SHARED_HID) // P)
CHUNKS = 5
CT = M_TILES // CHUNKS
KINDS = EXPERTS + 1
LO, W_ROWS = 32, 64
M_UNITS = GROUPS * CT
QHD = 192


def route(nc, ident, xTh, xTl, gate_w, wT):
    PAD = EXPERTS + 4
    with ExitStack() as stack:
        s = Scope(nc, stack, "e")
        raw = s.sb("raw", [P, KT, EXPERTS])
        gw = s.sb("gw", [P, KT, 2, EXPERTS], F32R)
        logits = s.sb("logits", [P, BATCHES, EXPERTS])
        mx = s.sb("mx", [P, BATCHES])
        sh = s.sb("sh", [P, BATCHES, EXPERTS])
        e = s.sb("e", [P, BATCHES, PAD])
        top = s.sb("top", [P, BATCHES, 8])
        rep = s.sb("rep", [P, BATCHES, PAD])
        den = s.sb("den", [P, BATCHES])
        rden = s.sb("rden", [P, BATCHES])
        sel = s.sb("sel", [P, BATCHES, EXPERTS])
        weight = s.sb("weight", [P, BATCHES, W_ROWS])
        l_ps = s.ps("l", [P, BATCHES, 2, EXPERTS])
        t_ps = [s.ps(f"t{k}", [W_ROWS, GT]) for k in range(GROUPS)]
        ld, g_hi, g_lo, l_psum = s.sem("ld"), s.sem("g_hi"), s.sem("g_lo"), s.sem("l_psum")
        consts, own, shifted, exp_ready = s.sem("consts"), s.sem("own"), s.sem("shifted"), s.sem("exp_ready")
        weight_ready, t_psum, t_hi, t_lo = s.sem("weight_ready"), s.sem("t_psum"), s.sem("t_hi"), s.sem("t_lo")
        with nc.Block() as block:

            @block.sync
            def _(sp):
                sp.dma_start(raw[:, :, :], gate_w).then_inc(ld, 16)

            @block.gpsimd
            def _(pool):
                pool.memset(e[:, :, EXPERTS:PAD], -1.0).then_inc(consts, 1)
                for a in (0, LO):
                    pool.memset(weight[:, :, a + EXPERTS:a + KINDS], 1.0).then_inc(consts, 1)
                    pool.memset(weight[:, :, a + KINDS:a + LO], 0.0).then_inc(consts, 1)

            @block.scalar
            def _(act):
                act.wait_ge(ld, 16)
                act.activation(gw[:, :, 0, :], raw[:, :, :], ACT.Copy).then_inc(g_hi, 1)
                act.wait_ge(shifted, 1)
                act.activation(e[:, :, 0:EXPERTS], sh[:, :, :], ACT.Exp).then_inc(exp_ready, 1)
                for g in range(GROUPS):
                    act.wait_ge(t_psum, g + 1)
                    act.activation(wT[:, GT * g:GT * g + GT], t_ps[g][:, :], ACT.Copy).then_inc(t_hi, 1)

            @block.tensor
            def _(pe):
                pe.wait_ge(g_lo, 1)
                for b in range(BATCHES):
                    tok = slice(P * b, P * b + P)
                    for k in range(KT):
                        pe.matmul(l_ps[:, b, :, :], xTh[:, k, tok], gw[:, k, :, :], start=(k == 0), stop=False)
                        mm = pe.matmul(l_ps[:, b, :, :], xTl[:, k, tok], gw[:, k, :, :], start=False,
                                       stop=(k == KT - 1))
                mm.then_inc(l_psum, 1)
                pe.wait_ge(weight_ready, 2)
                for g in range(GROUPS):
                    for b in range(GB):
                        mm = pe.transpose(t_ps[g][:, P * b:P * b + P], weight[:, GB * g + b, :], ident[:, :])
                    mm.then_inc(t_psum, 1)

            @block.vector
            def _(dve):
                count = [0]

                def chained(ins):
                    count[0] += 1
                    ins.then_inc(own, 1)
                    dve.wait_ge(own, count[0])

                dve.wait_ge(g_hi, 1)
                dve.tensor_tensor(gw[:, :, 1, :], raw[:, :, :], gw[:, :, 0, :].bitcast(F32), ALU.subtract)\
                   .then_inc(g_lo, 1)
                dve.wait_ge(l_psum, 1)
                chained(dve.tensor_copy(logits[:, :, :], l_ps[:, :, 0, :]))
                chained(dve.tensor_tensor(logits[:, :, :], logits[:, :, :], l_ps[:, :, 1, :], ALU.add))
                chained(dve.tensor_reduce(mx[:, :], logits[:, :, :], AX.X, ALU.max))
                dve.tensor_tensor(sh[:, :, :], logits[:, :, :], mx[:, :].unsqueeze(2).broadcast_to([P, BATCHES, EXPERTS]),
                                  ALU.subtract).then_inc(shifted, 1)
                dve.wait_ge(exp_ready, 1)
                dve.wait_ge(consts, 5)
                for b in range(BATCHES):
                    ins = dve.max(top[:, b, :], e[:, b, 0:EXPERTS])
                chained(ins)
                chained(dve.tensor_reduce(den[:, :], top[:, :, 0:TOPK], AX.X, ALU.add))
                chained(dve.memset(top[:, :, TOPK:8], -1.0))
                for b in range(BATCHES):
                    ins = dve.match_replace(rep[:, b, :], top[:, b, :], e[:, b, :], -2.0)
                chained(ins)
                chained(dve.reciprocal(rden[:, :], den[:, :]))
                chained(dve.scalar_tensor_tensor(sel[:, :, :], rep[:, :, 0:EXPERTS], -1.5, e[:, :, 0:EXPERTS],
                                                 ALU.is_lt, ALU.mult))
                for a in (0, LO):
                    dve.tensor_tensor(weight[:, :, a:a + EXPERTS], sel[:, :, :],
                                      rden[:, :].unsqueeze(2).broadcast_to([P, BATCHES, EXPERTS]), ALU.mult)\
                       .then_inc(weight_ready, 1)
                for g in range(GROUPS):
                    dve.wait_ge(t_hi, g + 1)
                    cols = slice(GT * g, GT * g + GT)
                    lo = slice(LO, W_ROWS)
                    dve.tensor_tensor(wT[lo, cols], t_ps[g][lo, :], wT[lo, cols].bitcast(F32), ALU.subtract)\
                       .then_inc(t_lo, 1)
                dve.wait_ge(t_lo, GROUPS)


class ChunkWeights:

    def __init__(self, nc, stack, gu_w, down_w, spread, before, gate):
        s = Scope(nc, stack, "mw")
        self.gu_w, self.down_w, self.spread, self.before, self.gate = gu_w, down_w, spread, before, gate
        self.gu = s.sb("raw_gu", [P, 2, KT, CT * P])
        self.d = s.sb("raw_d", [P, CT, DIM])
        self.s = s.sb("raw_s", [W_ROWS, CT * P])
        self.x0 = s.sb("x0", [P, BATCHES, DIM])
        self.g = s.sb("g", [P, 1])
        self.ld_gu, self.ld_d, self.ld_x = s.sem("ld_gu"), s.sem("ld_d"), s.sem("ld_x")

    def load_gu(self, sp, i):
        c = ds(i * CT * P, CT * P)
        for n in range(2):
            sp.dma_start(self.gu[:, n, :, :], self.gu_w[:, n, :, c]).then_inc(self.ld_gu, 16)
        sp.dma_start(self.s[:, :], self.spread[:, c]).then_inc(self.ld_gu, 16)

    def load_d(self, sp, i):
        sp.dma_start(self.d[:, :, :], self.down_w[:, ds(i * CT, CT), :]).then_inc(self.ld_d, 16)

    def fetch(self, sp):
        self.load_gu(sp, 0)
        self.load_d(sp, 0)
        sp.dma_start(self.x0[:, :, :], self.before.rearrange("b p n -> p b n")).then_inc(self.ld_x, 16)
        sp.dma_start(self.g[:, :], self.gate.broadcast_to([P, 1])).then_inc(self.ld_x, 16)


def experts(nc, x_sb, xTh, xTl, wT, first):
    with ExitStack() as stack:
        s = Scope(nc, stack, "m")
        CC = CT * P
        raw_gu, raw_d, raw_s, ld_gu, ld_d = first.gu, first.d, first.s, first.ld_gu, first.ld_d
        gu_h = s.sb("gu_h", [P, 2, KT, CC], F32R)
        gu_l = s.sb("gu_l", [P, 2, KT, CC], F32R)
        d_h = s.sb("d_h", [P, CT, DIM], F32R)
        d_l = s.sb("d_l", [P, CT, DIM], F32R)
        sp_h = s.sb("sp_h", [W_ROWS, CC], F32R)
        silu = s.sb("silu", [P, 2, GT])
        prod = s.sb("prod", [P, 2, GT])
        hid = s.sb("hid", [P, 2, GT])
        hid_h = s.sb("hid_h", [P, 2, GT], F32R)
        hid_l = s.sb("hid_l", [P, 2, GT], F32R)
        g_ps = [s.ps(f"g{k}", [P, GT]) for k in range(2)]
        u_ps = [s.ps(f"u{k}", [P, GT]) for k in range(2)]
        w_ps = [s.ps(f"w{k}", [P, GT]) for k in range(2)]
        acc = s.ps("acc", [P, GB, DIM])
        gu_hi, gu_lo, d_hi, d_lo = s.sem("gu_hi"), s.sem("gu_lo"), s.sem("d_hi"), s.sem("d_lo")
        g_psum, u_psum, w_psum = s.sem("g_psum"), s.sem("u_psum"), s.sem("w_psum")
        silu_ready, prod_ready, hid_ready = s.sem("silu_ready"), s.sem("prod_ready"), s.sem("hid_ready")
        hid_hi, hid_lo, acc_psum, x_added = s.sem("hid_hi"), s.sem("hid_lo"), s.sem("acc_psum"), s.sem("x_added")

        def chunks(eng, body):
            body(0)
            with eng.Fori(1, CHUNKS - 1) as i:
                body(i)
            body(CHUNKS - 1)

        def gu_turn(i, k):
            if k == 0 and not (isinstance(i, int) and i == 0):
                return i, 4
            if k >= 16 and not (isinstance(i, int) and i == CHUNKS - 1):
                return i + 1, k - 16
            return None

        def d_turn(i, k):
            if k < 3 and not (isinstance(i, int) and i == 0):
                return i, k + 2
            if k >= 18 and not (isinstance(i, int) and i == CHUNKS - 1):
                return i + 1, k - 18
            return None

        def known(t):
            return not isinstance(t, int) or t >= 0

        with nc.Block() as block:

            @block.sync
            def _(sp):
                with sp.Fori(1, CHUNKS) as i:
                    sp.wait_ge(gu_lo, i * CT)
                    first.load_gu(sp, i)
                    sp.wait_ge(d_lo, i * CT)
                    first.load_d(sp, i)

            @block.scalar
            def _(act):
                def split_gu(i, j):
                    act.wait_ge(ld_gu, 48 * (i + 1))
                    after(act, w_psum, i * M_UNITS - CT + j + 1)
                    c = slice(P * j, P * j + P)
                    act.activation(sp_h[:, c], raw_s[:, c], ACT.Copy).then_inc(gu_hi, 1)
                    for n in range(2):
                        ins = act.activation(gu_h[:, n, :, c], raw_gu[:, n, :, c], ACT.Copy)
                    ins.then_inc(gu_hi, 1)

                def split_d(i, j):
                    act.wait_ge(ld_d, 16 * (i + 1))
                    after(act, acc_psum, i * M_UNITS - CT + j + 1)
                    act.activation(d_h[:, j, :], raw_d[:, j, :], ACT.Copy).then_inc(d_hi, 1)

                def gates(t, k):
                    act.wait_ge(g_psum, t + 1)
                    after(act, prod_ready, t - 1)
                    act.activation(silu[:, k % 2, :], g_ps[k % 2][:, :], ACT.Silu).then_inc(silu_ready, 1)

                def round_hid(t, k):
                    act.wait_ge(hid_ready, t + 1)
                    after(act, acc_psum, t - 1)
                    act.activation(hid_h[:, k % 2, :], hid[:, k % 2, :], ACT.Copy).then_inc(hid_hi, 1)

                def body(i):
                    for k in range(M_UNITS):
                        t = i * M_UNITS + k
                        gates(t, k)
                        if gu_turn(i, k):
                            split_gu(*gu_turn(i, k))
                        if d_turn(i, k):
                            split_d(*d_turn(i, k))
                        if known(t - 1):
                            round_hid(t - 1, k - 1)

                for j in range(CT):
                    split_gu(0, j)
                for j in range(CT):
                    split_d(0, j)
                chunks(act, body)
                round_hid(CHUNKS * M_UNITS - 1, M_UNITS - 1)

            @block.tensor
            def _(pe):
                def gates_and_values(i, k):
                    t, (g_, j), p = i * M_UNITS + k, divmod(k, CT), k % 2
                    if g_ == 0:
                        pe.wait_ge(gu_lo, i * CT + j + 1)
                    c, tok = slice(P * j, P * j + P), slice(GT * g_, GT * g_ + GT)
                    for n, ps, free, done in ((0, g_ps, silu_ready, g_psum), (1, u_ps, prod_ready, u_psum)):
                        after(pe, free, t - 1)
                        for kt in range(KT):
                            h, l = gu_h[:, n, kt, c], gu_l[:, n, kt, c]
                            pe.matmul(ps[p][:, :], h, xTh[:, kt, tok], start=(kt == 0), stop=False)
                            pe.matmul(ps[p][:, :], h, xTl[:, kt, tok], start=False, stop=False)
                            mm = pe.matmul(ps[p][:, :], l, xTh[:, kt, tok], start=False, stop=(kt == KT - 1))
                        mm.then_inc(done, 1)
                    after(pe, hid_ready, t - 1)
                    pe.matmul(w_ps[p][:, :], sp_h[:, c], wT[:, tok], start=True, stop=True).then_inc(w_psum, 1)

                def down(i, k):
                    t, (g_, j), p = i * M_UNITS + k, divmod(k % M_UNITS, CT), k % 2
                    pe.wait_ge(hid_lo, t + 1)
                    if g_ == 0:
                        pe.wait_ge(d_lo, i * CT + j + 1)
                    if j == 0:
                        after(pe, x_added, i * GROUPS + g_)
                    for b in range(GB):
                        ah, al = (a[:, p, P * b:P * b + P] for a in (hid_h, hid_l))
                        pe.matmul(acc[:, b, :], ah, d_h[:, j, :], start=(j == 0 and b % 2 == 0), stop=False,
                                  skip_group_check=True)
                        pe.matmul(acc[:, b, :], ah, d_l[:, j, :], start=False, stop=False, skip_group_check=True)
                        mm = pe.matmul(acc[:, b, :], al, d_h[:, j, :], start=False, stop=(j == CT - 1),
                                       skip_group_check=True)
                    mm.then_inc(acc_psum, 1)

                def body(i):
                    for k in range(M_UNITS):
                        gates_and_values(i, k)
                        if known(i * M_UNITS + k - 2):
                            down(i, k - 2)

                chunks(pe, body)
                down(CHUNKS, -2)
                down(CHUNKS, -1)

            @block.vector
            def _(dve):
                def split_gu(i, j):
                    dve.wait_ge(gu_hi, 2 * (i * CT + j + 1))
                    c = slice(P * j, P * j + P)
                    for n in range(2):
                        ins = dve.tensor_tensor(gu_l[:, n, :, c], raw_gu[:, n, :, c], gu_h[:, n, :, c].bitcast(F32),
                                                ALU.subtract)
                    ins.then_inc(gu_lo, 1)

                def split_d(i, j):
                    dve.wait_ge(d_hi, i * CT + j + 1)
                    dve.tensor_tensor(d_l[:, j, :], raw_d[:, j, :], d_h[:, j, :].bitcast(F32), ALU.subtract)\
                       .then_inc(d_lo, 1)

                def hidden(t, k):
                    p = k % 2
                    dve.wait_ge(silu_ready, t + 1)
                    dve.wait_ge(u_psum, t + 1)
                    dve.tensor_tensor(prod[:, p, :], silu[:, p, :], u_ps[p][:, :], ALU.mult).then_inc(prod_ready, 1)
                    dve.wait_ge(prod_ready, t + 1)
                    dve.wait_ge(w_psum, t + 1)
                    dve.tensor_tensor(hid[:, p, :], prod[:, p, :], w_ps[p][:, :], ALU.mult).then_inc(hid_ready, 1)

                def rest_hid(t, k):
                    p = k % 2
                    dve.wait_ge(hid_hi, t + 1)
                    dve.tensor_tensor(hid_l[:, p, :], hid[:, p, :], hid_h[:, p, :].bitcast(F32), ALU.subtract)\
                       .then_inc(hid_lo, 1)

                def add_group(i, k):
                    g_ = (k % M_UNITS) // CT
                    dve.wait_ge(acc_psum, i * M_UNITS + k + 1)
                    b = slice(GB * g_, GB * g_ + GB)
                    dve.tensor_tensor(x_sb[:, b, :], x_sb[:, b, :], acc[:, :, :], ALU.add).then_inc(x_added, 1)

                def body(i):
                    for k in range(M_UNITS):
                        t = i * M_UNITS + k
                        if known(t - 1):
                            rest_hid(t - 1, k - 1)
                        if gu_turn(i, k):
                            split_gu(*gu_turn(i, k))
                        if d_turn(i, k):
                            split_d(*d_turn(i, k))
                        hidden(t, k)
                        if k % CT == 1 and known(t - 2):
                            add_group(i, k - 2)

                for j in range(CT):
                    split_gu(0, j)
                for j in range(CT):
                    split_d(0, j)
                chunks(dve, body)
                rest_hid(CHUNKS * M_UNITS - 1, M_UNITS - 1)
                add_group(CHUNKS, -1)
                dve.wait_ge(x_added, CHUNKS * GROUPS)


def expert_layer(nc, res, w, ln1, gate_w, ln2, gu_w, down_w, spread, gate, out):
    x_sb, ident = res["x"], res["ident"]
    before = nc.dram_tensor("x_before", (BATCHES, TOKENS, DIM), F32, kind="Internal").ap()
    with ExitStack() as stack:
        s = Scope(nc, stack, "d")
        xTh = s.sb("xTh", [P, KT, BATCHES * TOKENS], F32R)
        xTl = s.sb("xTl", [P, KT, BATCHES * TOKENS], F32R)
        scale = float(QHD) ** -0.5
        with ExitStack() as inner:
            s1 = Scope(nc, inner, "d1")
            causal = s1.sb("causal", [P, GB, TOKENS])
            rqs = s1.sb("rqs", [P, BATCHES])
            nrqs = s1.sb("nrqs", [P, BATCHES])
            saved, blank = s1.sem("saved"), s1.sem("blank")
            with nc.Block() as block:

                @block.sync
                def _(sp):
                    sp.dma_start(before.rearrange("b p n -> p b n"), x_sb[:, :, :]).then_inc(saved, 16)

                @block.gpsimd
                def _(pool):
                    pool.memset(causal[:, :, :], 0.0).then_inc(blank, 1)
                    pool.memset(rqs[:, :], scale).then_inc(blank, 1)
                    pool.memset(nrqs[:, :], -scale).then_inc(blank, 1)
                    pool.wait_ge(blank, 3)
                    pool.affine_select(out=causal[:, :, :], in_=causal[:, :, :], compare_op=ALU.is_ge,
                                       fill=-1.0e9 / scale, base=0, pattern=[[0, GB], [-1, TOKENS]],
                                       channel_multiplier=1).then_inc(blank, 1)

            first = QuadWeights(nc, inner, "dw", w, None)
            with nc.sbuf_tensor("d_xn1", [P, BATCHES, DIM], F32) as xn:
                prepare_tokens(nc, x_sb, ident, xn, xTh, xTl, 1e-6, ln1, centre=True, fetch=first.fetch,
                               saved=saved)
            attend_tokens(nc, "da", x_sb, ident, (xTh, xTl), (xTh, xTl), first, None, None, causal, rqs, nrqs)
        wT = s.sb("wT", [W_ROWS, BATCHES * TOKENS], F32R)
        yTh = s.sb("yTh", [P, KT, BATCHES * TOKENS], F32R)
        yTl = s.sb("yTl", [P, KT, BATCHES * TOKENS], F32R)
        first = ChunkWeights(nc, stack, gu_w, down_w, spread, before, gate)
        with nc.sbuf_tensor("d_xn2", [P, BATCHES, DIM], F32) as xn:
            prepare_tokens(nc, x_sb, ident, xn, yTh, yTl, 1e-6, ln2, fetch=first.fetch)
        route(nc, ident, yTh, yTl, gate_w, wT)
        experts(nc, x_sb, yTh, yTl, wT, first)
        finish(nc, x_sb, first, out)


def finish(nc, x_sb, first, out):
    with ExitStack() as stack:
        s = Scope(nc, stack, "f")
        x0, g = first.x0, first.g
        tg = s.sb("tg", [P, 1])
        tanh_ready, x_ready, sent = s.sem("tanh_ready"), s.sem("x_ready"), s.sem("sent")
        with nc.Block() as block:

            @block.sync
            def _(sp):
                for n in range(GROUPS):
                    b = slice(GB * n, GB * n + GB)
                    sp.wait_ge(x_ready, n + 1)
                    sp.dma_start(out[b].rearrange("b p n -> p b n"), x_sb[:, b, :]).then_inc(sent, 16)
                sp.wait_ge(sent, 16 * GROUPS)

            @block.scalar
            def _(act):
                act.wait_ge(first.ld_x, 32)
                act.activation(tg[:, :], g[:, :], ACT.Tanh).then_inc(tanh_ready, 1)

            @block.vector
            def _(dve):
                dve.wait_ge(tanh_ready, 1)
                for n in range(GROUPS):
                    b = slice(GB * n, GB * n + GB)
                    dve.scalar_tensor_tensor(x_sb[:, b, :], x_sb[:, b, :], tg[:, 0:1], x0[:, b, :], ALU.mult, ALU.add)\
                       .then_inc(x_ready, 1)


def gated_layers(nc, io, out):
    with ExitStack() as stack:
        res = make_resident(nc, stack, io)
        attend_channels(nc, res, io["x"], io["ctx"], io["mask"], io["maskT"], io["a_wq4"], io["a_wk4"], io["a_wv"],
                        io["a_bq4"], io["a_bk4"], io["a_bv"], io["a_consts"], io["g_xattn"][0:1, 0:1])
        bit_linear_ffn(nc, res, io["b_gate_w"], io["b_val_w"], io["b_out_w"], io["b_gate_b"], io["b_val_b"],
                       io["b_out_b"], io["g_ffn"][0:1, 0:1])
        text_free_attention(nc, res, io["ctx"], io["ctxT"], io["c_wqT"], io["c_wkT"],
                            (io["c_wq"], io["c_wk"], io["c_wv"], io["c_wo"]), io["c_cols"],
                            (io["c_nq"], io["c_nk"]), io["c_ob"], io["g_xattn"][0:1, 1:2])
        expert_layer(nc, res, (io["d_wq"], io["d_wk"], io["d_wv"], io["d_wo"]), io["d_ln1"], io["d_gate_w"],
                     io["d_ln2"], io["d_gu_w"], io["d_down_w"], io["d_spread"], io["g_ffn"][0:1, 1:2], out)


def lay_out(inputs):
    f = {n: np.ascontiguousarray(v) for n, v in inputs.items()}
    out = {"x": f["x"], "ctx": f["ctx_2048"], "mask": f["mask_Bx1x2048_fk1"][:, 0, :]}
    out["maskT"] = out["mask"].reshape(BATCHES, 2, P).transpose(2, 0, 1).reshape(P, 2 * BATCHES)
    out["mask"] = out["mask"].reshape(1, BATCHES * DIM)
    out["g_xattn"], out["g_ffn"] = f["g_xattn"][None, :], f["g_ffn"][None, :]

    def strips(rows):
        w = np.zeros((A_TILES, A_SLOTS, A_ROWS) + rows.shape[1:], rows.dtype)
        for j in range(A_TILES):
            for r in range(A_SLOTS):
                h = A_TILES * r + j
                for k in range(3):
                    w[j, r, A_HD * k:A_HD * k + A_HD] = rows[A_HD * h:A_HD * h + A_HD]
        return w.reshape((A_TILES * P,) + rows.shape[1:])

    out["a_wq4"], out["a_wk4"] = strips(f["L0_xattn_Wq"]).T, strips(f["L0_xattn_Wk"]).T
    out["a_wv"], out["a_bv"] = f["L0_xattn_Wv"].T, f["L0_xattn_bv"][None, :]
    out["a_bq4"] = strips(f["L0_xattn_bq"]).reshape(A_TILES, P).T
    out["a_bk4"] = strips(f["L0_xattn_bk"]).reshape(A_TILES, P).T
    c = np.zeros((A_ROWS, 8), np.float32)
    c[[*range(16, 24), 26], 0] = -1.0
    c[[*range(8, 16), 25], 1] = -1.0
    c[:, 2] = 1.0
    c[24:27, 2], c[24:27, 3], c[24:27, 5] = -1.0, 1.0, 1.0
    c[24:27, 4] = -NEG * A_ROOT
    c[27, 2], c[27, 3], c[27, 5] = 0.0, 1.0, 1.0
    out["a_consts"] = np.tile(c, (A_SLOTS, 1))

    def stationary(w):
        return w.T.reshape(-1, P, w.shape[0]).transpose(1, 0, 2).reshape(P, -1)

    for n in ("gate", "val", "out"):
        out[f"b_{n}_w"] = stationary(f[f"L0_ffn_{n}_w"])
        out[f"b_{n}_b"] = f[f"L0_ffn_{n}_b"][None, :]

    def by_heads(w, b):
        t = np.zeros((P, HEADS, DIM + 2), w.dtype)
        t[:, :, :DIM] = w.T.reshape(HEADS, P, DIM).transpose(1, 0, 2)
        t[:, :, DIM] = b.reshape(HEADS, P).T
        return t

    def tokens_last(a):
        return a.transpose(2, 0, 1).reshape(KT, P, -1).transpose(1, 0, 2)

    pre = "L1_xattn_"
    out["ctxT"] = tokens_last(out["ctx"])
    out["c_wqT"], out["c_wkT"] = by_heads(f[pre + "q_w"], f[pre + "q_b"]), by_heads(f[pre + "ki_w"], f[pre + "ki_b"])
    for n, m in (("q", "q_w"), ("k", "ki_w"), ("v", "vi_w")):
        out[f"c_w{n}"] = f[pre + m].reshape(KT, P, INNER).transpose(1, 0, 2)
    out["c_wo"] = f[pre + "o_w"].reshape(HEADS, P, DIM).transpose(1, 0, 2)
    out["c_cols"] = np.stack([f[pre + n].reshape(HEADS, P).T for n in ("q_b", "ki_b", "vi_b", "nq_s", "nki_s")], 1)
    out["c_nq"], out["c_nk"], out["c_ob"] = (f[pre + n][None, :] for n in ("nq_s", "nki_s", "o_b"))

    def natural(w):
        return w.T.reshape(KT, P, -1).transpose(1, 0, 2)

    pre = "L1_ffn_"
    out["d_wq"] = natural(f[pre + "q_w"].reshape(HEADS, QHD, DIM)[:, :HD].reshape(INNER, DIM))
    out["d_wk"], out["d_wv"] = natural(f[pre + "kv_w"][:INNER]), natural(f[pre + "kv_w"][INNER:2 * INNER])
    out["d_wo"] = f[pre + "o_w"].T.reshape(HEADS, P, DIM).transpose(1, 0, 2)
    out["d_ln1"], out["d_ln2"] = f[pre + "ln1_w"][None, :], f[pre + "ln2_w"][None, :]
    out["d_gate_w"] = natural(f[pre + "gate_w"])

    w1, sh = f[pre + "w1"], f[pre + "sh_gu_w"]
    gu = np.zeros((2, M_TILES * P, DIM), w1.dtype)
    down = np.zeros((M_TILES * P, DIM), w1.dtype)
    split = EXPERTS * EXPERT_HID
    for n in range(2):
        gu[n, :split] = w1[:, EXPERT_HID * n:EXPERT_HID * n + EXPERT_HID].reshape(split, DIM)
        gu[n, split:split + SHARED_HID] = sh[SHARED_HID * n:SHARED_HID * n + SHARED_HID]
    down[:split] = f[pre + "w2"].transpose(0, 2, 1).reshape(split, DIM)
    down[split:split + SHARED_HID] = f[pre + "sh_down_w"].T
    out["d_gu_w"] = gu.transpose(2, 0, 1).reshape(KT, P, 2, M_TILES * P).transpose(1, 2, 0, 3)
    out["d_down_w"] = down.reshape(M_TILES, P, DIM).transpose(1, 0, 2)
    owner = np.minimum(np.arange(M_TILES * P) // EXPERT_HID, EXPERTS)
    kind = np.arange(W_ROWS)[:, None] % LO
    out["d_spread"] = (owner[None, :] == kind).astype(np.float32)
    return {n: np.ascontiguousarray(v) for n, v in out.items()}


def kernel(**inputs):
    import concourse.bacc as bacc
    from concourse.bass_utils import run_bass_kernel_spmd

    nc = bacc.Bacc("TRN2", target_bir_lowering=False, num_devices=1)
    arrays = lay_out(inputs)
    io = {n: nc.dram_tensor(f"in_{n}", a.shape, mybir.dt.from_np(a.dtype), kind="ExternalInput").ap()
          for n, a in arrays.items()}
    out = nc.dram_tensor("out_x", (BATCHES, TOKENS, DIM), F32, kind="ExternalOutput").ap()
    gated_layers(nc, io, out)
    r = run_bass_kernel_spmd(nc, [{f"in_{n}": a for n, a in arrays.items()}], core_ids=[0])
    return r.results[0]["out_x"]
```
